# Optimizing a Trainium2 kernel written in Bass

```python
import numpy as np
import jax
import jax.numpy as jnp

def _softmax(x, axis=-1):
    return jax.nn.softmax(x, axis=axis)

def _gelu(x):
    return jax.nn.gelu(x, approximate=True)

def _silu(x):
    return jax.nn.silu(x)

def _sigmoid(x):
    return jax.nn.sigmoid(x)

def _layernorm(x, axis=-1, eps=1e-05):
    m = jnp.mean(x, axis=axis, keepdims=True)
    v = jnp.var(x, axis=axis, keepdims=True)
    return (x - m) / jnp.sqrt(v + eps)

def _scatter_add(tgt, idx, src, axis=0):
    return tgt.at[idx].add(src)

def _segment_sum(src, seg, n):
    return jax.ops.segment_sum(src, seg, n)
kernel_name = 'mk_hybrid_d1_jaxref_r4_dce73a'

def setup_inputs(seed: int=0):
    np.random.seed(seed)
    _w = jnp.asarray

    def _L0_attn_a_setup():
        import jax, jax.numpy as jnp
        import numpy as np
        D = 256
        H = 16
        KVH = 4
        HD = D // H
        LAT = 64
        WIN = 64
        B, S = (1, 512)
        BASE_G, BASE_L = (1000000.0, 10000.0)
        EPS = 1e-06

        def rmsnorm(x, w):
            return x * jax.lax.rsqrt(jnp.mean(x * x, axis=-1, keepdims=True) + EPS) * w

        def qk_norm(x):
            return x * jax.lax.rsqrt(jnp.mean(x * x, axis=-1, keepdims=True) + EPS)

        def rope(x, base):
            s, hd = (x.shape[-2], x.shape[-1])
            inv_freq = 1.0 / base ** (jnp.arange(0, hd, 2, dtype=jnp.float32) / hd)
            freqs = jnp.arange(s, dtype=jnp.float32)[:, None] * inv_freq[None, :]
            cos, sin = (jnp.cos(freqs), jnp.sin(freqs))
            xe, xo = (x[..., ::2], x[..., 1::2])
            out = jnp.stack([xe * cos - xo * sin, xe * sin + xo * cos], axis=-1)
            return out.reshape(x.shape)

        def split_heads(x, n_heads):
            b, s, _ = x.shape
            return x.reshape(b, s, n_heads, HD).transpose(0, 2, 1, 3)

        def repeat_kv(x):
            return jnp.repeat(x, H // KVH, axis=1)

        def sdpa(q, k, v, mask):
            scores = jnp.einsum('bhqd,bhkd->bhqk', q, k) / np.sqrt(HD).astype(np.float32)
            scores = jnp.where(mask, scores, jnp.float32(-1e+30))
            probs = jax.nn.softmax(scores, axis=-1)
            return jnp.einsum('bhqk,bhkd->bhqd', probs, v)

        def merge_heads(x):
            b, h, s, hd = x.shape
            return x.transpose(0, 2, 1, 3).reshape(b, s, h * hd)

        def global_latent_attn(x, wq, w_kv_down, w_k_up, w_v_up, wo):
            q = split_heads(x @ wq, H)
            latent = x @ w_kv_down
            k = split_heads(latent @ w_k_up, KVH)
            v = split_heads(latent @ w_v_up, KVH)
            q, k = (rope(q, BASE_G), rope(k, BASE_G))
            q, k = (qk_norm(q), qk_norm(k))
            k, v = (repeat_kv(k), repeat_kv(v))
            i = jnp.arange(x.shape[1])
            causal = i[:, None] >= i[None, :]
            return merge_heads(sdpa(q, k, v, causal)) @ wo

        def local_gqa_attn(x, wq, wk, wv, wo):
            q = split_heads(x @ wq, H)
            k = split_heads(x @ wk, KVH)
            v = split_heads(x @ wv, KVH)
            q, k = (rope(q, BASE_L), rope(k, BASE_L))
            q, k = (qk_norm(q), qk_norm(k))
            k, v = (repeat_kv(k), repeat_kv(v))
            i = jnp.arange(x.shape[1])
            diff = i[:, None] - i[None, :]
            mask = (diff >= 0) & (diff < WIN)
            return merge_heads(sdpa(q, k, v, mask)) @ wo
        key = jax.random.key(seed)
        ks = jax.random.split(key, 12)
        std = 0.02
        return {'hidden': jax.random.normal(ks[0], (B, S, D), dtype=jnp.float32), 'norm1_w': jnp.ones((D,), jnp.float32), 'norm2_w': jnp.ones((D,), jnp.float32), 'g_wq': jax.random.normal(ks[1], (D, H * HD), jnp.float32) * std, 'g_kv_down': jax.random.normal(ks[2], (D, LAT), jnp.float32) * std, 'g_k_up': jax.random.normal(ks[3], (LAT, KVH * HD), jnp.float32) * std, 'g_v_up': jax.random.normal(ks[4], (LAT, KVH * HD), jnp.float32) * std, 'g_wo': jax.random.normal(ks[5], (D, D), jnp.float32) * std, 'l_wq': jax.random.normal(ks[6], (D, H * HD), jnp.float32) * std, 'l_wk': jax.random.normal(ks[7], (D, KVH * HD), jnp.float32) * std, 'l_wv': jax.random.normal(ks[8], (D, KVH * HD), jnp.float32) * std, 'l_wo': jax.random.normal(ks[9], (D, D), jnp.float32) * std}
    _L0_attn_a_in = _L0_attn_a_setup()

    def _L0_attn_b_setup():
        import jax, jax.numpy as jnp
        import numpy as np
        B, L, D_MODEL = (4, 512, 256)
        DC = D_MODEL // 2
        NL = 2
        NS = 16
        DI = 2 * DC
        DTR = (DC + 15) // 16
        DCONV = 4
        EPS = 1e-05

        def _rmsnorm(x, w):
            return x * jax.lax.rsqrt(jnp.mean(x * x, axis=-1, keepdims=True) + EPS) * w

        def _mamba_block(x, inW, cw, cb, xpW, dtW, dtb, A_log, Dp, moW):
            xz = x @ inW.T
            xc, z = jnp.split(xz, 2, axis=-1)
            xt = jnp.pad(xc.transpose(0, 2, 1), ((0, 0), (0, 0), (DCONV - 1, 0)))
            xc = jax.lax.conv_general_dilated(xt, cw, window_strides=(1,), padding='VALID', dimension_numbers=('NCH', 'OIH', 'NCH'), feature_group_count=DI)
            xc = jax.nn.silu((xc + cb[None, :, None]).transpose(0, 2, 1))
            dbc = xc @ xpW.T
            dt, Bm, Cm = (dbc[..., :DTR], dbc[..., DTR:DTR + NS], dbc[..., DTR + NS:])
            delta = jax.nn.softplus(dt @ dtW.T + dtb)
            A = -jnp.exp(A_log)
            dA = jnp.exp(delta[..., None] * A)
            dBx = (delta * xc)[..., None] * Bm[:, :, None, :]

            def step(h, inp):
                a, b, c = inp
                h = a * h + b
                return (h, jnp.einsum('bdn,bn->bd', h, c))
            h0 = jnp.zeros((xc.shape[0], DI, NS), xc.dtype)
            _, ys = jax.lax.scan(step, h0, (dA.transpose(1, 0, 2, 3), dBx.transpose(1, 0, 2, 3), Cm.transpose(1, 0, 2)))
            y = ys.transpose(1, 0, 2) + Dp * xc
            y = y * jax.nn.silu(z)
            return y @ moW.T
        key = jax.random.key(seed)
        ks = jax.random.split(key, 12)
        s = 0.02
        p = {}
        p['src'] = jax.random.normal(ks[0], (B, L, D_MODEL), jnp.float32)
        p['ln_g'] = jnp.ones((D_MODEL,), jnp.float32)
        p['ln_b'] = jnp.zeros((D_MODEL,), jnp.float32)
        p['po_W'] = s * jax.random.normal(ks[1], (D_MODEL, D_MODEL), jnp.float32)
        p['po_b'] = jnp.zeros((D_MODEL,), jnp.float32)
        p['rms_w'] = jnp.ones((NL, DC), jnp.float32)
        p['in_W'] = s * jax.random.normal(ks[2], (NL, 2 * DI, DC), jnp.float32)
        p['conv_w'] = s * jax.random.normal(ks[3], (NL, DI, 1, DCONV), jnp.float32)
        p['conv_b'] = jnp.zeros((NL, DI), jnp.float32)
        p['xp_W'] = s * jax.random.normal(ks[4], (NL, DTR + 2 * NS, DI), jnp.float32)
        p['dt_W'] = s * jax.random.normal(ks[5], (NL, DI, DTR), jnp.float32)
        p['dt_b'] = 0.1 * jax.random.normal(ks[6], (NL, DI), jnp.float32)
        p['A_log'] = jnp.tile(jnp.log(jnp.arange(1, NS + 1, dtype=jnp.float32)), (NL, DI, 1))
        p['Dp'] = jnp.ones((NL, DI), jnp.float32)
        p['mo_W'] = s * jax.random.normal(ks[7], (NL, DC, DI), jnp.float32)
        return p
    _L0_attn_b_in = _L0_attn_b_setup()

    def _L0_ffn_setup():
        import jax, jax.numpy as jnp
        import numpy as np
        D_MODEL = 256
        DEPTH = 8
        M = 2 ** DEPTH
        N_INTERNAL = M - 1
        B, T = (8, 1024)

        def _leaf_probs(gate):
            BT = gate.shape[0]
            lp = jnp.ones((BT, M), dtype=gate.dtype)
            for level in range(DEPTH):
                n = 2 ** level
                half = M // (2 * n)
                g = gate[:, n - 1:2 * n - 1]
                f = jnp.stack([1.0 - g, g], axis=-1)
                f = jnp.broadcast_to(f[..., None], (BT, n, 2, half))
                lp = lp * f.reshape(BT, M)
            return lp
        key = jax.random.key(seed)
        ks = jax.random.split(key, 7)
        x = jax.random.normal(ks[0], (B, T, D_MODEL), dtype=jnp.float32)
        Wq = jax.random.normal(ks[1], (D_MODEL, D_MODEL), dtype=jnp.float32) * 0.02
        routers = jax.random.normal(ks[2], (N_INTERNAL, D_MODEL), dtype=jnp.float32) * 0.02
        leaf_keys = jax.random.normal(ks[3], (M, D_MODEL), dtype=jnp.float32) * 0.02
        leaf_values = jax.random.normal(ks[4], (M, D_MODEL), dtype=jnp.float32) * 0.02
        Wout_w = jax.random.normal(ks[5], (D_MODEL, D_MODEL), dtype=jnp.float32) * 0.02
        Wout_b = jax.random.normal(ks[6], (D_MODEL,), dtype=jnp.float32) * 0.02
        return {'x': x, 'Wq': Wq, 'routers': routers, 'leaf_keys': leaf_keys, 'leaf_values': leaf_values, 'Wout_w': Wout_w, 'Wout_b': Wout_b}
    _L0_ffn_in = _L0_ffn_setup()
    _d = {'L0_attn_a_hidden': _L0_attn_a_in['hidden'], 'L0_attn_a_norm1_w': _L0_attn_a_in['norm1_w'], 'L0_attn_a_norm2_w': _L0_attn_a_in['norm2_w'], 'L0_attn_a_g_wq': _L0_attn_a_in['g_wq'], 'L0_attn_a_g_kv_down': _L0_attn_a_in['g_kv_down'], 'L0_attn_a_g_k_up': _L0_attn_a_in['g_k_up'], 'L0_attn_a_g_v_up': _L0_attn_a_in['g_v_up'], 'L0_attn_a_g_wo': _L0_attn_a_in['g_wo'], 'L0_attn_a_l_wq': _L0_attn_a_in['l_wq'], 'L0_attn_a_l_wk': _L0_attn_a_in['l_wk'], 'L0_attn_a_l_wv': _L0_attn_a_in['l_wv'], 'L0_attn_a_l_wo': _L0_attn_a_in['l_wo'], 'L0_attn_b_ln_g': _L0_attn_b_in['ln_g'], 'L0_attn_b_ln_b': _L0_attn_b_in['ln_b'], 'L0_attn_b_po_W': _L0_attn_b_in['po_W'], 'L0_attn_b_po_b': _L0_attn_b_in['po_b'], 'L0_attn_b_rms_w': _L0_attn_b_in['rms_w'], 'L0_attn_b_in_W': _L0_attn_b_in['in_W'], 'L0_attn_b_conv_w': _L0_attn_b_in['conv_w'], 'L0_attn_b_conv_b': _L0_attn_b_in['conv_b'], 'L0_attn_b_xp_W': _L0_attn_b_in['xp_W'], 'L0_attn_b_dt_W': _L0_attn_b_in['dt_W'], 'L0_attn_b_dt_b': _L0_attn_b_in['dt_b'], 'L0_attn_b_A_log': _L0_attn_b_in['A_log'], 'L0_attn_b_Dp': _L0_attn_b_in['Dp'], 'L0_attn_b_mo_W': _L0_attn_b_in['mo_W'], 'L0_ffn_Wq': _L0_ffn_in['Wq'], 'L0_ffn_routers': _L0_ffn_in['routers'], 'L0_ffn_leaf_keys': _L0_ffn_in['leaf_keys'], 'L0_ffn_leaf_values': _L0_ffn_in['leaf_values'], 'L0_ffn_Wout_w': _L0_ffn_in['Wout_w'], 'L0_ffn_Wout_b': _L0_ffn_in['Wout_b']}
    _x0 = _d['L0_attn_a_hidden']
    _d['L0_attn_a_hidden'] = jax.random.normal(jax.random.fold_in(jax.random.key(seed), 1), (1, 4096, 256), dtype=_x0.dtype)
    del _x0
    return _d

def reference(L0_attn_a_hidden, L0_attn_a_norm1_w, L0_attn_a_norm2_w, L0_attn_a_g_wq, L0_attn_a_g_kv_down, L0_attn_a_g_k_up, L0_attn_a_g_v_up, L0_attn_a_g_wo, L0_attn_a_l_wq, L0_attn_a_l_wk, L0_attn_a_l_wv, L0_attn_a_l_wo, L0_attn_b_ln_g, L0_attn_b_ln_b, L0_attn_b_po_W, L0_attn_b_po_b, L0_attn_b_rms_w, L0_attn_b_in_W, L0_attn_b_conv_w, L0_attn_b_conv_b, L0_attn_b_xp_W, L0_attn_b_dt_W, L0_attn_b_dt_b, L0_attn_b_A_log, L0_attn_b_Dp, L0_attn_b_mo_W, L0_ffn_Wq, L0_ffn_routers, L0_ffn_leaf_keys, L0_ffn_leaf_values, L0_ffn_Wout_w, L0_ffn_Wout_b):

    def _L0_attn_a_ref(hidden, norm1_w, norm2_w, g_wq, g_kv_down, g_k_up, g_v_up, g_wo, l_wq, l_wk, l_wv, l_wo):
        import jax, jax.numpy as jnp
        import numpy as np
        D = 256
        H = 16
        KVH = 4
        HD = D // H
        LAT = 64
        WIN = 64
        B, S = (1, 512)
        BASE_G, BASE_L = (1000000.0, 10000.0)
        EPS = 1e-06

        def rmsnorm(x, w):
            return x * jax.lax.rsqrt(jnp.mean(x * x, axis=-1, keepdims=True) + EPS) * w

        def qk_norm(x):
            return x * jax.lax.rsqrt(jnp.mean(x * x, axis=-1, keepdims=True) + EPS)

        def rope(x, base):
            s, hd = (x.shape[-2], x.shape[-1])
            inv_freq = 1.0 / base ** (jnp.arange(0, hd, 2, dtype=jnp.float32) / hd)
            freqs = jnp.arange(s, dtype=jnp.float32)[:, None] * inv_freq[None, :]
            cos, sin = (jnp.cos(freqs), jnp.sin(freqs))
            xe, xo = (x[..., ::2], x[..., 1::2])
            out = jnp.stack([xe * cos - xo * sin, xe * sin + xo * cos], axis=-1)
            return out.reshape(x.shape)

        def split_heads(x, n_heads):
            b, s, _ = x.shape
            return x.reshape(b, s, n_heads, HD).transpose(0, 2, 1, 3)

        def repeat_kv(x):
            return jnp.repeat(x, H // KVH, axis=1)

        def sdpa(q, k, v, mask):
            scores = jnp.einsum('bhqd,bhkd->bhqk', q, k) / np.sqrt(HD).astype(np.float32)
            scores = jnp.where(mask, scores, jnp.float32(-1e+30))
            probs = jax.nn.softmax(scores, axis=-1)
            return jnp.einsum('bhqk,bhkd->bhqd', probs, v)

        def merge_heads(x):
            b, h, s, hd = x.shape
            return x.transpose(0, 2, 1, 3).reshape(b, s, h * hd)

        def global_latent_attn(x, wq, w_kv_down, w_k_up, w_v_up, wo):
            q = split_heads(x @ wq, H)
            latent = x @ w_kv_down
            k = split_heads(latent @ w_k_up, KVH)
            v = split_heads(latent @ w_v_up, KVH)
            q, k = (rope(q, BASE_G), rope(k, BASE_G))
            q, k = (qk_norm(q), qk_norm(k))
            k, v = (repeat_kv(k), repeat_kv(v))
            i = jnp.arange(x.shape[1])
            causal = i[:, None] >= i[None, :]
            return merge_heads(sdpa(q, k, v, causal)) @ wo

        def local_gqa_attn(x, wq, wk, wv, wo):
            q = split_heads(x @ wq, H)
            k = split_heads(x @ wk, KVH)
            v = split_heads(x @ wv, KVH)
            q, k = (rope(q, BASE_L), rope(k, BASE_L))
            q, k = (qk_norm(q), qk_norm(k))
            k, v = (repeat_kv(k), repeat_kv(v))
            i = jnp.arange(x.shape[1])
            diff = i[:, None] - i[None, :]
            mask = (diff >= 0) & (diff < WIN)
            return merge_heads(sdpa(q, k, v, mask)) @ wo
        x = hidden
        x = x + global_latent_attn(rmsnorm(x, norm1_w), g_wq, g_kv_down, g_k_up, g_v_up, g_wo)
        x = x + local_gqa_attn(rmsnorm(x, norm2_w), l_wq, l_wk, l_wv, l_wo)
        return x

    def _L0_attn_b_ref(src, ln_g, ln_b, po_W, po_b, rms_w, in_W, conv_w, conv_b, xp_W, dt_W, dt_b, A_log, Dp, mo_W):
        import jax, jax.numpy as jnp
        import numpy as np
        B, L, D_MODEL = (4, 512, 256)
        DC = D_MODEL // 2
        NL = 2
        NS = 16
        DI = 2 * DC
        DTR = (DC + 15) // 16
        DCONV = 4
        EPS = 1e-05

        def _rmsnorm(x, w):
            return x * jax.lax.rsqrt(jnp.mean(x * x, axis=-1, keepdims=True) + EPS) * w

        def _mamba_block(x, inW, cw, cb, xpW, dtW, dtb, A_log, Dp, moW):
            xz = x @ inW.T
            xc, z = jnp.split(xz, 2, axis=-1)
            xt = jnp.pad(xc.transpose(0, 2, 1), ((0, 0), (0, 0), (DCONV - 1, 0)))
            xc = jax.lax.conv_general_dilated(xt, cw, window_strides=(1,), padding='VALID', dimension_numbers=('NCH', 'OIH', 'NCH'), feature_group_count=DI)
            xc = jax.nn.silu((xc + cb[None, :, None]).transpose(0, 2, 1))
            dbc = xc @ xpW.T
            dt, Bm, Cm = (dbc[..., :DTR], dbc[..., DTR:DTR + NS], dbc[..., DTR + NS:])
            delta = jax.nn.softplus(dt @ dtW.T + dtb)
            A = -jnp.exp(A_log)
            dA = jnp.exp(delta[..., None] * A)
            dBx = (delta * xc)[..., None] * Bm[:, :, None, :]

            def step(h, inp):
                a, b, c = inp
                h = a * h + b
                return (h, jnp.einsum('bdn,bn->bd', h, c))
            h0 = jnp.zeros((xc.shape[0], DI, NS), xc.dtype)
            _, ys = jax.lax.scan(step, h0, (dA.transpose(1, 0, 2, 3), dBx.transpose(1, 0, 2, 3), Cm.transpose(1, 0, 2)))
            y = ys.transpose(1, 0, 2) + Dp * xc
            y = y * jax.nn.silu(z)
            return y @ moW.T
        mu = jnp.mean(src, axis=-1, keepdims=True)
        var = jnp.mean((src - mu) ** 2, axis=-1, keepdims=True)
        s = (src - mu) * jax.lax.rsqrt(var + EPS) * ln_g + ln_b
        x1, x2 = jnp.split(s, 2, axis=-1)
        h = x1
        for i in range(NL):
            h = h + _mamba_block(_rmsnorm(h, rms_w[i]), in_W[i], conv_w[i], conv_b[i], xp_W[i], dt_W[i], dt_b[i], A_log[i], Dp[i], mo_W[i])
        y2 = x2 + h
        out = jnp.concatenate([x1, y2], axis=-1)
        return s + (out @ po_W.T + po_b)

    def _L0_ffn_ref(x, Wq, routers, leaf_keys, leaf_values, Wout_w, Wout_b):
        import jax, jax.numpy as jnp
        import numpy as np
        D_MODEL = 256
        DEPTH = 8
        M = 2 ** DEPTH
        N_INTERNAL = M - 1
        B, T = (8, 1024)

        def _leaf_probs(gate):
            BT = gate.shape[0]
            lp = jnp.ones((BT, M), dtype=gate.dtype)
            for level in range(DEPTH):
                n = 2 ** level
                half = M // (2 * n)
                g = gate[:, n - 1:2 * n - 1]
                f = jnp.stack([1.0 - g, g], axis=-1)
                f = jnp.broadcast_to(f[..., None], (BT, n, 2, half))
                lp = lp * f.reshape(BT, M)
            return lp
        Bv, Tv, d = x.shape
        q = jnp.einsum('btd,ed->bte', x, Wq)
        q_flat = q.reshape(Bv * Tv, d)
        gate = jax.nn.sigmoid(q_flat @ routers.T)
        leaf_prob = _leaf_probs(gate)
        ret = (leaf_prob @ leaf_values).reshape(Bv, Tv, d)
        return jnp.einsum('btd,ed->bte', ret, Wout_w) + Wout_b
    x = L0_attn_a_hidden
    x = x + _L0_attn_a_ref(_layernorm(x, axis=-1), L0_attn_a_norm1_w, L0_attn_a_norm2_w, L0_attn_a_g_wq, L0_attn_a_g_kv_down, L0_attn_a_g_k_up, L0_attn_a_g_v_up, L0_attn_a_g_wo, L0_attn_a_l_wq, L0_attn_a_l_wk, L0_attn_a_l_wv, L0_attn_a_l_wo)
    x = x + _L0_ffn_ref(_layernorm(x, axis=-1), L0_ffn_Wq, L0_ffn_routers, L0_ffn_leaf_keys, L0_ffn_leaf_values, L0_ffn_Wout_w, L0_ffn_Wout_b)
    x = x + _L0_attn_b_ref(_layernorm(x, axis=-1), L0_attn_b_ln_g, L0_attn_b_ln_b, L0_attn_b_po_W, L0_attn_b_po_b, L0_attn_b_rms_w, L0_attn_b_in_W, L0_attn_b_conv_w, L0_attn_b_conv_b, L0_attn_b_xp_W, L0_attn_b_dt_W, L0_attn_b_dt_b, L0_attn_b_A_log, L0_attn_b_Dp, L0_attn_b_mo_W)
    x = x + _L0_ffn_ref(_layernorm(x, axis=-1), L0_ffn_Wq, L0_ffn_routers, L0_ffn_leaf_keys, L0_ffn_leaf_values, L0_ffn_Wout_w, L0_ffn_Wout_b)
    return x

_drawn_inputs = setup_inputs


def setup_inputs(seed=0):
    import zlib

    import numpy as np

    out = dict(_drawn_inputs(seed))
    spreads = {'L0_attn_a_norm1_w': (1.0, 0.6),
     'L0_attn_a_norm2_w': (1.0, 0.6),
     'L0_attn_b_ln_g': (1.0, 0.2),
     'L0_attn_b_ln_b': (0.0, 0.1),
     'L0_attn_b_po_b': (0.0, 0.8),
     'L0_attn_b_rms_w': (1.0, 0.6),
     'L0_attn_b_conv_b': (0.0, 0.8),
     'L0_attn_b_Dp': (1.0, 0.6)}
    factors = {'L0_attn_a_g_wq': 8.0,
     'L0_attn_a_g_kv_down': 8.0,
     'L0_attn_a_g_k_up': 8.0,
     'L0_attn_a_g_v_up': 8.0,
     'L0_attn_a_g_wo': 8.0,
     'L0_attn_a_l_wq': 7.351,
     'L0_attn_a_l_wk': 7.372,
     'L0_attn_a_l_wv': 5.588,
     'L0_attn_a_l_wo': 5.563,
     'L0_attn_b_in_W': 8.0,
     'L0_attn_b_conv_w': 8.0,
     'L0_attn_b_xp_W': 8.0,
     'L0_attn_b_dt_W': 8.0,
     'L0_attn_b_dt_b': 8.0,
     'L0_attn_b_A_log': 8.0,
     'L0_attn_b_mo_W': 8.0,
     'L0_ffn_Wq': 8.0,
     'L0_ffn_routers': 8.0,
     'L0_ffn_leaf_values': 8.0,
     'L0_ffn_Wout_w': 8.0,
     'L0_ffn_Wout_b': 3.307}
    for name, (base, spread) in spreads.items():
        noise = np.random.default_rng([zlib.crc32(name.encode()), seed]).standard_normal(out[name].shape)
        drawn = base * np.exp(spread * noise) if base else spread * noise
        out[name] = jnp.asarray(drawn.astype(out[name].dtype))
    for name, factor in factors.items():
        out[name] = (out[name] * factor).astype(out[name].dtype)
    return out
```

```python
from contextlib import ExitStack

import numpy as np

import concourse.bass as bass
from concourse import mybir

F32 = mybir.dt.float32
BF16 = mybir.dt.bfloat16
I32 = mybir.dt.int32
ACT = mybir.ActivationFunctionType
ALU = mybir.AluOpType
AX = mybir.AxisListType.X

P = 128
S, D = 4096, 256
NT = S // P
TPC = 4
CH = TPC * P
NCH = S // CH
KD = D // P
H, KVH, HD = 16, 4, 16
GQ = H // KVH
NQK = H + KVH
QKW, QKVW = NQK * HD, (NQK + KVH) * HD
LAT, WIN = 64, 64
TERMS = 8
VW = 32
NL, NS, DTR, TAPS = 2, 16, 8, 4
HALVES = 2
DI = HALVES * P
XPW = 3 * 2 * NS + DTR
LN_EPS, RMS_EPS, MAMBA_EPS = 1e-5, 1e-6, 1e-5
NEG = -30000.0
SCORE_SCALE = 1.0 / 4.0


class Tiles:
    pass


class Chain:

    def __init__(self, eng, sem):
        self.eng, self.sem, self.count = eng, sem, 0

    def do(self, ins):
        ins.then_inc(self.sem, 1)
        self.count += 1

    def sync(self):
        self.eng.wait_ge(self.sem, self.count)

    def link(self, ins):
        self.do(ins)
        self.sync()

    def restart(self):
        self.eng.sem_clear(self.sem)
        self.count = 0


def rsqrt(nc, chain, y, x, half, tmp):
    v = nc.vector
    chain.do(v.tensor_scalar(half, x, -0.5, None, ALU.mult))
    chain.link(v.tensor_single_scalar(tmp.bitcast(I32), x.bitcast(I32), 1, ALU.logical_shift_right))
    chain.link(v.tensor_scalar(y.bitcast(I32), tmp.bitcast(I32), -1.0, float(0x5F3759DF), ALU.mult, ALU.add))
    for _ in range(4):
        chain.link(v.tensor_tensor(tmp, y, y, ALU.mult))
        chain.link(v.tensor_tensor(tmp, tmp, half, ALU.mult))
        chain.link(v.scalar_tensor_tensor(y, tmp, 1.5, y, ALU.add, ALU.mult))


def pair_swap(ap):
    return ap.rearrange("p h (e t) -> p h e t", t=2)[:, :, :, ::-1]


def heads(ap, n):
    return ap.rearrange("p (h e) -> p h e", h=n)


def spread(ap, n):
    return ap.unsqueeze(2).to_broadcast([P, n, HD])


def rope_norm_split(nc, chain, b, cos, sin):
    v = nc.vector
    qk = heads(b.qkv[:, 0:QKW], NQK)
    cosb = cos.unsqueeze(1).to_broadcast([P, NQK, HD])
    sinb = sin.rearrange("p (e t) -> p e t", t=2).unsqueeze(1).to_broadcast([P, NQK, HD // 2, 2])
    t1, t2 = heads(b.t1[:, :], NQK), heads(b.t2[:, :], NQK)
    chain.do(v.tensor_tensor(t1, qk, cosb, ALU.mult))
    chain.link(v.tensor_tensor(t2.rearrange("p h (e t) -> p h e t", t=2), pair_swap(qk), sinb, ALU.mult))
    chain.link(v.tensor_tensor(b.t1[:, :], b.t1[:, :], b.t2[:, :], ALU.add))
    chain.link(v.tensor_tensor(b.t2[:, :], b.t1[:, :], b.t1[:, :], ALU.mult))
    chain.link(v.tensor_reduce(b.ss[:, :], t2, AX, ALU.add))
    chain.link(v.tensor_scalar(b.ss[:, :], b.ss[:, :], 1.0 / HD, RMS_EPS, ALU.mult, ALU.add))
    rsqrt(nc, chain, b.rs[:, :], b.ss[:, :], b.n1[:, :], b.n2[:, :])
    chain.link(v.tensor_tensor(t1, t1, spread(b.rs[:, :], NQK), ALU.mult))
    q, k = t1[:, 0:H, :], t1[:, H:NQK, :]
    qs = b.qs[:, :].rearrange("p (h r e) -> p h r e", h=H, r=TERMS)
    ks = b.ks[:, :].rearrange("p (h r e) -> p h r e", h=KVH, r=TERMS)
    qterms, kterms = ((0, 3), (3, 6), (6, 8)), ((0, 8), (1, 8), (2, 6))
    for part in range(3):
        q0, q1 = qterms[part]
        k0, k1 = kterms[part]
        nk = len(range(k0, k1, 3))
        chain.do(v.tensor_copy(qs[:, :, q0:q1, :], q.unsqueeze(2).to_broadcast([P, H, q1 - q0, HD])))
        last = v.tensor_copy(ks[:, :, k0:k1:3, :], k.unsqueeze(2).to_broadcast([P, KVH, nk, HD]))
        if part == 2:
            return last
        chain.link(last)
        chain.do(v.tensor_tensor(q, q, qs[:, :, q0, :], ALU.subtract))
        chain.link(v.tensor_tensor(k, k, ks[:, :, k0, :], ALU.subtract))


def global_attention(nc, g, dram):
    ctx = ExitStack()
    with ctx:
        def sb(name, shape, dt=F32):
            return ctx.enter_context(nc.sbuf_tensor(name, shape, dt))

        def pb(name, shape):
            return ctx.enter_context(nc.psum_tensor(name, shape, F32))

        def sem(name):
            return ctx.enter_context(nc.semaphore(name))

        x = g.x
        w = g.wa_col
        kT = sb("ga_kT", [P, NCH * KVH * CH], BF16)
        qT = sb("ga_qT", [P, 2, H, CH], BF16)
        vals = sb("ga_vals", [P, NCH, KVH, TPC, HD])
        probs = sb("ga_probs", [P, 2, 2, 2 * CH])
        wqkv = sb("ga_wqkv", [P, KD, QKVW])
        xnT = sb("ga_xnT", [P, KD, P])
        b = Tiles()
        b.qkv, b.t1, b.t2 = (sb("ga_" + n, [P, QKW]) for n in ("qkv", "t1", "t2"))
        b.ss, b.rs, b.n1, b.n2 = (sb("ga_" + n, [P, NQK]) for n in ("ss", "rs", "n1", "n2"))
        b.qs, b.ks = sb("ga_qs", [P, H * P], BF16), sb("ga_ks", [P, KVH * P], BF16)
        bn = sb("ga_bn", [P, NT, 6])
        mv = sb("ga_mv", [P, NT, 2])
        var = sb("ga_var", [P, NT])
        rln = sb("ga_rln", [P, NT])
        rms = sb("ga_rms", [P, NT])
        st1 = sb("ga_st1", [P, NT])
        st2 = sb("ga_st2", [P, NT])
        v_diag = sb("ga_v_diag", [P, 3, VW])
        v_ab = sb("ga_v_ab", [P, 2, VW])
        v_cd = sb("ga_v_cd", [P, 2, VW])
        oT = sb("ga_oT", [P, CH])
        den = sb("ga_den", [P, H])
        attn = sb("ga_attn", [P, 2, TPC, D])
        attnT = sb("ga_attnT", [P, KD, P])

        score = [pb(f"ga_score{i}", [P, 2 * CH]) for i in range(2)]
        out_acc = pb("ga_out_acc", [P, CH])
        bank_a = pb("ga_bank_a", [P, 512])
        bank_b = pb("ga_bank_b", [P, 512])
        bank_c = pb("ga_bank_c", [P, 512])

        x_in = [sem(f"ga_x_in{c}") for c in range(NCH)]
        w_in = sem("ga_w_in")
        v_const = sem("ga_v_const")
        w_prod, w_ready = sem("ga_w_prod"), sem("ga_w_ready")
        dve_seq = sem("ga_dve_seq")
        xn_ready, xT_done, xT_copied = sem("ga_xn_ready"), sem("ga_xT_done"), sem("ga_xT_copied")
        qkv_done, qkv_copied = sem("ga_qkv_done"), sem("ga_qkv_copied")
        split_ready = sem("ga_split_ready")
        qa_done, qb_done, kk_done = sem("ga_qa_done"), sem("ga_qb_done"), sem("ga_kk_done")
        qa_copied, qb_copied, kk_copied = sem("ga_qa_copied"), sem("ga_qb_copied"), sem("ga_kk_copied")
        scores_done, exp_done, kb_done = sem("ga_scores_done"), sem("ga_exp_done"), sem("ga_kb_done")
        vd_staged, vab_staged, vcd_staged = sem("ga_vd_staged"), sem("ga_vab_staged"), sem("ga_vcd_staged")
        o_copied, oT_done, o_normed = sem("ga_o_copied"), sem("ga_oT_done"), sem("ga_o_normed")
        aT_done, aT_copied, proj_done, proj_added = (sem("ga_aT_done"), sem("ga_aT_copied"),
                                                     sem("ga_proj_done"), sem("ga_proj_added"))

        NG = NCH * KVH
        LEAD = 5
        first_kb = [0]
        for n in range(NG):
            first_kb.append(first_kb[-1] + TPC + TPC * (n // KVH))

        def kcols(c, kv, j):
            return ((c * KVH + kv) * TPC + j) * P

        block = ctx.enter_context(nc.Block())

        @block.sync
        def _(sp):
            sp.dma_start(g.wa[:, :], dram["wa"]).then_inc(w_in, 16)
            for c in range(NCH):
                sp.dma_start(x[:, c * TPC:(c + 1) * TPC, :], dram["x"][:, c * TPC:(c + 1) * TPC, :]).then_inc(x_in[c], 16)
            for name in ("wb", "wc", "wd"):
                sp.dma_start(g.later[name][:, :], dram[name]).then_inc(g.later_in[name], 16)

        @block.gpsimd
        def _(pool):
            def copy(out, in_):
                zero = g.zero[:, 0:1]
                for _ in in_.shape[2:]:
                    zero = zero.unsqueeze(2)
                return nc.gpsimd.tensor_tensor(out, in_, zero.to_broadcast(list(in_.shape)), ALU.add)

            make_constants(nc, pool, g)
            for t in (v_diag, v_ab, v_cd):
                nc.gpsimd.memset(t[:, :, :], 0.0).then_inc(v_const, 1)
            pool.wait_ge(v_const, 3)
            for t in (v_diag, v_ab, v_cd):
                nc.gpsimd.memset(t[:, :, HD:HD + 1], 1.0).then_inc(v_const, 1)
            pool.wait_ge(v_const, 6)
            for n in range(NG):
                c, kv = divmod(n, KVH)
                pool.wait_ge(qkv_copied, 2 * TPC * (c + 1))
                if n:
                    pool.wait_ge(kb_done, first_kb[n - 1] + 3)
                copy(v_diag[:, :, 0:HD], vals[:, c, kv, 1:TPC, :]).then_inc(vd_staged, 1)
                if n:
                    pool.wait_ge(kb_done, first_kb[n])
                copy(v_cd[:, 1, 0:HD], vals[:, c, kv, 0, :]).then_inc(vcd_staged, 1)
                if c:
                    with pool.Fori(0, c) as q:
                        row = vals[:, bass.ds(q, 1), kv, :, :]
                        pool.wait_ge(kb_done, q * TPC + (first_kb[n] + 2))
                        copy(v_ab[:, :, 0:HD], row[:, 0, 0:2, :]).then_inc(vab_staged, 1)
                        pool.wait_ge(kb_done, q * TPC + (first_kb[n] + TPC))
                        copy(v_cd[:, :, 0:HD], row[:, 0, 2:4, :]).then_inc(vcd_staged, 1)

        @block.scalar
        def _(act):
            for n in range(NG):
                c = n // KVH
                k0 = first_kb[n]
                for j in range(TPC):
                    for pr in range(2):
                        width = (j + 1) * P
                        act.wait_ge(scores_done, 2 * (k0 + j) + pr + 1)
                        if k0 + j >= 2:
                            act.wait_ge(kb_done, k0 + j - 1)
                        src = score[pr][:, :].rearrange("p (h q) -> p h q", h=2)[:, :, 0:width]
                        dst = probs[:, j % 2, pr, :].rearrange("p (h q) -> p h q", h=2)[:, :, 0:width]
                        nc.scalar.activation(dst, src, ACT.Exp, scale=SCORE_SCALE).then_inc(exp_done, 1)
                if c:
                    with act.Fori(0, c) as q:
                        for j in range(TPC):
                            for pr in range(2):
                                act.wait_ge(scores_done, q * (2 * TPC) + (2 * (k0 + TPC + j) + pr + 1))
                                if pr == 0:
                                    act.wait_ge(kb_done, q * TPC + (k0 + TPC + j - 1))
                                nc.scalar.activation(probs[:, j % 2, pr, :], score[pr][:, :], ACT.Exp,
                                                     scale=SCORE_SCALE).then_inc(exp_done, 1)

        @block.tensor
        def _(pe):
            mm, tr = nc.tensor.matmul, nc.tensor.transpose
            identf, identb = g.identf, g.identb

            pe.wait_ge(w_in, 16)
            for k in range(KD):
                last = mm(bank_a[:, k * P:(k + 1) * P], w("kv_downT")[0:LAT, k * P:(k + 1) * P],
                          w("kv_up")[0:LAT, :], start=True, stop=True)
            last.then_inc(w_prod, 1)

            def transpose_x(i):
                pe.wait_ge(xn_ready, i + 1)
                pe.wait_ge(g.ident_ready, 1)
                for k in range(KD):
                    last = tr(bank_b[:, k * P:(k + 1) * P], x[:, i, k * P:(k + 1) * P], identf[:, :])
                last.then_inc(xT_done, 1)

            def project_qkv(i):
                pe.wait_ge(xT_copied, i + 1)
                pe.wait_ge(w_ready, 4)
                for k in range(KD):
                    last = mm(bank_a[:, 0:QKVW], xnT[:, k, :], wqkv[:, k, :], start=(k == 0), stop=(k == KD - 1))
                last.then_inc(qkv_done, 1)

            def transpose_heads(i, bank, src, h0, nh, done):
                for h in range(nh):
                    last = tr(bank[:, :].bitcast(BF16)[:, h * P:(h + 1) * P], src[:, (h0 + h) * P:(h0 + h + 1) * P],
                              identb[:, :])
                last.then_inc(done, 1)

            def transpose_qa(i):
                pe.wait_ge(split_ready, i + 1)
                transpose_heads(i, bank_a, b.qs, 0, 8, qa_done)

            def transpose_qb(i):
                if i >= LEAD + KVH:
                    pe.wait_ge(proj_added, i - (LEAD - 1) - KVH)
                transpose_heads(i, bank_b, b.qs, 8, 8, qb_done)

            def transpose_k(i):
                pe.wait_ge(qa_copied, i + 1)
                transpose_heads(i, bank_a, b.ks, 0, KVH, kk_done)

            def scores(n, pr, kcol, wait_unit, j=None):
                if wait_unit is not None:
                    pe.wait_ge(exp_done, wait_unit)
                c, kv = divmod(n, KVH)
                q0 = 0 if j is None else j * P
                for a in range(2):
                    dst = score[pr][:, a * CH:a * CH + CH - q0]
                    last = mm(dst, kcol, qT[:, c % 2, kv * GQ + 2 * pr + a, q0:CH], start=True, stop=j is None)
                    if j is not None:
                        last = mm(dst[:, 0:P], identb[:, :], g.causal[:, :], start=False, stop=True)
                last.then_inc(scores_done, 1)

            def diag_scores(n, s):
                k = first_kb[n] + s
                c, kv = divmod(n, KVH)
                if s == 0 and kv == 0:
                    pe.wait_ge(qb_copied, TPC * (c + 1))
                    pe.wait_ge(kk_copied, TPC * (c + 1))
                at = kcols(c, kv, TPC - 1 - s)
                for pr in range(2):
                    scores(n, pr, kT[:, at:at + P], 2 * k + pr - 1 if k else None, TPC - 1 - s)

            def weighted(rows, slot, q0, first=False, last=False):
                for h in range(GQ):
                    out = mm(out_acc[h * VW:(h + 1) * VW, q0:CH], rows,
                             probs[:, slot, h // 2, (h % 2) * CH:(h % 2) * CH + CH - q0],
                             start=first, stop=last, skip_group_check=True)
                out.then_inc(kb_done, 1)

            def transpose_out(n):
                pe.wait_ge(o_copied, n + 1)
                if n >= KVH:
                    pe.wait_ge(aT_copied, n - KVH + 1)
                for t in range(TPC):
                    last = tr(bank_c[:, t * P:(t + 1) * P], oT[:, t * P:(t + 1) * P], identf[:, :])
                last.then_inc(oT_done, 1)

            def transpose_attn(i):
                pe.wait_ge(o_normed, min(i + KVH, NG))
                if i > NT - TPC:
                    pe.wait_ge(aT_copied, i)
                for k in range(KD):
                    last = tr(bank_c[:, k * P:(k + 1) * P], attn[:, (i // TPC) % 2, i % TPC, k * P:(k + 1) * P],
                              identf[:, :])
                last.then_inc(aT_done, 1)

            def project_out(i):
                pe.wait_ge(aT_copied, i + 1)
                pe.wait_ge(qb_copied, min(i + KVH + LEAD, NT))
                if i:
                    pe.wait_ge(proj_added, i)
                for k in range(KD):
                    last = mm(bank_b[:, 0:D], attnT[:, k, :], w("wo", k), start=(k == 0), stop=(k == KD - 1))
                last.then_inc(proj_done, 1)

            for i in range(LEAD):
                if i:
                    pe.wait_ge(kk_copied, i - 1)
                    pe.wait_ge(qb_copied, i - 1)
                pe.wait_ge(w_ready, 4)
                transpose_x(i)
                project_qkv(i)
                if i:
                    pe.wait_ge(qkv_copied, 2 * (i + 1))
                    transpose_qa(i - 1)
                    transpose_qb(i - 1)
                    transpose_k(i - 1)
            diag_scores(0, 0)
            quads = 0
            for n in range(NG):
                c = n // KVH
                late, ahead = n + LEAD - 1, n + LEAD
                if late < NT:
                    transpose_qa(late)
                diag_scores(n, 1)
                if n:
                    transpose_out(n - 1)
                pe.wait_ge(vd_staged, n + 1)
                weighted(v_diag[:, 2, :], 0, 3 * P, first=True)
                if late < NT:
                    transpose_qb(late)
                diag_scores(n, 2)
                weighted(v_diag[:, 1, :], 1, 2 * P)
                if late < NT:
                    transpose_k(late)
                if ahead < NT:
                    pe.wait_ge(qb_copied, ahead)
                    transpose_x(ahead)
                diag_scores(n, 3)
                weighted(v_diag[:, 0, :], 0, P)
                if ahead < NT:
                    pe.wait_ge(kk_copied, ahead)
                    project_qkv(ahead)
                if c:
                    transpose_attn(n - KVH)
                    with pe.Fori(0, c) as q:
                        for j in range(TPC):
                            k = first_kb[n] + TPC + j
                            for pr in range(2):
                                scores(n, pr, kT[:, bass.ds(q * (KVH * CH) + kcols(0, n % KVH, j), P)],
                                       q * (2 * TPC) + (2 * k + pr - 1))
                            if j == 0:
                                pe.wait_ge(vcd_staged, q + (n + quads + 1))
                            if j == 1:
                                pe.wait_ge(vab_staged, q + (quads + 1))
                            if j == 3:
                                pe.wait_ge(vcd_staged, q + (n + quads + 2))
                            rows = (v_cd[:, 1, :], v_ab[:, 0, :], v_ab[:, 1, :], v_cd[:, 0, :])[j]
                            weighted(rows, (j + 1) % 2, 0)
                    quads += c
                    project_out(n - KVH)
                if n + 1 < NG:
                    diag_scores(n + 1, 0)
                else:
                    pe.wait_ge(exp_done, 2 * first_kb[NG])
                pe.wait_ge(vcd_staged, n + quads + 1)
                weighted(v_cd[:, 1, :], 1, 0, last=True)
            transpose_out(NG - 1)
            for i in range(NT - TPC, NT):
                transpose_attn(i)
                project_out(i)

        @block.vector
        def _(dve):
            chain = Chain(dve, dve_seq)
            v = nc.vector

            def stats(c0, c1):
                ts = slice(c0 * TPC, c1 * TPC)
                for c in range(c0, c1):
                    dve.wait_ge(x_in[c], 16)
                    for i in range(c * TPC, (c + 1) * TPC):
                        chain.do(v.bn_stats(bn[:, i, :], x[:, i, :]))
                chain.sync()
                for i in range(c0 * TPC, c1 * TPC):
                    chain.do(v.bn_aggr(mv[:, i, :], bn[:, i, :]))
                chain.sync()
                chain.link(v.tensor_scalar(var[:, ts], mv[:, ts, 1], LN_EPS, None, ALU.add))
                rsqrt(nc, chain, rln[:, ts], var[:, ts], st1[:, ts], st2[:, ts])
                chain.link(v.tensor_tensor(var[:, ts], rln[:, ts], rln[:, ts], ALU.mult))
                chain.link(v.tensor_tensor(var[:, ts], var[:, ts], mv[:, ts, 1], ALU.mult))
                chain.link(v.tensor_scalar(var[:, ts], var[:, ts], RMS_EPS, None, ALU.add))
                rsqrt(nc, chain, rms[:, ts], var[:, ts], st1[:, ts], st2[:, ts])

            def normalise(i):
                v.tensor_scalar(x[:, i, :], x[:, i, :], mv[:, i, 0:1], rln[:, i:i + 1],
                                ALU.subtract, ALU.mult).then_inc(xn_ready, 1)

            def copy_xT(i):
                dve.wait_ge(xT_done, i + 1)
                if i:
                    dve.wait_ge(qkv_done, i)
                v.tensor_copy(xnT[:, :, :], bank_b[:, 0:D].rearrange("p (k t) -> p k t", k=KD)).then_inc(xT_copied, 1)

            def copy_qkv(i):
                dve.wait_ge(qkv_done, i + 1)
                v.tensor_scalar(b.qkv[:, :], bank_a[:, 0:QKW], rms[:, i:i + 1], None, ALU.mult).then_inc(qkv_copied, 1)
                v.tensor_scalar(vals[:, i // TPC, :, i % TPC, :], heads(bank_a[:, QKW:QKVW], KVH), rms[:, i:i + 1],
                                None, ALU.mult).then_inc(qkv_copied, 1)

            def split(i):
                dve.wait_ge(qkv_copied, 2 * (i + 1))
                rope_norm_split(nc, chain, b, w("cos", i), w("sin", i)).then_inc(split_ready, 1)

            def lay_q(i, bank, h0, done, copied):
                dve.wait_ge(done, i + 1)
                t0 = (i % TPC) * P
                v.tensor_copy(qT[:, (i // TPC) % 2, h0:h0 + 8, t0:t0 + P],
                              bank[:, :].bitcast(BF16)[:, 0:8 * P].rearrange("p (h t) -> p h t", h=8)).then_inc(copied, 1)

            def lay_k(i):
                dve.wait_ge(kk_done, i + 1)
                c, j = divmod(i, TPC)
                dst = kT[:, kcols(c, 0, 0):kcols(c + 1, 0, 0)].rearrange("p (h t) -> p h t", h=KVH)
                v.tensor_copy(dst[:, :, j * P:(j + 1) * P],
                              bank_a[:, :].bitcast(BF16)[:, 0:KVH * P].rearrange("p (h t) -> p h t", h=KVH)).then_inc(kk_copied, 1)

            def copy_out(n):
                dve.wait_ge(kb_done, first_kb[n + 1])
                if n:
                    dve.wait_ge(oT_done, n)
                v.tensor_copy(oT[:, :], out_acc[:, :]).then_inc(o_copied, 1)

            def normalise_out(n):
                c, kv = divmod(n, KVH)
                dve.wait_ge(oT_done, n + 1)
                if c >= 2:
                    dve.wait_ge(aT_done, TPC * (c - 1))
                o = bank_c[:, :].rearrange("p (m e) -> p m e", e=VW)
                chain.link(v.reciprocal(den[:, :], o[:, :, HD]))
                dst = attn[:, c % 2, :, kv * GQ * HD:(kv + 1) * GQ * HD]
                v.tensor_tensor(dst.rearrange("p t (h e) -> p t h e", h=GQ),
                                o[:, :, 0:HD].rearrange("p (t h) e -> p t h e", t=TPC),
                                den[:, :].rearrange("p (t h) -> p t h", t=TPC).unsqueeze(3).to_broadcast([P, TPC, GQ, HD]),
                                ALU.mult).then_inc(o_normed, 1)

            def copy_aT(i):
                dve.wait_ge(aT_done, i + 1)
                if i:
                    dve.wait_ge(proj_done, i)
                v.tensor_copy(attnT[:, :, :], bank_c[:, 0:D].rearrange("p (k t) -> p k t", k=KD)).then_inc(aT_copied, 1)

            def add_proj(i):
                dve.wait_ge(proj_done, i + 1)
                v.tensor_tensor(x[:, i, :], x[:, i, :], bank_b[:, 0:D], ALU.add).then_inc(proj_added, 1)

            dve.wait_ge(w_in, 16)
            dve.wait_ge(w_prod, 1)
            for k in range(KD):
                n1 = w("norm1")[:, k:k + 1]
                v.tensor_scalar(wqkv[:, k, 0:D], w("wq", k), n1, None, ALU.mult).then_inc(w_ready, 1)
                v.tensor_scalar(wqkv[:, k, D:QKVW], bank_a[:, k * P:(k + 1) * P], n1, None, ALU.mult).then_inc(w_ready, 1)
            stats(0, 2)
            for i in range(LEAD + 1):
                normalise(i)
            for i in range(LEAD):
                copy_xT(i)
                copy_qkv(i)
                if i:
                    lay_q(i - 1, bank_a, 0, qa_done, qa_copied)
                    lay_q(i - 1, bank_b, 8, qb_done, qb_copied)
                    lay_k(i - 1)
                split(i)
            for n in range(NG):
                late, ahead = n + LEAD - 1, n + LEAD
                if n:
                    copy_out(n - 1)
                if late < NT:
                    lay_q(late, bank_a, 0, qa_done, qa_copied)
                if n:
                    normalise_out(n - 1)
                if late < NT:
                    lay_q(late, bank_b, 8, qb_done, qb_copied)
                    lay_k(late)
                if ahead < NT:
                    copy_xT(ahead)
                    copy_qkv(ahead)
                if n >= KVH:
                    copy_aT(n - KVH)
                if n == 1:
                    stats(2, NCH)
                if ahead < NT:
                    split(ahead)
                if ahead + 1 < NT:
                    normalise(ahead + 1)
                if n >= KVH:
                    add_proj(n - KVH)
            copy_out(NG - 1)
            normalise_out(NG - 1)
            for i in range(NT - TPC, NT):
                copy_aT(i)
                add_proj(i)


def make_constants(nc, pool, g):
    gp = nc.gpsimd
    steps = [0]

    def link(ins):
        steps[0] += 1
        ins.then_inc(g.const_seq, 1)
        pool.wait_ge(g.const_seq, steps[0])

    link(gp.memset(g.zero[:, :], 0.0))
    link(gp.memset(g.identf[:, :], 0.0))
    link(gp.affine_select(out=g.identf[:, :], in_=g.identf[:, :], compare_op=ALU.not_equal, fill=1.0, base=0,
                          pattern=[[-1, P]], channel_multiplier=1))
    link(gp.tensor_copy(g.identb[:, :], g.identf[:, :]))
    link(gp.memset(g.causal[:, :], 0.0))
    gp.affine_select(out=g.causal[:, :], in_=g.causal[:, :], compare_op=ALU.is_ge, fill=NEG, base=0,
                     pattern=[[1, P]], channel_multiplier=-1).then_inc(g.ident_ready, 1)
    pool.wait_ge(g.ident_ready, 1)


def pack(columns):
    at, out = 0, {}
    for name, n in columns:
        out[name] = (at, n)
        at += n
    return out, at


PACKS = {
    "wa": pack([("kv_downT", D), ("kv_up", 2 * KVH * HD), ("wq", KD * D), ("norm1", KD), ("wo", KD * D),
                ("cos", NT * HD), ("sin", NT * HD)]),
    "wb": pack([("wqkv", KD * QKVW), ("norm2", KD), ("wo", KD * D), ("cos", NT * HD), ("sin", NT * HD)]),
    "wc": pack([("wq", KD * D), ("routersT", KD * D), ("valuesT", KD * D), ("woutT", KD * D)]),
    "wd": pack([("bias", D), ("ln_g", KD), ("ln_b", KD), ("po_b", D), ("in_WT", NL * 2 * DI), ("rms_w", NL),
                ("conv_w", NL * HALVES * TAPS), ("conv_b", NL * HALVES), ("dt_b", NL * HALVES), ("Dp", NL * HALVES),
                ("A_log", NL * HALVES * NS), ("xp_WT", NL * HALVES * XPW), ("dt_WT", NL * DI), ("mo_WT", NL * HALVES * P),
                ("po_WT", KD * D)]),
}
PIECE = {"wq": D, "wo": D, "wqkv": QKVW, "cos": HD, "sin": HD, "routersT": D, "valuesT": D, "woutT": D,
         "in_WT": 2 * DI, "conv_w": HALVES * TAPS, "conv_b": HALVES, "dt_b": HALVES, "Dp": HALVES, "xp_WT": XPW,
         "dt_WT": DI, "mo_WT": P, "po_WT": D}


def piece(tile, table):
    def w(name, k=None):
        at, n = table[name]
        if k is not None:
            n = PIECE[name]
            at += k * n
        return tile[:, at:at + n]
    return w


def build(nc, dram, out, upto=9):
    with ExitStack() as ctx:
        early = ctx.enter_context(ExitStack())

        def sb(stack, name, shape, dt=F32):
            return stack.enter_context(nc.sbuf_tensor(name, shape, dt))

        def sem(name):
            return ctx.enter_context(nc.semaphore(name))

        g = Tiles()
        g.x = sb(ctx, "x", [P, NT, D])
        g.identf, g.identb = sb(ctx, "identf", [P, P]), sb(ctx, "identb", [P, P], BF16)
        g.zero = sb(ctx, "zero", [P, 1])
        g.causal = sb(ctx, "causal", [P, P], BF16)
        g.w_gate, g.w_out = sb(ctx, "w_gate", [P, KD, D]), sb(ctx, "w_out", [P, KD, D])
        tiles = {name: sb(ctx if name == "wd" else early, name, [P, PACKS[name][1]]) for name in ("wd", "wa", "wb", "wc")}
        g.wa, g.later = tiles["wa"], tiles
        g.later_in = {name: sem(f"{name}_in") for name in ("wb", "wc", "wd")}
        g.wa_col = piece(g.wa, PACKS["wa"][0])
        g.xr_in, g.stored = sem("xr_in"), sem("stored")
        g.const_seq, g.ident_ready = sem("const_seq"), sem("ident_ready")
        g.dram, g.out = dram, out

        global_attention(nc, g, dram)
        local_attention(nc, g, dram)
        tree_ffn(nc, g, "fa", True, False)
        early.close()
        with ExitStack() as late:
            g.x1T, g.x2T, g.hT = (sb(late, name, [P, S]) for name in ("x1T", "x2T", "hT"))
            mamba_norms(nc, g)
            mamba_layers(nc, g)
            mamba_out(nc, g)
        tree_ffn(nc, g, "fb", False, True)


def rope_tables(base):
    inv = (np.float32(1.0) / np.float32(base) ** (np.arange(0, HD, 2, dtype=np.float32) / np.float32(HD))).astype(np.float32)
    ang = np.arange(S, dtype=np.float32)[:, None] * inv[None, :]
    cos, sin = np.cos(ang).astype(np.float32), np.sin(ang).astype(np.float32)
    cos2 = np.repeat(cos, 2, axis=1)
    sin2 = np.stack([-sin, sin], axis=2).reshape(S, HD)
    return [np.ascontiguousarray(t.reshape(NT, P, HD).transpose(1, 0, 2).reshape(P, NT * HD)) for t in (cos2, sin2)]


def lay_out(inputs):
    a = {k: np.asarray(v) for k, v in inputs.items()}

    def rows(m):
        return m.reshape(-1, P, m.shape[1]).transpose(1, 0, 2).reshape(P, -1)

    def pad(m):
        return np.concatenate([m, np.zeros((P - m.shape[0], m.shape[1]), m.dtype)], axis=0)

    def cols(v):
        return v.reshape(-1, P).T

    def everywhere(v):
        return np.broadcast_to(v[None, :], (P, v.shape[0]))

    ga, la, ff, mb = "L0_attn_a_g_", "L0_attn_a_l_", "L0_ffn_", "L0_attn_b_"
    halves = rows

    def layers(f):
        return np.concatenate([f(l) for l in range(NL)], axis=1)

    def xp_rows(l):
        m = a[mb + "xp_W"][l].T
        bc = m[:, DTR:]
        return rows(np.concatenate([bc, bc, bc, m[:, 0:DTR]], axis=1))

    def dt_rows(l):
        m = np.zeros((P, DI), np.float32)
        m[XPW - DTR:XPW] = a[mb + "dt_W"][l].T
        return m

    cg, sg = rope_tables(1000000.0)
    cl, sl = rope_tables(10000.0)
    parts = {
        "wa": dict(kv_downT=pad(a[ga + "kv_down"].T), kv_up=pad(np.concatenate([a[ga + "k_up"], a[ga + "v_up"]], axis=1)),
                   wq=rows(a[ga + "wq"]), norm1=cols(a["L0_attn_a_norm1_w"]), wo=rows(a[ga + "wo"]), cos=cg, sin=sg),
        "wb": dict(wqkv=rows(np.concatenate([a[la + "wq"], a[la + "wk"], a[la + "wv"]], axis=1)),
                   norm2=cols(a["L0_attn_a_norm2_w"]), wo=rows(a[la + "wo"]), cos=cl, sin=sl),
        "wc": dict(wq=rows(a[ff + "Wq"]),
                   routersT=rows(np.concatenate([a[ff + "routers"].T, np.zeros((D, 1), np.float32)], axis=1)),
                   valuesT=rows(a[ff + "leaf_values"].T), woutT=rows(a[ff + "Wout_w"].T)),
        "wd": dict(bias=everywhere(a[ff + "Wout_b"]), ln_g=cols(a[mb + "ln_g"]), ln_b=cols(a[mb + "ln_b"]),
                   po_b=everywhere(a[mb + "po_b"]), in_WT=layers(lambda l: a[mb + "in_W"][l].T),
                   rms_w=a[mb + "rms_w"].T, conv_w=layers(lambda l: halves(a[mb + "conv_w"][l, :, 0, :])),
                   conv_b=layers(lambda l: cols(a[mb + "conv_b"][l])), dt_b=layers(lambda l: cols(a[mb + "dt_b"][l])),
                   Dp=layers(lambda l: cols(a[mb + "Dp"][l])), A_log=layers(lambda l: halves(a[mb + "A_log"][l])),
                   xp_WT=layers(xp_rows), dt_WT=layers(dt_rows), mo_WT=layers(lambda l: rows(a[mb + "mo_W"][l].T)),
                   po_WT=rows(a[mb + "po_W"].T)),
    }
    arrays = {"x": np.ascontiguousarray(a["L0_attn_a_hidden"].reshape(NT, P, D).transpose(1, 0, 2))}
    for name, (table, width) in PACKS.items():
        whole = np.concatenate([parts[name][n] for n in table], axis=1)
        assert whole.shape == (P, width), (name, whole.shape, width)
        arrays[name] = np.ascontiguousarray(whole)
    return arrays


def local_attention(nc, g, dram):
    ctx = ExitStack()
    with ctx:
        def sb(name, shape, dt=F32):
            return ctx.enter_context(nc.sbuf_tensor("la_" + name, shape, dt))

        def sem(name):
            return ctx.enter_context(nc.semaphore("la_" + name))

        x, w = g.x, piece(g.later["wb"], PACKS["wb"][0])
        HALF = H // 2
        PW = WIN
        UNIT = 2 * CH + 2 * TPC * PW
        LAYS = 2 * TPC + 2
        wqkv = sb("wqkv", [P, KD, QKVW])
        xs = sb("xs", [P, TPC, D])
        xT = sb("xT", [P, TPC, KD, P])
        xr = sb("xr", [P, TPC, D])
        qk = sb("qk", [P, TPC * QKW])
        t1, t2 = sb("t1", [P, TPC * QKW]), sb("t2", [P, TPC * QKW])
        ss, rs, n1, n2 = (sb(n, [P, TPC * NQK]) for n in ("ss", "rs", "n1", "n2"))
        qn, kn = sb("qn", [P, TPC * H, HD]), sb("kn", [P, TPC * KVH, HD])
        qs, ks = sb("qs", [P, TPC * H, TERMS, HD], BF16), sb("ks", [P, TPC * KVH, TERMS, HD], BF16)
        qT = sb("qT", [P, H, CH], BF16)
        kT = sb("kT", [P, KVH, P + CH], BF16)
        vnew = sb("vnew", [P, TPC, KVH, HD])
        vals = sb("vals", [P, TPC + 1, KVH, VW])
        probs = sb("probs", [P, 2, 2, UNIT])
        oT = sb("oT", [P, CH])
        den = sb("den", [P, H])
        attn = sb("attn", [P, TPC, D])
        attnT = sb("attnT", [P, TPC, KD, P])
        bn, mv = sb("bn", [P, TPC, 6]), sb("mv", [P, TPC, 2])
        var, rms, s1, s2 = (sb(n, [P, TPC]) for n in ("var", "rms", "s1", "s2"))
        band = sb("band", [P, P], BF16)
        before = sb("before", [P, PW], BF16)

        score = [ctx.enter_context(nc.psum_tensor(f"la_score{i}", [P, UNIT], F32)) for i in range(2)]
        out_acc = ctx.enter_context(nc.psum_tensor("la_out_acc", [P, CH], F32))
        bank_p = ctx.enter_context(nc.psum_tensor("la_bank_p", [P, 512], F32))
        sbank = [score[i // 3][:, (i % 3) * 512:(i % 3 + 1) * 512] for i in range(6)]

        dve_seq, pool_seq, masks_ready, w_ready = sem("dve_seq"), sem("pool_seq"), sem("masks_ready"), sem("w_ready")
        xr_in, xr_added, xs_ready = g.xr_in, sem("xr_added"), sem("xs_ready")
        xT_done, xT_copied = sem("xT_done"), sem("xT_copied")
        qkv_done, qkv_copied, split_ready = sem("qkv_done"), sem("qkv_copied"), sem("split_ready")
        lay_done, lay_dve, lay_act = sem("lay_done"), sem("lay_dve"), sem("lay_act")
        k_moved, vals_ready = sem("k_moved"), sem("vals_ready")
        scores_done, exp_done, pv_done = sem("scores_done"), sem("exp_done"), sem("pv_done")
        o_copied, oT_done, o_normed = sem("o_copied"), sem("oT_done"), sem("o_normed")
        aT_done, aT_copied, proj_done, added = sem("aT_done"), sem("aT_copied"), sem("proj_done"), sem("added")

        def chunk(c):
            return x[:, bass.ds(c * TPC, TPC), :]

        def turns(eng, body):
            body(0, True, True)
            with eng.Fori(1, NCH - 2) as c:
                body(c, True, True)
            body(NCH - 2, True, False)
            body(NCH - 1, False, False)

        def qkv_bank(t):
            return (sbank[2], sbank[3], out_acc[:, :], bank_p[:, :])[t]

        def lay_views(n):
            bank = sbank[n % 6].bitcast(BF16)
            if n < 2 * TPC:
                t, half = divmod(n, 2)
                return (qT[:, half * HALF:(half + 1) * HALF, t * P:(t + 1) * P],
                        bank.rearrange("p (h t) -> p h t", h=HALF))
            t = 2 * (n - 2 * TPC)
            dst = kT[:, :, P + t * P:P + (t + 2) * P].rearrange("p h (t n) -> p t h n", t=2)
            return dst, bank.rearrange("p (t h n) -> p t h n", t=2, h=KVH)

        block = ctx.enter_context(nc.Block())

        @block.sync
        def _(sp):
            sp.dma_start(xr[:, :, :], dram["x"][:, 0:TPC, :]).then_inc(xr_in, 16)
            with sp.Fori(1, NCH) as c:
                sp.wait_ge(xr_added, c)
                sp.dma_start(xr[:, :, :], dram["x"][:, bass.ds(c * TPC, TPC), :]).then_inc(xr_in, 16)

        @block.gpsimd
        def _(pool):
            def copy(out, in_):
                zero = g.zero[:, 0:1]
                for _ in in_.shape[2:]:
                    zero = zero.unsqueeze(2)
                return nc.gpsimd.tensor_tensor(out, in_, zero.to_broadcast(list(in_.shape)), ALU.add)

            gp = nc.gpsimd
            chain = Chain(pool, pool_seq)
            for t in (band, before):
                chain.do(gp.memset(t[:, :], 0.0))
            chain.do(gp.memset(kT[:, :, 0:P], 0.0))
            chain.do(gp.memset(vals[:, :, :, :], 0.0))
            chain.sync()
            chain.link(gp.affine_select(out=band[:, :], in_=band[:, :], compare_op=ALU.is_ge, fill=NEG, base=0,
                                        pattern=[[1, P]], channel_multiplier=-1))
            gp.affine_select(out=band[:, :], in_=band[:, :], compare_op=ALU.is_gt, fill=NEG, base=WIN,
                             pattern=[[-1, P]], channel_multiplier=1).then_inc(masks_ready, 1)
            gp.affine_select(out=before[:, :], in_=before[:, :], compare_op=ALU.is_gt, fill=NEG, base=WIN - P,
                             pattern=[[-1, PW]], channel_multiplier=1).then_inc(masks_ready, 1)
            chain.link(gp.memset(vals[:, 1:TPC + 1, :, HD:HD + 1], 1.0))

            def new_values(c):
                pool.wait_ge(qkv_copied, c * (2 * TPC) + 2 * TPC)
                copy(vals[:, 1:TPC + 1, :, 0:HD], vnew[:, :, :, :]).then_inc(vals_ready, 1)

            def add_input(c):
                pool.wait_ge(xr_in, c * 16 + 16)
                pool.wait_ge(xs_ready, c + 1)
                gp.tensor_tensor(chunk(c), chunk(c), xr[:, :, :], ALU.add).then_inc(xr_added, 1)

            def turn(c, ahead, far):
                add_input(c)
                if ahead:
                    pool.wait_ge(scores_done, c * 8 + 8)
                    copy(kT[:, :, 0:P], kT[:, :, CH:P + CH]).then_inc(k_moved, 1)
                    pool.wait_ge(pv_done, c * KVH + KVH)
                    chain.link(copy(vals[:, 0, :, 0:HD + 1], vals[:, TPC, :, 0:HD + 1]))
                    new_values(c + 1)
                    chain.restart()

            new_values(0)
            chain.restart()
            turns(pool, turn)

        @block.scalar
        def _(act):
            def copy(out, in_, scale=1.0):
                return nc.scalar.activation(out, in_, ACT.Copy, scale=scale)

            def copy_xT(c):
                for p in range(2):
                    act.wait_ge(xT_done, c * 2 + (p + 1))
                    if p == 0:
                        act.wait_ge(qkv_done, c * TPC)
                    copy(xT[:, 2 * p:2 * p + 2, :, :].rearrange("p t k n -> p (t k n)"), sbank[p]).then_inc(xT_copied, 1)

            def copy_qkv(c):
                act.wait_ge(split_ready, c)
                act.wait_ge(vals_ready, c)
                for t in range(TPC):
                    act.wait_ge(qkv_done, c * TPC + (t + 1))
                    bank = qkv_bank(t)
                    copy(qk[:, t * QKW:(t + 1) * QKW], bank[:, 0:QKW]).then_inc(qkv_copied, 1)
                    copy(vnew[:, t, :, :], heads(bank[:, QKW:QKVW], KVH)).then_inc(qkv_copied, 1)

            def lay(c):
                for n in range(1, LAYS, 2):
                    act.wait_ge(lay_done, c * LAYS + (n + 1))
                    if n == LAYS - 1:
                        act.wait_ge(k_moved, c)
                    dst, src = lay_views(n)
                    copy(dst, src).then_inc(lay_act, 1)

            def turn(c, ahead, far):
                if ahead:
                    copy_xT(c + 1)
                    copy_qkv(c + 1)
                for kv in range(KVH):
                    for pr in range(2):
                        act.wait_ge(scores_done, c * 8 + (2 * kv + pr + 1))
                        nc.scalar.activation(probs[:, kv % 2, pr, :], score[pr][:, :], ACT.Exp,
                                             scale=SCORE_SCALE).then_inc(exp_done, 1)
                    if kv:
                        copy_out(c, kv - 1)
                copy_out(c, KVH - 1)
                if ahead:
                    lay(c + 1)
                for p in range(2):
                    act.wait_ge(aT_done, c * 2 + (p + 1))
                    if p == 0:
                        act.wait_ge(proj_done, c * 2)
                    copy(attnT[:, 2 * p:2 * p + 2, :, :].rearrange("p t k n -> p (t k n)"),
                         (out_acc, bank_p)[p][:, :]).then_inc(aT_copied, 1)

            def copy_out(c, kv):
                act.wait_ge(pv_done, c * KVH + (kv + 1))
                act.wait_ge(oT_done, c * KVH + kv)
                copy(oT[:, :], out_acc[:, :]).then_inc(o_copied, 1)

            copy_xT(0)
            copy_qkv(0)
            lay(0)
            turns(act, turn)

        @block.tensor
        def _(pe):
            mm, tr = nc.tensor.matmul, nc.tensor.transpose
            identf, identb = g.identf, g.identb

            def project(c):
                pe.wait_ge(xs_ready, c + 1)
                for p in range(2):
                    for t in range(2 * p, 2 * p + 2):
                        for k in range(KD):
                            at = ((t % 2) * KD + k) * P
                            last = tr(sbank[p][:, at:at + P], xs[:, t, k * P:(k + 1) * P], identf[:, :])
                    last.then_inc(xT_done, 1)
                for t in range(TPC):
                    if t % 2 == 0:
                        pe.wait_ge(xT_copied, c * 2 + (t // 2 + 1))
                    for k in range(KD):
                        last = mm(qkv_bank(t)[:, 0:QKVW], xT[:, t, k, :], wqkv[:, k, :], start=(k == 0), stop=(k == KD - 1))
                    last.then_inc(qkv_done, 1)

            def transpose_qk(c):
                pe.wait_ge(split_ready, c + 1)
                for n in range(LAYS):
                    if n >= 6:
                        pe.wait_ge((lay_dve, lay_act)[n % 2], c * (LAYS // 2) + (n - 6) // 2 + 1)
                    bank = sbank[n % 6].bitcast(BF16)
                    for m in range(HALF):
                        if n < 2 * TPC:
                            src = qs[:, (n // 2) * H + (n % 2) * HALF + m, :, :]
                        else:
                            src = ks[:, (n - 2 * TPC) * HALF + m, :, :]
                        last = tr(bank[:, m * P:(m + 1) * P], src.rearrange("p r e -> p (r e)"), identb[:, :])
                    last.then_inc(lay_done, 1)

            def scores(c, kv):
                for pr in range(2):
                    u = 2 * kv + pr
                    if kv:
                        pe.wait_ge(exp_done, c * 8 + (u - 1))
                    elif pr:
                        pe.wait_ge(added, c * 2)
                    s = score[pr]
                    for a in range(2):
                        mm(s[:, a * CH:(a + 1) * CH], identb[:, :], band[:, :].unsqueeze(1).to_broadcast([P, TPC, P]),
                           start=True, stop=False, skip_group_check=True)
                    mm(s[:, 2 * CH:UNIT], identb[:, :], before[:, :].unsqueeze(1).to_broadcast([P, 2 * TPC, PW]),
                       start=True, stop=False, skip_group_check=True)
                    for j in range(TPC):
                        for a in range(2):
                            h = kv * GQ + 2 * pr + a
                            mm(s[:, a * CH + j * P:a * CH + (j + 1) * P], kT[:, kv, (j + 1) * P:(j + 2) * P],
                               qT[:, h, j * P:(j + 1) * P], start=False, stop=True, skip_group_check=True)
                        for a in range(2):
                            h = kv * GQ + 2 * pr + a
                            at = 2 * CH + (a * TPC + j) * PW
                            last = mm(s[:, at:at + PW], kT[:, kv, j * P:(j + 1) * P],
                                      qT[:, h, j * P:j * P + PW], start=False, stop=True, skip_group_check=True)
                    last.then_inc(scores_done, 1)

            def weighted(c, kv):
                pe.wait_ge(exp_done, c * 8 + (2 * kv + 2))
                if kv:
                    pe.wait_ge(o_copied, c * KVH + kv)
                for j in range(TPC):
                    for own in (True, False):
                        for h in range(GQ):
                            a = h % 2
                            at, n = (a * CH + j * P, P) if own else (2 * CH + (a * TPC + j) * PW, PW)
                            last = mm(out_acc[h * VW:(h + 1) * VW, j * P:j * P + n], vals[:, j + own, kv, :],
                                      probs[:, kv % 2, h // 2, at:at + n], start=(j == 0 and own), stop=(j == TPC - 1 and not own),
                                      skip_group_check=True)
                last.then_inc(pv_done, 1)

            def transpose_out(c, kv):
                pe.wait_ge(o_copied, c * KVH + (kv + 1))
                if kv:
                    pe.wait_ge(o_normed, c * KVH + kv)
                for t in range(TPC):
                    last = tr(bank_p[:, t * P:(t + 1) * P], oT[:, t * P:(t + 1) * P], identf[:, :])
                last.then_inc(oT_done, 1)

            def project_out(c, ahead):
                pe.wait_ge(o_normed, c * KVH + KVH)
                for p in range(2):
                    for t in range(2 * p, 2 * p + 2):
                        for k in range(KD):
                            at = ((t % 2) * KD + k) * P
                            last = tr((out_acc, bank_p)[p][:, at:at + P], attn[:, t, k * P:(k + 1) * P], identf[:, :])
                    last.then_inc(aT_done, 1)
                for p in range(2):
                    pe.wait_ge(aT_copied, c * 2 + (p + 1))
                    if ahead:
                        pe.wait_ge((lay_dve, lay_act)[p], (c + 1) * (LAYS // 2) + 3)
                    for t in range(2 * p, 2 * p + 2):
                        for k in range(KD):
                            last = mm(sbank[4 + p][:, (t % 2) * D:(t % 2 + 1) * D], attnT[:, t, k, :], w("wo", k),
                                      start=(k == 0), stop=(k == KD - 1))
                    last.then_inc(proj_done, 1)

            def turn(c, ahead, far):
                pe.wait_ge(lay_dve, c * (LAYS // 2) + LAYS // 2)
                pe.wait_ge(lay_act, c * (LAYS // 2) + LAYS // 2)
                if ahead:
                    pe.wait_ge(aT_copied, c * 2)
                    project(c + 1)
                    pe.wait_ge(qkv_copied, c * (2 * TPC) + 4 * TPC)
                else:
                    pe.wait_ge(aT_copied, c * 2)
                scores(c, 0)
                pe.wait_ge(vals_ready, c + 1)
                for kv in range(1, KVH):
                    scores(c, kv)
                    if kv >= 2:
                        transpose_out(c, kv - 2)
                    weighted(c, kv - 1)
                transpose_out(c, KVH - 2)
                weighted(c, KVH - 1)
                transpose_out(c, KVH - 1)
                if ahead:
                    transpose_qk(c + 1)
                project_out(c, ahead)

            pe.wait_ge(w_ready, KD)
            pe.wait_ge(masks_ready, 2)
            project(0)
            transpose_qk(0)
            turns(pe, turn)

        @block.vector
        def _(dve):
            v = nc.vector
            chain = Chain(dve, dve_seq)

            def scale_x(c):
                src = chunk(c)
                for t in range(TPC):
                    chain.do(v.bn_stats(bn[:, t, :], src[:, t, :]))
                chain.sync()
                for t in range(TPC):
                    chain.do(v.bn_aggr(mv[:, t, :], bn[:, t, :]))
                chain.sync()
                chain.link(v.tensor_tensor(var[:, :], mv[:, :, 0], mv[:, :, 0], ALU.mult))
                chain.link(v.scalar_tensor_tensor(var[:, :], var[:, :], RMS_EPS, mv[:, :, 1], ALU.add, ALU.add))
                rsqrt(nc, chain, rms[:, :], var[:, :], s1[:, :], s2[:, :])
                dve.wait_ge(xT_done, c * 2)
                for t in range(TPC - 1):
                    chain.do(v.tensor_scalar(xs[:, t, :], src[:, t, :], rms[:, t:t + 1], None, ALU.mult))
                chain.sync()
                v.tensor_scalar(xs[:, TPC - 1, :], src[:, TPC - 1, :], rms[:, TPC - 1:TPC], None,
                                ALU.mult).then_inc(xs_ready, 1)

            def rope(c):
                dve.wait_ge(qkv_copied, c * (2 * TPC) + 2 * TPC)
                shape = [P, TPC, NQK, HD // 2]
                cos = w("cos")[:, bass.ds(c * (TPC * HD), TPC * HD)].rearrange("p (t e) -> p t e", t=TPC)
                sin = w("sin")[:, bass.ds(c * (TPC * HD), TPC * HD)].rearrange("p (t e) -> p t e", t=TPC)
                as4 = lambda a: a[:, :].rearrange("p (t h e) -> p t h e", t=TPC, h=NQK)
                chain.do(v.tensor_tensor(as4(t1), as4(qk), cos.unsqueeze(2).to_broadcast([P, TPC, NQK, HD]), ALU.mult))
                for e in range(2):
                    chain.do(v.tensor_tensor(as4(t2)[:, :, :, e::2], as4(qk)[:, :, :, 1 - e::2],
                                             sin[:, :, e::2].unsqueeze(2).to_broadcast(shape), ALU.mult))
                chain.sync()
                chain.link(v.tensor_tensor(t1[:, :], t1[:, :], t2[:, :], ALU.add))

            def norm(c):
                chain.link(v.tensor_tensor(t2[:, :], t1[:, :], t1[:, :], ALU.mult))
                chain.link(v.tensor_reduce(ss[:, :], t2[:, :].rearrange("p (h e) -> p h e", e=HD), AX, ALU.add))
                chain.link(v.tensor_scalar(ss[:, :], ss[:, :], 1.0 / HD, RMS_EPS, ALU.mult, ALU.add))
                rsqrt(nc, chain, rs[:, :], ss[:, :], n1[:, :], n2[:, :])
                src = t1[:, :].rearrange("p (t h e) -> p t h e", t=TPC, h=NQK)
                scale = rs[:, :].rearrange("p (t h) -> p t h", t=TPC)
                for dst, h0, h1 in ((qn, 0, H), (kn, H, NQK)):
                    chain.do(v.tensor_tensor(dst[:, :, :].rearrange("p (t h) e -> p t h e", t=TPC), src[:, :, h0:h1, :],
                                             scale[:, :, h0:h1].unsqueeze(3).to_broadcast([P, TPC, h1 - h0, HD]), ALU.mult))
                chain.sync()

            def split(c, part):
                q0, q1 = ((0, 3), (3, 6), (6, 8))[part]
                k0, k1 = ((0, 8), (1, 8), (2, 6))[part]
                nk = len(range(k0, k1, 3))
                if part == 0:
                    dve.wait_ge(lay_done, c * LAYS)
                chain.do(v.tensor_copy(qs[:, :, q0:q1, :], qn[:, :, :].unsqueeze(2).to_broadcast([P, TPC * H, q1 - q0, HD])))
                kc = v.tensor_copy(ks[:, :, k0:k1:3, :], kn[:, :, :].unsqueeze(2).to_broadcast([P, TPC * KVH, nk, HD]))
                if part == 2:
                    chain.sync()
                    kc.then_inc(split_ready, 1)
                    return
                chain.link(kc)
                chain.do(v.tensor_tensor(qn[:, :, :], qn[:, :, :], qs[:, :, q0, :], ALU.subtract))
                chain.link(v.tensor_tensor(kn[:, :, :], kn[:, :, :], ks[:, :, k0, :], ALU.subtract))

            def lay(c):
                for n in range(0, LAYS, 2):
                    dve.wait_ge(lay_done, c * LAYS + (n + 1))
                    if n == 2 * TPC:
                        dve.wait_ge(k_moved, c)
                    dst, src = lay_views(n)
                    v.tensor_copy(dst, src).then_inc(lay_dve, 1)

            def normalise_out(c, kv):
                dve.wait_ge(oT_done, c * KVH + (kv + 1))
                dve.wait_ge(aT_done, c * 2)
                o = bank_p[:, :].rearrange("p (m e) -> p m e", e=VW)
                chain.link(v.reciprocal(den[:, :], o[:, :, HD]))
                dst = attn[:, :, kv * GQ * HD:(kv + 1) * GQ * HD]
                v.tensor_tensor(dst.rearrange("p t (h e) -> p t h e", h=GQ),
                                o[:, :, 0:HD].rearrange("p (t h) e -> p t h e", t=TPC),
                                den[:, :].rearrange("p (t h) -> p t h", t=TPC).unsqueeze(3).to_broadcast([P, TPC, GQ, HD]),
                                ALU.mult).then_inc(o_normed, 1)

            def add_proj(c):
                dve.wait_ge(xr_added, c + 1)
                for p in range(2):
                    dve.wait_ge(proj_done, c * 2 + (p + 1))
                    dst = chunk(c)[:, 2 * p:2 * p + 2, :]
                    v.tensor_tensor(dst, dst, sbank[4 + p].rearrange("p (t d) -> p t d", t=2), ALU.add).then_inc(added, 1)

            def turn(c, ahead, far):
                if ahead:
                    rope(c + 1)
                    norm(c + 1)
                    normalise_out(c, 0)
                    split(c + 1, 0)
                    normalise_out(c, 1)
                    split(c + 1, 1)
                    normalise_out(c, 2)
                    split(c + 1, 2)
                    normalise_out(c, 3)
                    lay(c + 1)
                else:
                    for kv in range(KVH):
                        normalise_out(c, kv)
                add_proj(c)
                if far:
                    scale_x(c + 2)
                if ahead:
                    chain.restart()

            dve.wait_ge(g.later_in["wb"], 16)
            for k in range(KD):
                v.tensor_scalar(wqkv[:, k, :], w("wqkv", k), w("norm2")[:, k:k + 1], None, ALU.mult).then_inc(w_ready, 1)
            scale_x(0)
            rope(0)
            norm(0)
            for part in range(3):
                split(0, part)
            lay(0)
            scale_x(1)
            chain.restart()
            turns(dve, turn)


def tree_ffn(nc, g, tag, first, store):
    ctx = ExitStack()
    with ctx:
        def sb(name, shape, dt=F32):
            return ctx.enter_context(nc.sbuf_tensor(f"{tag}_{name}", shape, dt))

        def sem(name):
            return ctx.enter_context(nc.semaphore(f"{tag}_{name}"))

        x, w = g.x, piece(g.later["wc"], PACKS["wc"][0])
        DEPTH = 8
        xs = sb("xs", [P, TPC, D])
        xT = sb("xT", [P, TPC, KD, P])
        gate = sb("gate", [P, TPC, D])
        leaf = [sb(f"leaf{i}", [P, TPC, D]) for i in range(2)]
        leafT = sb("leafT", [P, TPC, KD, P])
        bn, mv = sb("bn", [P, TPC, 6]), sb("mv", [P, TPC, 2])
        var, rstd, s1, s2 = (sb(n, [P, TPC]) for n in ("var", "rstd", "s1", "s2"))

        def banks(name):
            return [ctx.enter_context(nc.psum_tensor(f"{tag}_{name}{i}", [P, 512], F32)) for i in range(2)]

        bank_x, bank_g, bank_l, bank_o = banks("bank_x"), banks("bank_g"), banks("bank_l"), banks("bank_o")
        dve_seq, w_prod, w_ready = sem("dve_seq"), sem("w_prod"), sem("w_ready")
        xs_ready, biased = sem("xs_ready"), sem("biased")
        xT_done, xT_copied, logits_done, gates_ready = sem("xT_done"), sem("xT_copied"), sem("logits_done"), sem("gates_ready")
        leaf_ready, leafT_done, leafT_copied = sem("leaf_ready"), sem("leafT_done"), sem("leafT_copied")
        out_done, added, stored = sem("out_done"), sem("added"), g.stored

        def chunk(c):
            return x[:, bass.ds(c * TPC, TPC), :]

        def turns(eng, body):
            body(0, True, True)
            with eng.Fori(1, NCH - 2) as c:
                body(c, True, True)
            body(NCH - 2, True, False)
            body(NCH - 1, False, False)

        block = ctx.enter_context(nc.Block())

        if store:
            @block.sync
            def _(sp):
                with sp.Fori(0, NCH) as c:
                    sp.wait_ge(added, c * 2 + 2)
                    sp.dma_start(g.out[:, bass.ds(c * TPC, TPC), :], chunk(c)).then_inc(stored, 16)
                sp.wait_ge(stored, 16 * NCH)

        @block.gpsimd
        def _(pool):
            pool.wait_ge(g.later_in["wd"], 16)
            with pool.Fori(0, NCH) as c:
                pool.wait_ge(xs_ready, c + 1)
                nc.gpsimd.tensor_tensor(chunk(c), chunk(c), piece(g.later["wd"], PACKS["wd"][0])("bias").unsqueeze(1).to_broadcast([P, TPC, D]),
                                        ALU.add).then_inc(biased, 1)

        @block.scalar
        def _(act):
            def copy(out, in_):
                return nc.scalar.activation(out, in_, ACT.Copy)

            def gates(c):
                for p in range(2):
                    act.wait_ge(xT_done, c * 2 + (p + 1))
                    if p == 0:
                        act.wait_ge(logits_done, c * 2)
                    copy(xT[:, 2 * p:2 * p + 2, :, :].rearrange("p t k n -> p (t k n)"), bank_x[p][:, :]).then_inc(xT_copied, 1)
                act.wait_ge(leaf_ready, c)
                for p in range(2):
                    act.wait_ge(logits_done, c * 2 + (p + 1))
                    nc.scalar.activation(gate[:, 2 * p:2 * p + 2, :].rearrange("p t n -> p (t n)"), bank_g[p][:, :],
                                         ACT.Sigmoid).then_inc(gates_ready, 1)

            def turn(c, ahead, far):
                if ahead:
                    gates(c + 1)
                for p in range(2):
                    act.wait_ge(leafT_done, c * 2 + (p + 1))
                    if p == 0:
                        act.wait_ge(out_done, c * 2)
                    copy(leafT[:, 2 * p:2 * p + 2, :, :].rearrange("p t k n -> p (t k n)"), bank_l[p][:, :]).then_inc(leafT_copied, 1)

            gates(0)
            turns(act, turn)

        @block.tensor
        def _(pe):
            mm, tr = nc.tensor.matmul, nc.tensor.transpose

            def transposed(src, banks, done):
                for p in range(2):
                    for t in range(2 * p, 2 * p + 2):
                        for k in range(KD):
                            at = ((t % 2) * KD + k) * P
                            last = tr(banks[p][:, at:at + P], src[:, t, k * P:(k + 1) * P], g.identf[:, :])
                    last.then_inc(done, 1)

            def product(src, weight, banks, done, ready, c):
                for p in range(2):
                    pe.wait_ge(ready, c * 2 + (p + 1))
                    for t in range(2 * p, 2 * p + 2):
                        for k in range(KD):
                            last = mm(banks[p][:, (t % 2) * D:(t % 2 + 1) * D], src[:, t, k, :], weight[:, k, :],
                                      start=(k == 0), stop=(k == KD - 1))
                    last.then_inc(done, 1)

            def logits(c):
                pe.wait_ge(xs_ready, c + 1)
                transposed(xs, bank_x, xT_done)
                pe.wait_ge(gates_ready, c * 2)
                product(xT, g.w_gate, bank_g, logits_done, xT_copied, c)

            def turn(c, ahead, far):
                if ahead:
                    logits(c + 1)
                pe.wait_ge(leaf_ready, c + 1)
                transposed(leaf[DEPTH % 2], bank_l, leafT_done)
                pe.wait_ge(added, c * 2)
                product(leafT, g.w_out, bank_o, out_done, leafT_copied, c)

            if first:
                pe.wait_ge(g.later_in["wc"], 16)
                for banks_, a, b in ((bank_g, "wq", "routersT"), (bank_o, "valuesT", "woutT")):
                    for m in range(KD):
                        for k in range(KD):
                            last = mm(banks_[m][:, 0:D], w(a, k)[:, m * P:(m + 1) * P], w(b, k), start=(k == 0), stop=(k == KD - 1))
                        last.then_inc(w_prod, 1)
                pe.wait_ge(w_ready, 2 * KD)
            logits(0)
            turns(pe, turn)

        @block.vector
        def _(dve):
            v = nc.vector
            chain = Chain(dve, dve_seq)

            def normalise(c):
                src = chunk(c)
                for t in range(TPC):
                    chain.do(v.bn_stats(bn[:, t, :], src[:, t, :]))
                chain.sync()
                for t in range(TPC):
                    chain.do(v.bn_aggr(mv[:, t, :], bn[:, t, :]))
                chain.sync()
                chain.link(v.tensor_scalar(var[:, :], mv[:, :, 1], LN_EPS, None, ALU.add))
                rsqrt(nc, chain, rstd[:, :], var[:, :], s1[:, :], s2[:, :])
                dve.wait_ge(xT_done, c * 2)
                for t in range(TPC):
                    last = v.tensor_scalar(xs[:, t, :], src[:, t, :], mv[:, t, 0:1], rstd[:, t:t + 1], ALU.subtract, ALU.mult)
                    if t < TPC - 1:
                        chain.do(last)
                last.then_inc(xs_ready, 1)
                chain.sync()

            def leaves(c):
                dve.wait_ge(gates_ready, c * 2 + 2)
                dve.wait_ge(leafT_done, c * 2)
                chain.do(v.tensor_copy(leaf[1][:, :, 1:2], gate[:, :, 0:1]))
                chain.link(v.tensor_scalar(leaf[1][:, :, 0:1], gate[:, :, 0:1], -1.0, 1.0, ALU.mult, ALU.add))
                for level in range(1, DEPTH):
                    n = 2 ** level
                    a, b = leaf[level % 2], leaf[(level + 1) % 2]
                    chain.link(v.tensor_tensor(b[:, :, 1:2 * n:2], a[:, :, 0:n], gate[:, :, n - 1:2 * n - 1], ALU.mult))
                    last = v.tensor_tensor(b[:, :, 0:2 * n:2], a[:, :, 0:n], b[:, :, 1:2 * n:2], ALU.subtract)
                    if level < DEPTH - 1:
                        chain.link(last)
                last.then_inc(leaf_ready, 1)

            def add_out(c):
                dve.wait_ge(biased, c + 1)
                for p in range(2):
                    dve.wait_ge(out_done, c * 2 + (p + 1))
                    dst = chunk(c)[:, 2 * p:2 * p + 2, :]
                    v.tensor_tensor(dst, dst, bank_o[p][:, :].rearrange("p (t d) -> p t d", t=2), ALU.add).then_inc(added, 1)

            def turn(c, ahead, far):
                leaves(c)
                if far:
                    normalise(c + 2)
                add_out(c)
                if ahead:
                    chain.sync()
                    chain.restart()

            if first:
                for m, (banks_, dst) in enumerate(((bank_g, g.w_gate), (bank_o, g.w_out))):
                    for k in range(KD):
                        dve.wait_ge(w_prod, m * KD + k + 1)
                        v.tensor_copy(dst[:, k, :], banks_[k][:, 0:D]).then_inc(w_ready, 1)
            normalise(0)
            normalise(1)
            chain.restart()
            turns(dve, turn)


def mamba_norms(nc, g):
    ctx = ExitStack()
    with ctx:
        def sb(name, shape, dt=F32):
            return ctx.enter_context(nc.sbuf_tensor("mn_" + name, shape, dt))

        def sem(name):
            return ctx.enter_context(nc.semaphore("mn_" + name))

        x, w = g.x, piece(g.later["wd"], PACKS["wd"][0])
        xs = sb("xs", [P, 2, TPC, D])
        bn, mv = sb("bn", [P, NT, 6]), sb("mv", [P, NT, 2])
        var, rln, rln2, s1, s2 = (sb(n, [P, NT]) for n in ("var", "rln", "rln2", "s1", "s2"))
        bank = [[ctx.enter_context(nc.psum_tensor(f"mn_bank{i}{k}", [P, CH], F32)) for k in range(KD)] for i in range(2)]
        dve_seq, xs_ready, xT_done, xT_copied, biased = (sem("dve_seq"), sem("xs_ready"), sem("xT_done"),
                                                         sem("xT_copied"), sem("biased"))
        block = ctx.enter_context(nc.Block())

        def pairs(eng, body):
            for b in range(2):
                body(b, b)
            with eng.Fori(1, NCH // 2) as i:
                for b in range(2):
                    body(i * 2 + b, b)

        @block.gpsimd
        def _(pool):
            def turn(c, b):
                pool.wait_ge(xs_ready, c + 1)
                nc.gpsimd.tensor_tensor(x[:, bass.ds(c * TPC, TPC), :], x[:, bass.ds(c * TPC, TPC), :],
                                        w("po_b").unsqueeze(1).to_broadcast([P, TPC, D]), ALU.add).then_inc(biased, 1)
            pairs(pool, turn)

        @block.scalar
        def _(act):
            def turn(c, b):
                for k in range(KD):
                    act.wait_ge(xT_done, c * KD + (k + 1))
                    nc.scalar.activation((g.x1T, g.x2T)[k][:, bass.ds(c * CH, CH)], bank[b][k][:, :], ACT.Identity,
                                         scale=w("ln_g")[:, k:k + 1], bias=w("ln_b")[:, k:k + 1]).then_inc(xT_copied, 1)
            pairs(act, turn)

        @block.tensor
        def _(pe):
            def turn(c, b):
                pe.wait_ge(xs_ready, c + 1)
                for k in range(KD):
                    if not isinstance(c, int):
                        pe.wait_ge(xT_copied, c * KD + (k + 1 - 2 * KD))
                    for t in range(TPC):
                        last = nc.tensor.transpose(bank[b][k][:, t * P:(t + 1) * P], xs[:, b, t, k * P:(k + 1) * P], g.identf[:, :])
                    last.then_inc(xT_done, 1)
            pairs(pe, turn)

        @block.vector
        def _(dve):
            v = nc.vector
            chain = Chain(dve, dve_seq)
            dve.wait_ge(g.later_in["wd"], 16)
            for i in range(NT):
                chain.do(v.bn_stats(bn[:, i, :], x[:, i, :]))
            chain.sync()
            for i in range(NT):
                chain.do(v.bn_aggr(mv[:, i, :], bn[:, i, :]))
            chain.sync()
            chain.link(v.tensor_scalar(var[:, :], mv[:, :, 1], LN_EPS, None, ALU.add))
            rsqrt(nc, chain, rln[:, :], var[:, :], s1[:, :], s2[:, :])
            chain.link(v.tensor_tensor(var[:, :], rln[:, :], rln[:, :], ALU.mult))
            chain.link(v.tensor_tensor(var[:, :], var[:, :], mv[:, :, 1], ALU.mult))
            chain.link(v.tensor_scalar(var[:, :], var[:, :], MAMBA_EPS, None, ALU.add))
            rsqrt(nc, chain, rln2[:, :], var[:, :], s1[:, :], s2[:, :])
            chain.link(v.tensor_tensor(rln[:, :], rln[:, :], rln2[:, :], ALU.mult))
            chain.restart()
            for c in range(NCH):
                if c >= 2:
                    dve.wait_ge(xT_done, KD * (c - 1))
                for t in range(TPC):
                    i = c * TPC + t
                    last = v.tensor_scalar(xs[:, c % 2, t, :], x[:, i, :], mv[:, i, 0:1], rln[:, i:i + 1], ALU.subtract, ALU.mult)
                    if t < TPC - 1:
                        chain.do(last)
                last.then_inc(xs_ready, 1)


def mamba_layers(nc, g):
    STEPS = 2 * NS
    BCR = 2 * NS
    ctx = ExitStack()
    with ctx:
        def sb(name, shape, dt=F32):
            return ctx.enter_context(nc.sbuf_tensor("mb_" + name, shape, dt))

        def sem(name):
            return ctx.enter_context(nc.semaphore("mb_" + name))

        w = piece(g.later["wd"], PACKS["wd"][0])
        x1T, x2T, hT = g.x1T, g.x2T, g.hT
        decay, decay_neg = (sb(n, [P, NL * 2 * NS]) for n in ("decay", "decay_neg"))
        rB = sb("rB", [P, TPC, P])
        ms, rr, mhalf = sb("ms", [P, TPC]), sb("rr", [P, TPC]), sb("mhalf", [P, TPC])
        mean_w, zeros = sb("mean_w", [P, 1]), sb("zeros", [P, 2 * TAPS])
        pick = sb("pick", [3 * BCR, BCR], BF16)
        hn = sb("hn", [P, CH])
        xpad = sb("xpad", [P, 2, TAPS - 1 + CH])
        conv = sb("conv", [P, 2, CH])
        xc, zs = sb("xc", [P, 2, 2, CH]), sb("zs", [P, 2, 2, CH])
        delta, u = sb("delta", [P, 2, 2, CH]), sb("u", [P, 2, 2, CH])
        proj = sb("proj", [3 * BCR + DTR, CH])
        bc = sb("bc", [3 * BCR, 2, CH], BF16)
        rest = sb("rest", [2 * BCR, CH])
        ea, lg, rl = sb("ea", [P, 2, CH]), sb("lg", [P, 2, CH]), sb("rl", [P, 2, CH])
        w1 = sb("w1", [P, 2, CH])
        yz = sb("yz", [P, 2, CH])
        bsb = sb("bsb", [P, 2, CH])
        RX, RH, RC = 4, 6, 4
        dbx, hs, hc = sb("dbx", [P, RX, CH]), sb("hs", [P, RH, CH]), sb("hc", [P, RC, CH])
        carry = sb("carry", [P, STEPS])

        def bank(name):
            return ctx.enter_context(nc.psum_tensor("mb_" + name, [P, CH], F32))

        ybank, cbank, abank = ([bank(f"{n}{i}") for i in range(2)] for n in ("y", "c", "a"))
        bbank, fbank = bank("b"), bank("f")

        (const_seq, consts, w_ready, sq_ready, ms_done, ms_ready, rr_ready, rB_ready, rB_done, hn_ready, xz_done, xz_copied,
         tail_moved, conv_seq, conv_done, xc_ready, z_ready, xp_done, p_copied, bc1, rest1, bc2, rest2, bc_ready, dt_done, dt_read,
         e_ready, l_ready, pool_seq, delta_ready, u_ready, b_done, b_copied, c_done, da_done, dbx_done, scan_done, hc_done,
         y_acc, y_read, yz_ready, mo_done, h_seq, h_added, carried, inw_ready, conv_done0, decay_ready, w1_ready) = (sem(n) for n in (
             "const_seq", "consts", "w_ready", "sq_ready", "ms_done", "ms_ready", "rr_ready", "rB_ready", "rB_done", "hn_ready", "xz_done",
             "xz_copied", "tail_moved", "conv_seq", "conv_done", "xc_ready", "z_ready", "xp_done", "p_copied", "bc1", "rest1", "bc2",
             "rest2", "bc_ready", "dt_done", "dt_read", "e_ready", "l_ready", "pool_seq", "delta_ready", "u_ready", "b_done",
             "b_copied", "c_done", "da_done", "dbx_done", "scan_done", "hc_done", "y_acc", "y_read", "yz_ready", "mo_done",
             "h_seq", "h_added", "carried", "inw_ready", "conv_done0", "decay_ready", "w1_ready"))

        def slab(ap, c):
            return ap[:, bass.ds(c * CH, CH)]

        def turns(eng, first, body):
            first(0, 0, 0, 0)
            for b in range(2):
                body(b, 0, b, b, (b + 1, 0, b + 1, 1 - b))
            for l in range(NL):
                with eng.Fori(1 if l == 0 else 0, NCH // 2 - 1) as i:
                    for b in range(2):
                        c = i * 2 + b
                        body(c + l * NCH, l, c, b, (c + (l * NCH + 1), l, c + 1, 1 - b))
                c, m = NCH - 2, l * NCH + NCH - 2
                body(m, l, c, 0, (m + 1, l, c + 1, 1))
                body(m + 1, l, c + 1, 1, (m + 2, l + 1, 0, 0) if l + 1 < NL else None)

        block = ctx.enter_context(nc.Block())

        @block.gpsimd
        def _(pool):
            gp = nc.gpsimd
            setup = Chain(pool, const_seq)
            for t, val in ((mhalf, -0.5), (mean_w, 1.0 / P), (zeros, 0.0), (carry, 0.0)):
                gp.memset(t[:, :], val).then_inc(consts, 1)
            setup.link(gp.memset(pick[:, :], 0.0))
            for q in range(3):
                ins = gp.affine_select(out=pick[:, :], in_=pick[:, :], compare_op=ALU.not_equal, fill=1.0, base=-q * BCR,
                                       pattern=[[-1, BCR]], channel_multiplier=1)
                if q < 2:
                    setup.link(ins)
            ins.then_inc(consts, 1)
            pool.wait_ge(consts, 5)

            def norm_power(f):
                pool.wait_ge(ms_ready, f + 1)
                gp.tensor_tensor(rr[:, :], ms[:, :], mhalf[:, :], ALU.pow).then_inc(rr_ready, 1)

            def rest_1(f, b):
                pool.wait_ge(bc1, f + 1)
                gp.tensor_tensor(rest[:, :], proj[0:2 * BCR, :], bc[0:2 * BCR, b, :], ALU.subtract).then_inc(rest1, 1)

            def rest_2(f, b):
                pool.wait_ge(bc2, f + 1)
                gp.tensor_tensor(rest[0:BCR, :], rest[0:BCR, :], bc[0:BCR, b, :], ALU.subtract).then_inc(rest2, 1)

            def softplus_sum(f, b):
                seq = pool_seq
                pool.wait_ge(w1_ready, f + 1)
                gp.tensor_tensor(w1[:, :, :], ea[:, :, :], w1[:, :, :], ALU.subtract).then_inc(seq, 1)
                pool.wait_ge(seq, f * 2 + 1)
                pool.wait_ge(l_ready, f + 1)
                gp.tensor_tensor(w1[:, :, :], w1[:, :, :], lg[:, :, :], ALU.add).then_inc(seq, 1)
                pool.wait_ge(seq, f * 2 + 2)
                gp.tensor_tensor(delta[:, b, :, :], w1[:, :, :], rl[:, :, :], ALU.add).then_inc(delta_ready, 1)

            def first(f, l, c, b):
                norm_power(f)
                rest_1(f, b)
                rest_2(f, b)
                softplus_sum(f, b)

            def body(m, l, c, b, nxt):
                pool.wait_ge(u_ready, m + 1)
                pool.wait_ge(scan_done, m * STEPS)
                for n in range(NS):
                    pool.wait_ge(b_copied, m * NS + (n + 1))
                    for half in range(2):
                        s = 2 * n + half
                        if s >= RX:
                            pool.wait_ge(scan_done, m * STEPS + (s - RX + 1))
                        gp.tensor_tensor(dbx[:, s % RX, :], u[:, b, half, :], bsb[:, n % 2, :], ALU.mult).then_inc(dbx_done, 1)
                    if nxt:
                        f, _, _, fb = nxt
                        if n == 3:
                            norm_power(f)
                        if n == 12:
                            rest_1(f, fb)
                        if n == 13:
                            rest_2(f, fb)
                        if n == 15:
                            softplus_sum(f, fb)

            turns(pool, first, body)

        @block.scalar
        def _(act):
            def fn(out, in_, func=ACT.Copy, **kw):
                return nc.scalar.activation(out, in_, func, **kw)

            def square(f, l, c):
                if l:
                    act.wait_ge(h_added, c + 1)
                act.wait_ge(xz_done, f * 4)
                fn(hn[:, :], slab((x1T, hT)[l], c), ACT.Square).then_inc(sq_ready, 1)

            def mean_square(f):
                act.wait_ge(ms_done, f + 1)
                fn(ms[:, :], fbank[:, 0:TPC], bias=MAMBA_EPS).then_inc(ms_ready, 1)

            def spread_norm(f):
                act.wait_ge(rr_ready, f + 1)
                fn(rB[:, :, :], rr[:, :].unsqueeze(2).to_broadcast([P, TPC, P])).then_inc(rB_ready, 1)

            def copy_xz(f, c, b, e):
                if e == 0:
                    act.wait_ge(conv_done, f)
                    src = zeros[:, 0:2 * (TAPS - 1)].rearrange("p (h t) -> p h t", h=2) if isinstance(c, int) and c == 0 \
                        else xpad[:, :, CH:CH + TAPS - 1]
                    fn(xpad[:, :, 0:TAPS - 1], src).then_inc(tail_moved, 1)
                    act.wait_ge(tail_moved, f + 1)
                act.wait_ge(xz_done, f * 4 + (e + 1))
                fn(xpad[:, e, TAPS - 1:] if e < 2 else zs[:, b, e - 2, :], fbank[:, :]).then_inc(xz_copied, 1)

            def silus(f, l, b):
                for half in range(2):
                    act.wait_ge((conv_done0, conv_done)[half], f + 1)
                    fn(xc[:, b, half, :], conv[:, half, :], ACT.Silu,
                       bias=w("conv_b", l)[:, half:half + 1]).then_inc(xc_ready, 1)
                act.wait_ge(xz_copied, f * 4 + 4)
                fn(zs[:, b, :, :], zs[:, b, :, :], ACT.Silu).then_inc(z_ready, 1)

            def part_1(f, b):
                act.wait_ge(xp_done, f + 1)
                fn(proj[:, :], fbank[0:3 * BCR + DTR, :]).then_inc(p_copied, 1)
                act.wait_ge(p_copied, f + 1)
                fn(bc[:, b, :], proj[0:3 * BCR, :]).then_inc(bc1, 1)

            def part_2(f, b):
                act.wait_ge(rest1, f + 1)
                fn(bc[0:2 * BCR, b, :], rest[:, :]).then_inc(bc2, 1)

            def part_3(f, b):
                act.wait_ge(rest2, f + 1)
                fn(bc[0:BCR, b, :], rest[0:BCR, :]).then_inc(bc_ready, 1)

            def abs_relu(f, l, half):
                act.wait_ge(dt_done, f * 2 + (half + 1))
                if half == 0:
                    act.wait_ge(delta_ready, f)
                bias = w("dt_b", l)[:, half:half + 1]
                fn(ea[:, half, :], fbank[:, :], ACT.Abs, bias=bias).then_inc(dt_read, 1)
                fn(rl[:, half, :], fbank[:, :], ACT.Relu, bias=bias).then_inc(dt_read, 1)

            def exp_ln(f):
                act.wait_ge(dt_read, f * 4 + 4)
                fn(ea[:, :, :], ea[:, :, :], ACT.Exp, scale=-1.0).then_inc(e_ready, 1)
                act.wait_ge(e_ready, f + 1)
                fn(lg[:, :, :], ea[:, :, :], ACT.Ln, bias=1.0).then_inc(l_ready, 1)

            def first(f, l, c, b):
                act.wait_ge(g.later_in["wd"], 16)
                fn(decay[:, :], w("A_log"), ACT.Exp).then_inc(w_ready, 1)
                act.wait_ge(consts, 5)
                square(f, l, c)
                mean_square(f)
                spread_norm(f)
                for e in range(4):
                    copy_xz(f, c, b, e)
                silus(f, l, b)
                part_1(f, b)
                part_2(f, b)
                part_3(f, b)
                for half in range(2):
                    abs_relu(f, l, half)
                exp_ln(f)

            def copy_b(m, n):
                act.wait_ge(b_done, m * NS + (n + 1))
                if n >= 2:
                    act.wait_ge(dbx_done, m * STEPS + (2 * n - 2))
                fn(bsb[:, n % 2, :], bbank[:, :]).then_inc(b_copied, 1)

            def carry_on(m, s, end):
                act.wait_ge(scan_done, m * STEPS + (s + 1))
                src = zeros[:, 0:1] if end else hs[:, s % RH, CH - 1:CH]
                fn(carry[:, s:s + 1], src).then_inc(carried, 1)

            def body(m, l, c, b, nxt):
                LAG = 3
                end = nxt is None or nxt[1] != l
                act.wait_ge(decay_ready, 1)
                act.wait_ge(delta_ready, m + 1)
                copy_b(m, 0)
                for n in range(NS):
                    if n + 1 < NS:
                        copy_b(m, n + 1)
                    for half in range(2):
                        s = 2 * n + half
                        if s >= 2:
                            act.wait_ge(scan_done, m * STEPS + (s - 1))
                        at = (l * 2 + half) * NS + n
                        fn(abank[s % 2][:, :], delta[:, b, half, :], ACT.Exp, scale=decay_neg[:, at:at + 1]).then_inc(da_done, 1)
                        if s >= LAG:
                            carry_on(m, s - LAG, end)
                    if nxt:
                        f, fl, fc, fb = nxt
                        if n == 0:
                            square(f, fl, fc)
                        if n == 2:
                            mean_square(f)
                        if n == 3:
                            spread_norm(f)
                        if 5 <= n < 9:
                            copy_xz(f, fc, fb, n - 5)
                        if n == 10:
                            silus(f, fl, fb)
                        if n == 11:
                            part_1(f, fb)
                        if n == 12:
                            part_2(f, fb)
                            abs_relu(f, fl, 0)
                        if n == 13:
                            part_3(f, fb)
                            abs_relu(f, fl, 1)
                            exp_ln(f)
                for s in range(STEPS - LAG, STEPS):
                    carry_on(m, s, end)

            turns(act, first, body)

        @block.tensor
        def _(pe):
            mm = nc.tensor.matmul

            def mean_sq(f, l):
                pe.wait_ge(sq_ready, f + 1)
                for t in range(TPC):
                    last = mm(fbank[:, t:t + 1], hn[:, t * P:(t + 1) * P], mean_w[:, :], start=True, stop=True)
                last.then_inc(ms_done, 1)

            def spread_rows(f):
                pe.wait_ge(rB_ready, f + 1)
                for t in range(TPC):
                    last = mm(fbank[:, t * P:(t + 1) * P], rB[:, t, :], g.identf[:, :], start=True, stop=True)
                last.then_inc(rB_done, 1)

            def in_proj(f, l, e):
                if e == 0:
                    pe.wait_ge(hn_ready, f + 1)
                else:
                    pe.wait_ge(xz_copied, f * 4 + e)
                mm(fbank[:, :], w("in_WT", l)[:, e * P:(e + 1) * P], hn[:, :], start=True, stop=True).then_inc(xz_done, 1)

            def x_proj(f, l, b):
                pe.wait_ge(xz_copied, f * 4 + 4)
                pe.wait_ge(xc_ready, f * 2 + 2)
                for half in range(2):
                    last = mm(fbank[0:3 * BCR + DTR, :], w("xp_WT", l * 2 + half), xc[:, b, half, :], start=(half == 0), stop=(half == 1))
                last.then_inc(xp_done, 1)

            def dt_proj(f, l, half):
                if half == 0:
                    pe.wait_ge(p_copied, f + 1)
                else:
                    pe.wait_ge(dt_read, f * 4 + 2)
                at = 3 * BCR
                mm(fbank[:, :], w("dt_WT", l)[at:at + DTR, half * P:(half + 1) * P], proj[at:at + DTR, :],
                   start=True, stop=True).then_inc(dt_done, 1)

            def mo_proj(m, l, nxt):
                pe.wait_ge(yz_ready, m + 1)
                pe.wait_ge(dt_read, m * 4 + (8 if nxt else 4))
                for half in range(2):
                    last = mm(fbank[:, :], w("mo_WT", l * 2 + half), yz[:, half, :], start=(half == 0), stop=(half == 1))
                last.then_inc(mo_done, 1)

            def rows_b(m, b, n):
                pe.wait_ge(b_copied, m * NS + n)
                mm(bbank[:, :], pick[:, n:n + 1].to_broadcast([3 * BCR, P]), bc[:, b, :], start=True, stop=True).then_inc(b_done, 1)

            def rows_c(m, b, n):
                if n >= 2:
                    pe.wait_ge(hc_done, m * STEPS + (2 * n - 2))
                mm(cbank[n % 2][:, :], pick[:, NS + n:NS + n + 1].to_broadcast([3 * BCR, P]), bc[:, b, :],
                   start=True, stop=True).then_inc(c_done, 1)

            def add_state(m, n):
                for half in range(2):
                    s = 2 * n + half
                    pe.wait_ge(hc_done, m * STEPS + (s + 1))
                    mm(ybank[half][:, :], g.identf[:, :], hc[:, s % RC, :], start=(n == 0), stop=(n == NS - 1)).then_inc(y_acc, 1)

            def first(f, l, c, b):
                pe.wait_ge(consts, 5)
                pe.wait_ge(inw_ready, 2)
                mean_sq(f, l)
                spread_rows(f)
                for e in range(4):
                    in_proj(f, l, e)
                x_proj(f, l, b)
                for half in range(2):
                    dt_proj(f, l, half)

            def body(m, l, c, b, nxt):
                pe.wait_ge(bc_ready, m + 1)
                rows_b(m, b, 0)
                rows_c(m, b, 0)
                for n in range(NS):
                    if n + 1 < NS:
                        rows_b(m, b, n + 1)
                        rows_c(m, b, n + 1)
                    if n == 0 and not (isinstance(m, int) and m == 0):
                        pe.wait_ge(y_read, m * 2)
                    if n:
                        add_state(m, n - 1)
                    if nxt:
                        f, fl, fc, fb = nxt
                        if n == 1:
                            pe.wait_ge(h_added, m)
                            mean_sq(f, fl)
                        if n == 4:
                            spread_rows(f)
                        if 5 <= n < 9:
                            in_proj(f, fl, n - 5)
                        if n == 11:
                            x_proj(f, fl, fb)
                        if n == 12:
                            dt_proj(f, fl, 0)
                        if n == 13:
                            dt_proj(f, fl, 1)
                add_state(m, NS - 1)
                mo_proj(m, l, nxt)

            turns(pe, first, body)

        @block.vector
        def _(dve):
            v = nc.vector

            def normed(f, l, c):
                dve.wait_ge(rB_done, f + 1)
                if l:
                    dve.wait_ge(h_added, c + 1)
                v.tensor_tensor(hn[:, :], slab((x1T, hT)[l], c), fbank[:, :], ALU.mult).then_inc(hn_ready, 1)

            def conv_step(f, l, k, half):
                i = 2 * k + half
                if i == 0:
                    dve.wait_ge(xz_copied, f * 4 + 2)
                    dve.wait_ge(xc_ready, f * 2)
                tap = w("conv_w", l)[:, half * TAPS + k:half * TAPS + k + 1]
                src = xpad[:, half, k:k + CH]
                if k == 0:
                    ins = v.tensor_scalar(conv[:, half, :], src, tap, None, ALU.mult)
                else:
                    dve.wait_ge(conv_seq, f * 6 + (i - 1))
                    ins = v.scalar_tensor_tensor(conv[:, half, :], src, tap, conv[:, half, :], ALU.mult, ALU.add)
                if k < TAPS - 1:
                    ins.then_inc(conv_seq, 1)
                elif half == 0:
                    ins.then_inc(conv_done0, 1)
                else:
                    ins.then_inc(conv_done, 1)

            def one_plus(f):
                dve.wait_ge(e_ready, f + 1)
                dve.wait_ge(delta_ready, f)
                v.tensor_scalar(w1[:, :, :], ea[:, :, :], 1.0, -1.0, ALU.add, ALU.add).then_inc(w1_ready, 1)

            def inputs(f, b):
                dve.wait_ge(delta_ready, f + 1)
                dve.wait_ge(xc_ready, f * 2 + 2)
                v.tensor_tensor(u[:, b, :, :], delta[:, b, :, :], xc[:, b, :, :], ALU.mult).then_inc(u_ready, 1)

            def finish_y(m, l, b):
                dve.wait_ge(y_acc, m * STEPS + STEPS)
                for half in range(2):
                    v.scalar_tensor_tensor(yz[:, half, :], xc[:, b, half, :], w("Dp", l)[:, half:half + 1], ybank[half][:, :],
                                           ALU.mult, ALU.add).then_inc(y_read, 1)
                dve.wait_ge(y_read, m * 2 + 2)
                dve.wait_ge(z_ready, m + 1)
                v.tensor_tensor(yz[:, :, :], yz[:, :, :], zs[:, b, :, :], ALU.mult).then_inc(yz_ready, 1)

            def add_h(m, l, c):
                if l == NL - 1:
                    v.tensor_tensor(slab(hT, c), slab(hT, c), slab(x2T, c), ALU.add).then_inc(h_seq, 1)
                    dve.wait_ge(h_seq, c + 1)
                dve.wait_ge(mo_done, m + 1)
                v.tensor_tensor(slab(hT, c), slab((x1T, hT)[l], c), fbank[:, :], ALU.add).then_inc(h_added, 1)

            def first(f, l, c, b):
                dve.wait_ge(g.later_in["wd"], 16)
                for i in range(NL):
                    v.tensor_scalar(w("in_WT", i), w("in_WT", i), w("rms_w")[:, i:i + 1], None, ALU.mult).then_inc(inw_ready, 1)
                dve.wait_ge(w_ready, 1)
                v.tensor_scalar(decay_neg[:, :], decay[:, :], -1.0, None, ALU.mult).then_inc(decay_ready, 1)
                normed(f, l, c)
                for k in range(TAPS):
                    for half in range(2):
                        conv_step(f, l, k, half)
                one_plus(f)
                inputs(f, b)

            def body(m, l, c, b, nxt):
                dve.wait_ge(carried, m * STEPS)
                def weighted(s):
                    n = s // 2
                    dve.wait_ge(scan_done, m * STEPS + (s + 1))
                    if s % 2 == 0:
                        dve.wait_ge(c_done, m * NS + (n + 1))
                    if s >= RC:
                        dve.wait_ge(y_acc, m * STEPS + (s - RC + 1))
                    v.tensor_tensor(hc[:, s % RC, :], hs[:, s % RH, :], cbank[n % 2][:, :], ALU.mult).then_inc(hc_done, 1)

                for n in range(NS):
                    for half in range(2):
                        s = 2 * n + half
                        dve.wait_ge(da_done, m * STEPS + (s + 1))
                        dve.wait_ge(dbx_done, m * STEPS + (s + 1))
                        if s >= RH:
                            dve.wait_ge(carried, m * STEPS + (s - RH + 1))
                        v.tensor_tensor_scan(hs[:, s % RH, :], abank[s % 2][:, :], dbx[:, s % RX, :], carry[:, s:s + 1],
                                             ALU.mult, ALU.add).then_inc(scan_done, 1)
                        if s:
                            weighted(s - 1)
                        if nxt:
                            f, fl, fc, fb = nxt
                            if s == 9:
                                normed(f, fl, fc)
                            if 13 <= s < 13 + TAPS:
                                conv_step(f, fl, s - 13, 0)
                                conv_step(f, fl, s - 13, 1)
                            if s == 29:
                                one_plus(f)
                weighted(STEPS - 1)
                finish_y(m, l, b)
                if nxt:
                    inputs(nxt[0], nxt[3])
                add_h(m, l, c)

            turns(dve, first, body)


def mamba_out(nc, g):
    ctx = ExitStack()
    with ctx:
        def sem(name):
            return ctx.enter_context(nc.semaphore("mo_" + name))

        w = piece(g.later["wd"], PACKS["wd"][0])
        yT = ctx.enter_context(nc.sbuf_tensor("mo_yT", [P, 2, KD, CH], F32))
        pbank, tbank = ([[ctx.enter_context(nc.psum_tensor(f"mo_{n}{b}{k}", [P, CH], F32)) for k in range(KD)]
                         for b in range(2)] for n in ("p", "t"))
        po_done, y_ready, yT_done, added = sem("po_done"), sem("y_ready"), sem("yT_done"), sem("added")
        block = ctx.enter_context(nc.Block())

        def slab(ap, c):
            return ap[:, bass.ds(c * CH, CH)]

        def pairs(eng, body):
            for b in range(2):
                body(b, b, False)
            with eng.Fori(1, NCH // 2) as i:
                for b in range(2):
                    body(i * 2 + b, b, True)

        @block.tensor
        def _(pe):
            def project(c, b, again):
                for k in range(KD):
                    if again:
                        pe.wait_ge(y_ready, c * KD + (k + 1 - 2 * KD))
                    for j, src in enumerate((g.x1T, g.hT)):
                        last = nc.tensor.matmul(pbank[b][k][:, :], w("po_WT", j)[:, k * P:(k + 1) * P], slab(src, c),
                                                start=(j == 0), stop=(j == KD - 1))
                    last.then_inc(po_done, 1)

            def back(c, b, again):
                pe.wait_ge(y_ready, c * KD + KD)
                for p in range(2):
                    if again:
                        pe.wait_ge(added, c * 2 + (p + 1 - 4))
                    for t in range(2):
                        for k in range(KD):
                            at = (2 * p + t) * P
                            last = nc.tensor.transpose(tbank[b][p][:, (t * KD + k) * P:(t * KD + k + 1) * P],
                                                       yT[:, b, k, at:at + P], g.identf[:, :])
                    last.then_inc(yT_done, 1)

            def turn(c, b, again):
                project(c, b, again)
                back(c, b, again)

            pairs(pe, turn)

        @block.vector
        def _(dve):
            v = nc.vector

            def turn(c, b, again):
                for k in range(KD):
                    dve.wait_ge(po_done, c * KD + (k + 1))
                    if again:
                        dve.wait_ge(yT_done, c * 2 - 2)
                    v.tensor_tensor(yT[:, b, k, :], pbank[b][k][:, :], slab((g.x1T, g.x2T)[k], c), ALU.add).then_inc(y_ready, 1)
                for p in range(2):
                    dve.wait_ge(yT_done, c * 2 + (p + 1))
                    dst = g.x[:, bass.ds(c * TPC + 2 * p, 2), :]
                    v.tensor_tensor(dst, dst, tbank[b][p][:, :].rearrange("p (t d) -> p t d", t=2), ALU.add).then_inc(added, 1)

            pairs(dve, turn)


def kernel(**inputs):
    import concourse.bacc as bacc
    from concourse.bass_utils import run_bass_kernel_spmd
    nc = bacc.Bacc("TRN2", target_bir_lowering=False, num_devices=1)
    arrays = lay_out(inputs)
    dram = {name: nc.dram_tensor("in_" + name, a.shape, mybir.dt.from_np(a.dtype), kind="ExternalInput").ap()
            for name, a in arrays.items()}
    out = nc.dram_tensor("out_x", (P, NT, D), F32, kind="ExternalOutput").ap()
    build(nc, dram, out)
    nc.compile()
    res = run_bass_kernel_spmd(nc, [{"in_" + name: a for name, a in arrays.items()}], core_ids=[0])
    return np.asarray(res.results[0]["out_x"]).transpose(1, 0, 2).reshape(1, S, D)
```

```python
from contextlib import ExitStack

import numpy as np

import concourse.bass as bass
from concourse import mybir

F32 = mybir.dt.float32
BF16 = mybir.dt.bfloat16
I32 = mybir.dt.int32
ACT = mybir.ActivationFunctionType
ALU = mybir.AluOpType
AX = mybir.AxisListType.X

P = 128
S, D = 4096, 256
NT = S // P
TPC = 4
CH = TPC * P
NCH = S // CH
KD = D // P
H, KVH, HD = 16, 4, 16
GQ = H // KVH
NQK = H + KVH
QKW, QKVW = NQK * HD, (NQK + KVH) * HD
LAT, WIN = 64, 64
TERMS = 8
VW = 32
NL, NS, DTR, TAPS = 2, 16, 8, 4
HALVES = 2
DI = HALVES * P
XPW = 3 * 2 * NS + DTR
LN_EPS, RMS_EPS, MAMBA_EPS = 1e-5, 1e-6, 1e-5
NEG = -30000.0
SCORE_SCALE = 1.0 / 4.0


class Tiles:
    pass


class Chain:

    def __init__(self, eng, sem):
        self.eng, self.sem, self.count = eng, sem, 0

    def do(self, ins):
        ins.then_inc(self.sem, 1)
        self.count += 1

    def sync(self):
        self.eng.wait_ge(self.sem, self.count)

    def link(self, ins):
        self.do(ins)
        self.sync()

    def restart(self):
        self.eng.sem_clear(self.sem)
        self.count = 0


def rsqrt(nc, chain, y, x, half, tmp):
    v = nc.vector
    chain.do(v.tensor_scalar(half, x, -0.5, None, ALU.mult))
    chain.link(v.tensor_single_scalar(tmp.bitcast(I32), x.bitcast(I32), 1, ALU.logical_shift_right))
    chain.link(v.tensor_scalar(y.bitcast(I32), tmp.bitcast(I32), -1.0, float(0x5F3759DF), ALU.mult, ALU.add))
    for _ in range(4):
        chain.link(v.tensor_tensor(tmp, y, y, ALU.mult))
        chain.link(v.tensor_tensor(tmp, tmp, half, ALU.mult))
        chain.link(v.scalar_tensor_tensor(y, tmp, 1.5, y, ALU.add, ALU.mult))


def pair_swap(ap):
    return ap.rearrange("p h (e t) -> p h e t", t=2)[:, :, :, ::-1]


def heads(ap, n):
    return ap.rearrange("p (h e) -> p h e", h=n)


def spread(ap, n):
    return ap.unsqueeze(2).to_broadcast([P, n, HD])


def rope_norm_split(nc, chain, b, cos, sin):
    v = nc.vector
    qk = heads(b.qkv[:, 0:QKW], NQK)
    cosb = cos.unsqueeze(1).to_broadcast([P, NQK, HD])
    sinb = sin.rearrange("p (e t) -> p e t", t=2).unsqueeze(1).to_broadcast([P, NQK, HD // 2, 2])
    t1, t2 = heads(b.t1[:, :], NQK), heads(b.t2[:, :], NQK)
    chain.do(v.tensor_tensor(t1, qk, cosb, ALU.mult))
    chain.link(v.tensor_tensor(t2.rearrange("p h (e t) -> p h e t", t=2), pair_swap(qk), sinb, ALU.mult))
    chain.link(v.tensor_tensor(b.t1[:, :], b.t1[:, :], b.t2[:, :], ALU.add))
    chain.link(v.tensor_tensor(b.t2[:, :], b.t1[:, :], b.t1[:, :], ALU.mult))
    chain.link(v.tensor_reduce(b.ss[:, :], t2, AX, ALU.add))
    chain.link(v.tensor_scalar(b.ss[:, :], b.ss[:, :], 1.0 / HD, RMS_EPS, ALU.mult, ALU.add))
    rsqrt(nc, chain, b.rs[:, :], b.ss[:, :], b.n1[:, :], b.n2[:, :])
    chain.link(v.tensor_tensor(t1, t1, spread(b.rs[:, :], NQK), ALU.mult))
    q, k = t1[:, 0:H, :], t1[:, H:NQK, :]
    qs = b.qs[:, :].rearrange("p (h r e) -> p h r e", h=H, r=TERMS)
    ks = b.ks[:, :].rearrange("p (h r e) -> p h r e", h=KVH, r=TERMS)
    qterms, kterms = ((0, 3), (3, 6), (6, 8)), ((0, 8), (1, 8), (2, 6))
    for part in range(3):
        q0, q1 = qterms[part]
        k0, k1 = kterms[part]
        nk = len(range(k0, k1, 3))
        chain.do(v.tensor_copy(qs[:, :, q0:q1, :], q.unsqueeze(2).to_broadcast([P, H, q1 - q0, HD])))
        last = v.tensor_copy(ks[:, :, k0:k1:3, :], k.unsqueeze(2).to_broadcast([P, KVH, nk, HD]))
        if part == 2:
            return last
        chain.link(last)
        chain.do(v.tensor_tensor(q, q, qs[:, :, q0, :], ALU.subtract))
        chain.link(v.tensor_tensor(k, k, ks[:, :, k0, :], ALU.subtract))


def global_attention(nc, g, dram):
    ctx = ExitStack()
    with ctx:
        def sb(name, shape, dt=F32):
            return ctx.enter_context(nc.sbuf_tensor(name, shape, dt))

        def pb(name, shape):
            return ctx.enter_context(nc.psum_tensor(name, shape, F32))

        def sem(name):
            return ctx.enter_context(nc.semaphore(name))

        x = g.x
        w = g.wa_col
        kT = sb("ga_kT", [P, NCH * KVH * CH], BF16)
        qT = sb("ga_qT", [P, 2, H, CH], BF16)
        vals = sb("ga_vals", [P, NCH, KVH, TPC, HD])
        probs = sb("ga_probs", [P, 2, 2, 2 * CH])
        wqkv = sb("ga_wqkv", [P, KD, QKVW])
        xnT = sb("ga_xnT", [P, KD, P])
        b = Tiles()
        b.qkv, b.t1, b.t2 = (sb("ga_" + n, [P, QKW]) for n in ("qkv", "t1", "t2"))
        b.ss, b.rs, b.n1, b.n2 = (sb("ga_" + n, [P, NQK]) for n in ("ss", "rs", "n1", "n2"))
        b.qs, b.ks = sb("ga_qs", [P, H * P], BF16), sb("ga_ks", [P, KVH * P], BF16)
        bn = sb("ga_bn", [P, NT, 6])
        mv = sb("ga_mv", [P, NT, 2])
        var = sb("ga_var", [P, NT])
        rln = sb("ga_rln", [P, NT])
        rms = sb("ga_rms", [P, NT])
        st1 = sb("ga_st1", [P, NT])
        st2 = sb("ga_st2", [P, NT])
        v_diag = sb("ga_v_diag", [P, 3, VW])
        v_ab = sb("ga_v_ab", [P, 2, VW])
        v_cd = sb("ga_v_cd", [P, 2, VW])
        oT = sb("ga_oT", [P, CH])
        den = sb("ga_den", [P, H])
        attn = sb("ga_attn", [P, 2, TPC, D])
        attnT = sb("ga_attnT", [P, KD, P])

        score = [pb(f"ga_score{i}", [P, 2 * CH]) for i in range(2)]
        out_acc = pb("ga_out_acc", [P, CH])
        bank_a = pb("ga_bank_a", [P, 512])
        bank_b = pb("ga_bank_b", [P, 512])
        bank_c = pb("ga_bank_c", [P, 512])

        x_in = [sem(f"ga_x_in{c}") for c in range(NCH)]
        w_in = sem("ga_w_in")
        v_const = sem("ga_v_const")
        w_prod, w_ready = sem("ga_w_prod"), sem("ga_w_ready")
        dve_seq = sem("ga_dve_seq")
        xn_ready, xT_done, xT_copied = sem("ga_xn_ready"), sem("ga_xT_done"), sem("ga_xT_copied")
        qkv_done, qkv_copied = sem("ga_qkv_done"), sem("ga_qkv_copied")
        split_ready = sem("ga_split_ready")
        qa_done, qb_done, kk_done = sem("ga_qa_done"), sem("ga_qb_done"), sem("ga_kk_done")
        qa_copied, qb_copied, kk_copied = sem("ga_qa_copied"), sem("ga_qb_copied"), sem("ga_kk_copied")
        scores_done, exp_done, kb_done = sem("ga_scores_done"), sem("ga_exp_done"), sem("ga_kb_done")
        vd_staged, vab_staged, vcd_staged = sem("ga_vd_staged"), sem("ga_vab_staged"), sem("ga_vcd_staged")
        o_copied, oT_done, o_normed = sem("ga_o_copied"), sem("ga_oT_done"), sem("ga_o_normed")
        aT_done, aT_copied, proj_done, proj_added = (sem("ga_aT_done"), sem("ga_aT_copied"),
                                                     sem("ga_proj_done"), sem("ga_proj_added"))

        NG = NCH * KVH
        LEAD = 5
        first_kb = [0]
        for n in range(NG):
            first_kb.append(first_kb[-1] + TPC + TPC * (n // KVH))

        def kcols(c, kv, j):
            return ((c * KVH + kv) * TPC + j) * P

        block = ctx.enter_context(nc.Block())

        @block.sync
        def _(sp):
            sp.dma_start(g.wa[:, :], dram["wa"]).then_inc(w_in, 16)
            for c in range(NCH):
                sp.dma_start(x[:, c * TPC:(c + 1) * TPC, :], dram["x"][:, c * TPC:(c + 1) * TPC, :]).then_inc(x_in[c], 16)
            for name in ("wb", "wc", "wd"):
                sp.dma_start(g.later[name][:, :], dram[name]).then_inc(g.later_in[name], 16)

        @block.gpsimd
        def _(pool):
            def copy(out, in_):
                zero = g.zero[:, 0:1]
                for _ in in_.shape[2:]:
                    zero = zero.unsqueeze(2)
                return nc.gpsimd.tensor_tensor(out, in_, zero.to_broadcast(list(in_.shape)), ALU.add)

            make_constants(nc, pool, g)
            for t in (v_diag, v_ab, v_cd):
                nc.gpsimd.memset(t[:, :, :], 0.0).then_inc(v_const, 1)
            pool.wait_ge(v_const, 3)
            for t in (v_diag, v_ab, v_cd):
                nc.gpsimd.memset(t[:, :, HD:HD + 1], 1.0).then_inc(v_const, 1)
            pool.wait_ge(v_const, 6)
            for n in range(NG):
                c, kv = divmod(n, KVH)
                pool.wait_ge(qkv_copied, 2 * TPC * (c + 1))
                if n:
                    pool.wait_ge(kb_done, first_kb[n - 1] + 3)
                copy(v_diag[:, :, 0:HD], vals[:, c, kv, 1:TPC, :]).then_inc(vd_staged, 1)
                if n:
                    pool.wait_ge(kb_done, first_kb[n])
                copy(v_cd[:, 1, 0:HD], vals[:, c, kv, 0, :]).then_inc(vcd_staged, 1)
                if c:
                    with pool.Fori(0, c) as q:
                        row = vals[:, bass.ds(q, 1), kv, :, :]
                        pool.wait_ge(kb_done, q * TPC + (first_kb[n] + 2))
                        copy(v_ab[:, :, 0:HD], row[:, 0, 0:2, :]).then_inc(vab_staged, 1)
                        pool.wait_ge(kb_done, q * TPC + (first_kb[n] + TPC))
                        copy(v_cd[:, :, 0:HD], row[:, 0, 2:4, :]).then_inc(vcd_staged, 1)

        @block.scalar
        def _(act):
            for n in range(NG):
                c = n // KVH
                k0 = first_kb[n]
                for j in range(TPC):
                    for pr in range(2):
                        width = (j + 1) * P
                        act.wait_ge(scores_done, 2 * (k0 + j) + pr + 1)
                        if k0 + j >= 2:
                            act.wait_ge(kb_done, k0 + j - 1)
                        src = score[pr][:, :].rearrange("p (h q) -> p h q", h=2)[:, :, 0:width]
                        dst = probs[:, j % 2, pr, :].rearrange("p (h q) -> p h q", h=2)[:, :, 0:width]
                        nc.scalar.activation(dst, src, ACT.Exp, scale=SCORE_SCALE).then_inc(exp_done, 1)
                if c:
                    with act.Fori(0, c) as q:
                        for j in range(TPC):
                            for pr in range(2):
                                act.wait_ge(scores_done, q * (2 * TPC) + (2 * (k0 + TPC + j) + pr + 1))
                                if pr == 0:
                                    act.wait_ge(kb_done, q * TPC + (k0 + TPC + j - 1))
                                nc.scalar.activation(probs[:, j % 2, pr, :], score[pr][:, :], ACT.Exp,
                                                     scale=SCORE_SCALE).then_inc(exp_done, 1)

        @block.tensor
        def _(pe):
            mm, tr = nc.tensor.matmul, nc.tensor.transpose
            identf, identb = g.identf, g.identb

            pe.wait_ge(w_in, 16)
            for k in range(KD):
                last = mm(bank_a[:, k * P:(k + 1) * P], w("kv_downT")[0:LAT, k * P:(k + 1) * P],
                          w("kv_up")[0:LAT, :], start=True, stop=True)
            last.then_inc(w_prod, 1)

            def transpose_x(i):
                pe.wait_ge(xn_ready, i + 1)
                pe.wait_ge(g.ident_ready, 1)
                for k in range(KD):
                    last = tr(bank_b[:, k * P:(k + 1) * P], x[:, i, k * P:(k + 1) * P], identf[:, :])
                last.then_inc(xT_done, 1)

            def project_qkv(i):
                pe.wait_ge(xT_copied, i + 1)
                pe.wait_ge(w_ready, 4)
                for k in range(KD):
                    last = mm(bank_a[:, 0:QKVW], xnT[:, k, :], wqkv[:, k, :], start=(k == 0), stop=(k == KD - 1))
                last.then_inc(qkv_done, 1)

            def transpose_heads(i, bank, src, h0, nh, done):
                for h in range(nh):
                    last = tr(bank[:, :].bitcast(BF16)[:, h * P:(h + 1) * P], src[:, (h0 + h) * P:(h0 + h + 1) * P],
                              identb[:, :])
                last.then_inc(done, 1)

            def transpose_qa(i):
                pe.wait_ge(split_ready, i + 1)
                transpose_heads(i, bank_a, b.qs, 0, 8, qa_done)

            def transpose_qb(i):
                if i >= LEAD + KVH:
                    pe.wait_ge(proj_added, i - (LEAD - 1) - KVH)
                transpose_heads(i, bank_b, b.qs, 8, 8, qb_done)

            def transpose_k(i):
                pe.wait_ge(qa_copied, i + 1)
                transpose_heads(i, bank_a, b.ks, 0, KVH, kk_done)

            def scores(n, pr, kcol, wait_unit, j=None):
                if wait_unit is not None:
                    pe.wait_ge(exp_done, wait_unit)
                c, kv = divmod(n, KVH)
                q0 = 0 if j is None else j * P
                for a in range(2):
                    dst = score[pr][:, a * CH:a * CH + CH - q0]
                    last = mm(dst, kcol, qT[:, c % 2, kv * GQ + 2 * pr + a, q0:CH], start=True, stop=j is None)
                    if j is not None:
                        last = mm(dst[:, 0:P], identb[:, :], g.causal[:, :], start=False, stop=True)
                last.then_inc(scores_done, 1)

            def diag_scores(n, s):
                k = first_kb[n] + s
                c, kv = divmod(n, KVH)
                if s == 0 and kv == 0:
                    pe.wait_ge(qb_copied, TPC * (c + 1))
                    pe.wait_ge(kk_copied, TPC * (c + 1))
                at = kcols(c, kv, TPC - 1 - s)
                for pr in range(2):
                    scores(n, pr, kT[:, at:at + P], 2 * k + pr - 1 if k else None, TPC - 1 - s)

            def weighted(rows, slot, q0, first=False, last=False):
                for h in range(GQ):
                    out = mm(out_acc[h * VW:(h + 1) * VW, q0:CH], rows,
                             probs[:, slot, h // 2, (h % 2) * CH:(h % 2) * CH + CH - q0],
                             start=first, stop=last, skip_group_check=True)
                out.then_inc(kb_done, 1)

            def transpose_out(n):
                pe.wait_ge(o_copied, n + 1)
                if n >= KVH:
                    pe.wait_ge(aT_copied, n - KVH + 1)
                for t in range(TPC):
                    last = tr(bank_c[:, t * P:(t + 1) * P], oT[:, t * P:(t + 1) * P], identf[:, :])
                last.then_inc(oT_done, 1)

            def transpose_attn(i):
                pe.wait_ge(o_normed, min(i + KVH, NG))
                if i > NT - TPC:
                    pe.wait_ge(aT_copied, i)
                for k in range(KD):
                    last = tr(bank_c[:, k * P:(k + 1) * P], attn[:, (i // TPC) % 2, i % TPC, k * P:(k + 1) * P],
                              identf[:, :])
                last.then_inc(aT_done, 1)

            def project_out(i):
                pe.wait_ge(aT_copied, i + 1)
                pe.wait_ge(qb_copied, min(i + KVH + LEAD, NT))
                if i:
                    pe.wait_ge(proj_added, i)
                for k in range(KD):
                    last = mm(bank_b[:, 0:D], attnT[:, k, :], w("wo", k), start=(k == 0), stop=(k == KD - 1))
                last.then_inc(proj_done, 1)

            for i in range(LEAD):
                if i:
                    pe.wait_ge(kk_copied, i - 1)
                    pe.wait_ge(qb_copied, i - 1)
                pe.wait_ge(w_ready, 4)
                transpose_x(i)
                project_qkv(i)
                if i:
                    pe.wait_ge(qkv_copied, 2 * (i + 1))
                    transpose_qa(i - 1)
                    transpose_qb(i - 1)
                    transpose_k(i - 1)
            diag_scores(0, 0)
            quads = 0
            for n in range(NG):
                c = n // KVH
                late, ahead = n + LEAD - 1, n + LEAD
                if late < NT:
                    transpose_qa(late)
                diag_scores(n, 1)
                if n:
                    transpose_out(n - 1)
                pe.wait_ge(vd_staged, n + 1)
                weighted(v_diag[:, 2, :], 0, 3 * P, first=True)
                if late < NT:
                    transpose_qb(late)
                diag_scores(n, 2)
                weighted(v_diag[:, 1, :], 1, 2 * P)
                if late < NT:
                    transpose_k(late)
                if ahead < NT:
                    pe.wait_ge(qb_copied, ahead)
                    transpose_x(ahead)
                diag_scores(n, 3)
                weighted(v_diag[:, 0, :], 0, P)
                if ahead < NT:
                    pe.wait_ge(kk_copied, ahead)
                    project_qkv(ahead)
                if c:
                    transpose_attn(n - KVH)
                    with pe.Fori(0, c) as q:
                        for j in range(TPC):
                            k = first_kb[n] + TPC + j
                            for pr in range(2):
                                scores(n, pr, kT[:, bass.ds(q * (KVH * CH) + kcols(0, n % KVH, j), P)],
                                       q * (2 * TPC) + (2 * k + pr - 1))
                            if j == 0:
                                pe.wait_ge(vcd_staged, q + (n + quads + 1))
                            if j == 1:
                                pe.wait_ge(vab_staged, q + (quads + 1))
                            if j == 3:
                                pe.wait_ge(vcd_staged, q + (n + quads + 2))
                            rows = (v_cd[:, 1, :], v_ab[:, 0, :], v_ab[:, 1, :], v_cd[:, 0, :])[j]
                            weighted(rows, (j + 1) % 2, 0)
                    quads += c
                    project_out(n - KVH)
                if n + 1 < NG:
                    diag_scores(n + 1, 0)
                else:
                    pe.wait_ge(exp_done, 2 * first_kb[NG])
                pe.wait_ge(vcd_staged, n + quads + 1)
                weighted(v_cd[:, 1, :], 1, 0, last=True)
            transpose_out(NG - 1)
            for i in range(NT - TPC, NT):
                transpose_attn(i)
                project_out(i)

        @block.vector
        def _(dve):
            chain = Chain(dve, dve_seq)
            v = nc.vector

            def stats(c0, c1):
                ts = slice(c0 * TPC, c1 * TPC)
                for c in range(c0, c1):
                    dve.wait_ge(x_in[c], 16)
                    for i in range(c * TPC, (c + 1) * TPC):
                        chain.do(v.bn_stats(bn[:, i, :], x[:, i, :]))
                chain.sync()
                for i in range(c0 * TPC, c1 * TPC):
                    chain.do(v.bn_aggr(mv[:, i, :], bn[:, i, :]))
                chain.sync()
                chain.link(v.tensor_scalar(var[:, ts], mv[:, ts, 1], LN_EPS, None, ALU.add))
                rsqrt(nc, chain, rln[:, ts], var[:, ts], st1[:, ts], st2[:, ts])
                chain.link(v.tensor_tensor(var[:, ts], rln[:, ts], rln[:, ts], ALU.mult))
                chain.link(v.tensor_tensor(var[:, ts], var[:, ts], mv[:, ts, 1], ALU.mult))
                chain.link(v.tensor_scalar(var[:, ts], var[:, ts], RMS_EPS, None, ALU.add))
                rsqrt(nc, chain, rms[:, ts], var[:, ts], st1[:, ts], st2[:, ts])

            def normalise(i):
                v.tensor_scalar(x[:, i, :], x[:, i, :], mv[:, i, 0:1], rln[:, i:i + 1],
                                ALU.subtract, ALU.mult).then_inc(xn_ready, 1)

            def copy_xT(i):
                dve.wait_ge(xT_done, i + 1)
                if i:
                    dve.wait_ge(qkv_done, i)
                v.tensor_copy(xnT[:, :, :], bank_b[:, 0:D].rearrange("p (k t) -> p k t", k=KD)).then_inc(xT_copied, 1)

            def copy_qkv(i):
                dve.wait_ge(qkv_done, i + 1)
                v.tensor_scalar(b.qkv[:, :], bank_a[:, 0:QKW], rms[:, i:i + 1], None, ALU.mult).then_inc(qkv_copied, 1)
                v.tensor_scalar(vals[:, i // TPC, :, i % TPC, :], heads(bank_a[:, QKW:QKVW], KVH), rms[:, i:i + 1],
                                None, ALU.mult).then_inc(qkv_copied, 1)

            def split(i):
                dve.wait_ge(qkv_copied, 2 * (i + 1))
                rope_norm_split(nc, chain, b, w("cos", i), w("sin", i)).then_inc(split_ready, 1)

            def lay_q(i, bank, h0, done, copied):
                dve.wait_ge(done, i + 1)
                t0 = (i % TPC) * P
                v.tensor_copy(qT[:, (i // TPC) % 2, h0:h0 + 8, t0:t0 + P],
                              bank[:, :].bitcast(BF16)[:, 0:8 * P].rearrange("p (h t) -> p h t", h=8)).then_inc(copied, 1)

            def lay_k(i):
                dve.wait_ge(kk_done, i + 1)
                c, j = divmod(i, TPC)
                dst = kT[:, kcols(c, 0, 0):kcols(c + 1, 0, 0)].rearrange("p (h t) -> p h t", h=KVH)
                v.tensor_copy(dst[:, :, j * P:(j + 1) * P],
                              bank_a[:, :].bitcast(BF16)[:, 0:KVH * P].rearrange("p (h t) -> p h t", h=KVH)).then_inc(kk_copied, 1)

            def copy_out(n):
                dve.wait_ge(kb_done, first_kb[n + 1])
                if n:
                    dve.wait_ge(oT_done, n)
                v.tensor_copy(oT[:, :], out_acc[:, :]).then_inc(o_copied, 1)

            def normalise_out(n):
                c, kv = divmod(n, KVH)
                dve.wait_ge(oT_done, n + 1)
                if c >= 2:
                    dve.wait_ge(aT_done, TPC * (c - 1))
                o = bank_c[:, :].rearrange("p (m e) -> p m e", e=VW)
                chain.link(v.reciprocal(den[:, :], o[:, :, HD]))
                dst = attn[:, c % 2, :, kv * GQ * HD:(kv + 1) * GQ * HD]
                v.tensor_tensor(dst.rearrange("p t (h e) -> p t h e", h=GQ),
                                o[:, :, 0:HD].rearrange("p (t h) e -> p t h e", t=TPC),
                                den[:, :].rearrange("p (t h) -> p t h", t=TPC).unsqueeze(3).to_broadcast([P, TPC, GQ, HD]),
                                ALU.mult).then_inc(o_normed, 1)

            def copy_aT(i):
                dve.wait_ge(aT_done, i + 1)
                if i:
                    dve.wait_ge(proj_done, i)
                v.tensor_copy(attnT[:, :, :], bank_c[:, 0:D].rearrange("p (k t) -> p k t", k=KD)).then_inc(aT_copied, 1)

            def add_proj(i):
                dve.wait_ge(proj_done, i + 1)
                v.tensor_tensor(x[:, i, :], x[:, i, :], bank_b[:, 0:D], ALU.add).then_inc(proj_added, 1)

            dve.wait_ge(w_in, 16)
            dve.wait_ge(w_prod, 1)
            for k in range(KD):
                n1 = w("norm1")[:, k:k + 1]
                v.tensor_scalar(wqkv[:, k, 0:D], w("wq", k), n1, None, ALU.mult).then_inc(w_ready, 1)
                v.tensor_scalar(wqkv[:, k, D:QKVW], bank_a[:, k * P:(k + 1) * P], n1, None, ALU.mult).then_inc(w_ready, 1)
            stats(0, 2)
            for i in range(LEAD + 1):
                normalise(i)
            for i in range(LEAD):
                copy_xT(i)
                copy_qkv(i)
                if i:
                    lay_q(i - 1, bank_a, 0, qa_done, qa_copied)
                    lay_q(i - 1, bank_b, 8, qb_done, qb_copied)
                    lay_k(i - 1)
                split(i)
            for n in range(NG):
                late, ahead = n + LEAD - 1, n + LEAD
                if n:
                    copy_out(n - 1)
                if late < NT:
                    lay_q(late, bank_a, 0, qa_done, qa_copied)
                if n:
                    normalise_out(n - 1)
                if late < NT:
                    lay_q(late, bank_b, 8, qb_done, qb_copied)
                    lay_k(late)
                if ahead < NT:
                    copy_xT(ahead)
                    copy_qkv(ahead)
                if n >= KVH:
                    copy_aT(n - KVH)
                if n == 1:
                    stats(2, NCH)
                if ahead < NT:
                    split(ahead)
                if ahead + 1 < NT:
                    normalise(ahead + 1)
                if n >= KVH:
                    add_proj(n - KVH)
            copy_out(NG - 1)
            normalise_out(NG - 1)
            for i in range(NT - TPC, NT):
                copy_aT(i)
                add_proj(i)


def make_constants(nc, pool, g):
    gp = nc.gpsimd
    steps = [0]

    def link(ins):
        steps[0] += 1
        ins.then_inc(g.const_seq, 1)
        pool.wait_ge(g.const_seq, steps[0])

    link(gp.memset(g.zero[:, :], 0.0))
    link(gp.memset(g.identf[:, :], 0.0))
    link(gp.affine_select(out=g.identf[:, :], in_=g.identf[:, :], compare_op=ALU.not_equal, fill=1.0, base=0,
                          pattern=[[-1, P]], channel_multiplier=1))
    link(gp.tensor_copy(g.identb[:, :], g.identf[:, :]))
    link(gp.memset(g.causal[:, :], 0.0))
    gp.affine_select(out=g.causal[:, :], in_=g.causal[:, :], compare_op=ALU.is_ge, fill=NEG, base=0,
                     pattern=[[1, P]], channel_multiplier=-1).then_inc(g.ident_ready, 1)
    pool.wait_ge(g.ident_ready, 1)


def pack(columns):
    at, out = 0, {}
    for name, n in columns:
        out[name] = (at, n)
        at += n
    return out, at


PACKS = {
    "wa": pack([("kv_downT", D), ("kv_up", 2 * KVH * HD), ("wq", KD * D), ("norm1", KD), ("wo", KD * D),
                ("cos", NT * HD), ("sin", NT * HD)]),
    "wb": pack([("wqkv", KD * QKVW), ("norm2", KD), ("wo", KD * D), ("cos", NT * HD), ("sin", NT * HD)]),
    "wc": pack([("wq", KD * D), ("routersT", KD * D), ("valuesT", KD * D), ("woutT", KD * D)]),
    "wd": pack([("bias", D), ("ln_g", KD), ("ln_b", KD), ("po_b", D), ("in_WT", NL * 2 * DI), ("rms_w", NL),
                ("conv_w", NL * HALVES * TAPS), ("conv_b", NL * HALVES), ("dt_b", NL * HALVES), ("Dp", NL * HALVES),
                ("A_log", NL * HALVES * NS), ("xp_WT", NL * HALVES * XPW), ("dt_WT", NL * DI), ("mo_WT", NL * HALVES * P),
                ("po_WT", KD * D)]),
}
PIECE = {"wq": D, "wo": D, "wqkv": QKVW, "cos": HD, "sin": HD, "routersT": D, "valuesT": D, "woutT": D,
         "in_WT": 2 * DI, "conv_w": HALVES * TAPS, "conv_b": HALVES, "dt_b": HALVES, "Dp": HALVES, "xp_WT": XPW,
         "dt_WT": DI, "mo_WT": P, "po_WT": D}


def piece(tile, table):
    def w(name, k=None):
        at, n = table[name]
        if k is not None:
            n = PIECE[name]
            at += k * n
        return tile[:, at:at + n]
    return w


def build(nc, dram, out, upto=9):
    with ExitStack() as ctx:
        early = ctx.enter_context(ExitStack())

        def sb(stack, name, shape, dt=F32):
            return stack.enter_context(nc.sbuf_tensor(name, shape, dt))

        def sem(name):
            return ctx.enter_context(nc.semaphore(name))

        g = Tiles()
        g.x = sb(ctx, "x", [P, NT, D])
        g.identf, g.identb = sb(ctx, "identf", [P, P]), sb(ctx, "identb", [P, P], BF16)
        g.zero = sb(ctx, "zero", [P, 1])
        g.causal = sb(ctx, "causal", [P, P], BF16)
        g.w_gate, g.w_out = sb(ctx, "w_gate", [P, KD, D]), sb(ctx, "w_out", [P, KD, D])
        tiles = {name: sb(ctx if name == "wd" else early, name, [P, PACKS[name][1]]) for name in ("wd", "wa", "wb", "wc")}
        g.wa, g.later = tiles["wa"], tiles
        g.later_in = {name: sem(f"{name}_in") for name in ("wb", "wc", "wd")}
        g.wa_col = piece(g.wa, PACKS["wa"][0])
        g.xr_in, g.stored = sem("xr_in"), sem("stored")
        g.const_seq, g.ident_ready = sem("const_seq"), sem("ident_ready")
        g.dram, g.out = dram, out

        global_attention(nc, g, dram)
        local_attention(nc, g, dram)
        tree_ffn(nc, g, "fa", True, False)
        early.close()
        with ExitStack() as late:
            g.hT = sb(late, "hT", [P, S])
            mamba_norms(nc, g)
            mamba_layers(nc, g)
            mamba_out(nc, g)
        tree_ffn(nc, g, "fb", False, True)


def rope_tables(base):
    inv = (np.float32(1.0) / np.float32(base) ** (np.arange(0, HD, 2, dtype=np.float32) / np.float32(HD))).astype(np.float32)
    ang = np.arange(S, dtype=np.float32)[:, None] * inv[None, :]
    cos, sin = np.cos(ang).astype(np.float32), np.sin(ang).astype(np.float32)
    cos2 = np.repeat(cos, 2, axis=1)
    sin2 = np.stack([-sin, sin], axis=2).reshape(S, HD)
    return [np.ascontiguousarray(t.reshape(NT, P, HD).transpose(1, 0, 2).reshape(P, NT * HD)) for t in (cos2, sin2)]


def lay_out(inputs):
    a = {k: np.asarray(v) for k, v in inputs.items()}

    def rows(m):
        return m.reshape(-1, P, m.shape[1]).transpose(1, 0, 2).reshape(P, -1)

    def pad(m):
        return np.concatenate([m, np.zeros((P - m.shape[0], m.shape[1]), m.dtype)], axis=0)

    def cols(v):
        return v.reshape(-1, P).T

    def everywhere(v):
        return np.broadcast_to(v[None, :], (P, v.shape[0]))

    ga, la, ff, mb = "L0_attn_a_g_", "L0_attn_a_l_", "L0_ffn_", "L0_attn_b_"
    halves = rows

    def layers(f):
        return np.concatenate([f(l) for l in range(NL)], axis=1)

    def xp_rows(l):
        m = a[mb + "xp_W"][l].T
        bc = m[:, DTR:]
        return rows(np.concatenate([bc, bc, bc, m[:, 0:DTR]], axis=1))

    def dt_rows(l):
        m = np.zeros((P, DI), np.float32)
        m[XPW - DTR:XPW] = a[mb + "dt_W"][l].T
        return m

    cg, sg = rope_tables(1000000.0)
    cl, sl = rope_tables(10000.0)
    parts = {
        "wa": dict(kv_downT=pad(a[ga + "kv_down"].T), kv_up=pad(np.concatenate([a[ga + "k_up"], a[ga + "v_up"]], axis=1)),
                   wq=rows(a[ga + "wq"]), norm1=cols(a["L0_attn_a_norm1_w"]), wo=rows(a[ga + "wo"]), cos=cg, sin=sg),
        "wb": dict(wqkv=rows(np.concatenate([a[la + "wq"], a[la + "wk"], a[la + "wv"]], axis=1)),
                   norm2=cols(a["L0_attn_a_norm2_w"]), wo=rows(a[la + "wo"]), cos=cl, sin=sl),
        "wc": dict(wq=rows(a[ff + "Wq"]),
                   routersT=rows(np.concatenate([a[ff + "routers"].T, np.zeros((D, 1), np.float32)], axis=1)),
                   valuesT=rows(a[ff + "leaf_values"].T), woutT=rows(a[ff + "Wout_w"].T)),
        "wd": dict(bias=everywhere(a[ff + "Wout_b"]), ln_g=cols(a[mb + "ln_g"]), ln_b=cols(a[mb + "ln_b"]),
                   po_b=everywhere(a[mb + "po_b"]), in_WT=layers(lambda l: a[mb + "in_W"][l].T),
                   rms_w=a[mb + "rms_w"].T, conv_w=layers(lambda l: halves(a[mb + "conv_w"][l, :, 0, :])),
                   conv_b=layers(lambda l: cols(a[mb + "conv_b"][l])), dt_b=layers(lambda l: cols(a[mb + "dt_b"][l])),
                   Dp=layers(lambda l: cols(a[mb + "Dp"][l])), A_log=layers(lambda l: halves(a[mb + "A_log"][l])),
                   xp_WT=layers(xp_rows), dt_WT=layers(dt_rows), mo_WT=layers(lambda l: rows(a[mb + "mo_W"][l].T)),
                   po_WT=rows(a[mb + "po_W"].T)),
    }
    arrays = {"x": np.ascontiguousarray(a["L0_attn_a_hidden"].reshape(NT, P, D).transpose(1, 0, 2))}
    for name, (table, width) in PACKS.items():
        whole = np.concatenate([parts[name][n] for n in table], axis=1)
        assert whole.shape == (P, width), (name, whole.shape, width)
        arrays[name] = np.ascontiguousarray(whole)
    return arrays


def local_attention(nc, g, dram):
    ctx = ExitStack()
    with ctx:
        def sb(name, shape, dt=F32):
            return ctx.enter_context(nc.sbuf_tensor("la_" + name, shape, dt))

        def sem(name):
            return ctx.enter_context(nc.semaphore("la_" + name))

        x, w = g.x, piece(g.later["wb"], PACKS["wb"][0])
        HALF = H // 2
        PW = WIN
        UNIT = 2 * CH + 2 * TPC * PW
        LAYS = 2 * TPC + 2
        wqkv = sb("wqkv", [P, KD, QKVW])
        xs = sb("xs", [P, TPC, D])
        xT = sb("xT", [P, TPC, KD, P])
        xr = sb("xr", [P, TPC, D])
        qk = sb("qk", [P, TPC * QKW])
        t1, t2 = sb("t1", [P, TPC * QKW]), sb("t2", [P, TPC * QKW])
        ss, rs, n1, n2 = (sb(n, [P, TPC * NQK]) for n in ("ss", "rs", "n1", "n2"))
        qn, kn = sb("qn", [P, TPC * H, HD]), sb("kn", [P, TPC * KVH, HD])
        qs, ks = sb("qs", [P, TPC * H, TERMS, HD], BF16), sb("ks", [P, TPC * KVH, TERMS, HD], BF16)
        qT = sb("qT", [P, H, CH], BF16)
        kT = sb("kT", [P, KVH, P + CH], BF16)
        vnew = sb("vnew", [P, TPC, KVH, HD])
        vals = sb("vals", [P, TPC + 1, KVH, VW])
        probs = sb("probs", [P, 2, 2, UNIT])
        oT = sb("oT", [P, CH])
        den = sb("den", [P, H])
        attn = sb("attn", [P, TPC, D])
        attnT = sb("attnT", [P, TPC, KD, P])
        bn, mv = sb("bn", [P, TPC, 6]), sb("mv", [P, TPC, 2])
        var, rms, s1, s2 = (sb(n, [P, TPC]) for n in ("var", "rms", "s1", "s2"))
        band = sb("band", [P, P], BF16)
        before = sb("before", [P, PW], BF16)

        score = [ctx.enter_context(nc.psum_tensor(f"la_score{i}", [P, UNIT], F32)) for i in range(2)]
        out_acc = ctx.enter_context(nc.psum_tensor("la_out_acc", [P, CH], F32))
        bank_p = ctx.enter_context(nc.psum_tensor("la_bank_p", [P, 512], F32))
        sbank = [score[i // 3][:, (i % 3) * 512:(i % 3 + 1) * 512] for i in range(6)]

        dve_seq, pool_seq, masks_ready, w_ready = sem("dve_seq"), sem("pool_seq"), sem("masks_ready"), sem("w_ready")
        xr_in, xr_added, xs_ready = g.xr_in, sem("xr_added"), sem("xs_ready")
        xT_done, xT_copied = sem("xT_done"), sem("xT_copied")
        qkv_done, qkv_copied, split_ready = sem("qkv_done"), sem("qkv_copied"), sem("split_ready")
        lay_done, lay_dve, lay_act = sem("lay_done"), sem("lay_dve"), sem("lay_act")
        k_moved, vals_ready = sem("k_moved"), sem("vals_ready")
        scores_done, exp_done, pv_done = sem("scores_done"), sem("exp_done"), sem("pv_done")
        o_copied, oT_done, o_normed = sem("o_copied"), sem("oT_done"), sem("o_normed")
        aT_done, aT_copied, proj_done, added = sem("aT_done"), sem("aT_copied"), sem("proj_done"), sem("added")

        def chunk(c):
            return x[:, bass.ds(c * TPC, TPC), :]

        def turns(eng, body):
            body(0, True, True)
            with eng.Fori(1, NCH - 2) as c:
                body(c, True, True)
            body(NCH - 2, True, False)
            body(NCH - 1, False, False)

        def qkv_bank(t):
            return (sbank[2], sbank[3], out_acc[:, :], bank_p[:, :])[t]

        def lay_views(n):
            bank = sbank[n % 6].bitcast(BF16)
            if n < 2 * TPC:
                t, half = divmod(n, 2)
                return (qT[:, half * HALF:(half + 1) * HALF, t * P:(t + 1) * P],
                        bank.rearrange("p (h t) -> p h t", h=HALF))
            t = 2 * (n - 2 * TPC)
            dst = kT[:, :, P + t * P:P + (t + 2) * P].rearrange("p h (t n) -> p t h n", t=2)
            return dst, bank.rearrange("p (t h n) -> p t h n", t=2, h=KVH)

        block = ctx.enter_context(nc.Block())

        @block.sync
        def _(sp):
            sp.dma_start(xr[:, :, :], dram["x"][:, 0:TPC, :]).then_inc(xr_in, 16)
            with sp.Fori(1, NCH) as c:
                sp.wait_ge(xr_added, c)
                sp.dma_start(xr[:, :, :], dram["x"][:, bass.ds(c * TPC, TPC), :]).then_inc(xr_in, 16)

        @block.gpsimd
        def _(pool):
            def copy(out, in_):
                zero = g.zero[:, 0:1]
                for _ in in_.shape[2:]:
                    zero = zero.unsqueeze(2)
                return nc.gpsimd.tensor_tensor(out, in_, zero.to_broadcast(list(in_.shape)), ALU.add)

            gp = nc.gpsimd
            chain = Chain(pool, pool_seq)
            for t in (band, before):
                chain.do(gp.memset(t[:, :], 0.0))
            chain.do(gp.memset(kT[:, :, 0:P], 0.0))
            chain.do(gp.memset(vals[:, :, :, :], 0.0))
            chain.sync()
            chain.link(gp.affine_select(out=band[:, :], in_=band[:, :], compare_op=ALU.is_ge, fill=NEG, base=0,
                                        pattern=[[1, P]], channel_multiplier=-1))
            gp.affine_select(out=band[:, :], in_=band[:, :], compare_op=ALU.is_gt, fill=NEG, base=WIN,
                             pattern=[[-1, P]], channel_multiplier=1).then_inc(masks_ready, 1)
            gp.affine_select(out=before[:, :], in_=before[:, :], compare_op=ALU.is_gt, fill=NEG, base=WIN - P,
                             pattern=[[-1, PW]], channel_multiplier=1).then_inc(masks_ready, 1)
            chain.link(gp.memset(vals[:, 1:TPC + 1, :, HD:HD + 1], 1.0))

            def new_values(c):
                pool.wait_ge(qkv_copied, c * (2 * TPC) + 2 * TPC)
                copy(vals[:, 1:TPC + 1, :, 0:HD], vnew[:, :, :, :]).then_inc(vals_ready, 1)

            def add_input(c):
                pool.wait_ge(xr_in, c * 16 + 16)
                pool.wait_ge(xs_ready, c + 1)
                gp.tensor_tensor(chunk(c), chunk(c), xr[:, :, :], ALU.add).then_inc(xr_added, 1)

            def turn(c, ahead, far):
                add_input(c)
                if ahead:
                    pool.wait_ge(scores_done, c * 8 + 8)
                    copy(kT[:, :, 0:P], kT[:, :, CH:P + CH]).then_inc(k_moved, 1)
                    pool.wait_ge(pv_done, c * KVH + KVH)
                    chain.link(copy(vals[:, 0, :, 0:HD + 1], vals[:, TPC, :, 0:HD + 1]))
                    new_values(c + 1)
                    chain.restart()

            new_values(0)
            chain.restart()
            turns(pool, turn)

        @block.scalar
        def _(act):
            def copy(out, in_, scale=1.0):
                return nc.scalar.activation(out, in_, ACT.Copy, scale=scale)

            def copy_xT(c):
                for p in range(2):
                    act.wait_ge(xT_done, c * 2 + (p + 1))
                    if p == 0:
                        act.wait_ge(qkv_done, c * TPC)
                    copy(xT[:, 2 * p:2 * p + 2, :, :].rearrange("p t k n -> p (t k n)"), sbank[p]).then_inc(xT_copied, 1)

            def copy_qkv(c):
                act.wait_ge(split_ready, c)
                act.wait_ge(vals_ready, c)
                for t in range(TPC):
                    act.wait_ge(qkv_done, c * TPC + (t + 1))
                    bank = qkv_bank(t)
                    copy(qk[:, t * QKW:(t + 1) * QKW], bank[:, 0:QKW]).then_inc(qkv_copied, 1)
                    copy(vnew[:, t, :, :], heads(bank[:, QKW:QKVW], KVH)).then_inc(qkv_copied, 1)

            def lay(c):
                for n in range(1, LAYS, 2):
                    act.wait_ge(lay_done, c * LAYS + (n + 1))
                    if n == LAYS - 1:
                        act.wait_ge(k_moved, c)
                    dst, src = lay_views(n)
                    copy(dst, src).then_inc(lay_act, 1)

            def turn(c, ahead, far):
                if ahead:
                    copy_xT(c + 1)
                    copy_qkv(c + 1)
                for kv in range(KVH):
                    for pr in range(2):
                        act.wait_ge(scores_done, c * 8 + (2 * kv + pr + 1))
                        nc.scalar.activation(probs[:, kv % 2, pr, :], score[pr][:, :], ACT.Exp,
                                             scale=SCORE_SCALE).then_inc(exp_done, 1)
                    if kv:
                        copy_out(c, kv - 1)
                copy_out(c, KVH - 1)
                if ahead:
                    lay(c + 1)
                for p in range(2):
                    act.wait_ge(aT_done, c * 2 + (p + 1))
                    if p == 0:
                        act.wait_ge(proj_done, c * 2)
                    copy(attnT[:, 2 * p:2 * p + 2, :, :].rearrange("p t k n -> p (t k n)"),
                         (out_acc, bank_p)[p][:, :]).then_inc(aT_copied, 1)

            def copy_out(c, kv):
                act.wait_ge(pv_done, c * KVH + (kv + 1))
                act.wait_ge(oT_done, c * KVH + kv)
                copy(oT[:, :], out_acc[:, :]).then_inc(o_copied, 1)

            copy_xT(0)
            copy_qkv(0)
            lay(0)
            turns(act, turn)

        @block.tensor
        def _(pe):
            mm, tr = nc.tensor.matmul, nc.tensor.transpose
            identf, identb = g.identf, g.identb

            def project(c):
                pe.wait_ge(xs_ready, c + 1)
                for p in range(2):
                    for t in range(2 * p, 2 * p + 2):
                        for k in range(KD):
                            at = ((t % 2) * KD + k) * P
                            last = tr(sbank[p][:, at:at + P], xs[:, t, k * P:(k + 1) * P], identf[:, :])
                    last.then_inc(xT_done, 1)
                for t in range(TPC):
                    if t % 2 == 0:
                        pe.wait_ge(xT_copied, c * 2 + (t // 2 + 1))
                    for k in range(KD):
                        last = mm(qkv_bank(t)[:, 0:QKVW], xT[:, t, k, :], wqkv[:, k, :], start=(k == 0), stop=(k == KD - 1))
                    last.then_inc(qkv_done, 1)

            def transpose_qk(c):
                pe.wait_ge(split_ready, c + 1)
                for n in range(LAYS):
                    if n >= 6:
                        pe.wait_ge((lay_dve, lay_act)[n % 2], c * (LAYS // 2) + (n - 6) // 2 + 1)
                    bank = sbank[n % 6].bitcast(BF16)
                    for m in range(HALF):
                        if n < 2 * TPC:
                            src = qs[:, (n // 2) * H + (n % 2) * HALF + m, :, :]
                        else:
                            src = ks[:, (n - 2 * TPC) * HALF + m, :, :]
                        last = tr(bank[:, m * P:(m + 1) * P], src.rearrange("p r e -> p (r e)"), identb[:, :])
                    last.then_inc(lay_done, 1)

            def scores(c, kv):
                for pr in range(2):
                    u = 2 * kv + pr
                    if kv:
                        pe.wait_ge(exp_done, c * 8 + (u - 1))
                    elif pr:
                        pe.wait_ge(added, c * 2)
                    s = score[pr]
                    for a in range(2):
                        mm(s[:, a * CH:(a + 1) * CH], identb[:, :], band[:, :].unsqueeze(1).to_broadcast([P, TPC, P]),
                           start=True, stop=False, skip_group_check=True)
                    mm(s[:, 2 * CH:UNIT], identb[:, :], before[:, :].unsqueeze(1).to_broadcast([P, 2 * TPC, PW]),
                       start=True, stop=False, skip_group_check=True)
                    for j in range(TPC):
                        for a in range(2):
                            h = kv * GQ + 2 * pr + a
                            mm(s[:, a * CH + j * P:a * CH + (j + 1) * P], kT[:, kv, (j + 1) * P:(j + 2) * P],
                               qT[:, h, j * P:(j + 1) * P], start=False, stop=True, skip_group_check=True)
                        for a in range(2):
                            h = kv * GQ + 2 * pr + a
                            at = 2 * CH + (a * TPC + j) * PW
                            last = mm(s[:, at:at + PW], kT[:, kv, j * P:(j + 1) * P],
                                      qT[:, h, j * P:j * P + PW], start=False, stop=True, skip_group_check=True)
                    last.then_inc(scores_done, 1)

            def weighted(c, kv):
                pe.wait_ge(exp_done, c * 8 + (2 * kv + 2))
                if kv:
                    pe.wait_ge(o_copied, c * KVH + kv)
                for j in range(TPC):
                    for own in (True, False):
                        for h in range(GQ):
                            a = h % 2
                            at, n = (a * CH + j * P, P) if own else (2 * CH + (a * TPC + j) * PW, PW)
                            last = mm(out_acc[h * VW:(h + 1) * VW, j * P:j * P + n], vals[:, j + own, kv, :],
                                      probs[:, kv % 2, h // 2, at:at + n], start=(j == 0 and own), stop=(j == TPC - 1 and not own),
                                      skip_group_check=True)
                last.then_inc(pv_done, 1)

            def transpose_out(c, kv):
                pe.wait_ge(o_copied, c * KVH + (kv + 1))
                if kv:
                    pe.wait_ge(o_normed, c * KVH + kv)
                for t in range(TPC):
                    last = tr(bank_p[:, t * P:(t + 1) * P], oT[:, t * P:(t + 1) * P], identf[:, :])
                last.then_inc(oT_done, 1)

            def project_out(c, ahead):
                pe.wait_ge(o_normed, c * KVH + KVH)
                for p in range(2):
                    for t in range(2 * p, 2 * p + 2):
                        for k in range(KD):
                            at = ((t % 2) * KD + k) * P
                            last = tr((out_acc, bank_p)[p][:, at:at + P], attn[:, t, k * P:(k + 1) * P], identf[:, :])
                    last.then_inc(aT_done, 1)
                for p in range(2):
                    pe.wait_ge(aT_copied, c * 2 + (p + 1))
                    if ahead:
                        pe.wait_ge((lay_dve, lay_act)[p], (c + 1) * (LAYS // 2) + 3)
                    for t in range(2 * p, 2 * p + 2):
                        for k in range(KD):
                            last = mm(sbank[4 + p][:, (t % 2) * D:(t % 2 + 1) * D], attnT[:, t, k, :], w("wo", k),
                                      start=(k == 0), stop=(k == KD - 1))
                    last.then_inc(proj_done, 1)

            def turn(c, ahead, far):
                pe.wait_ge(lay_dve, c * (LAYS // 2) + LAYS // 2)
                pe.wait_ge(lay_act, c * (LAYS // 2) + LAYS // 2)
                if ahead:
                    pe.wait_ge(aT_copied, c * 2)
                    project(c + 1)
                    pe.wait_ge(qkv_copied, c * (2 * TPC) + 4 * TPC)
                else:
                    pe.wait_ge(aT_copied, c * 2)
                scores(c, 0)
                pe.wait_ge(vals_ready, c + 1)
                for kv in range(1, KVH):
                    scores(c, kv)
                    if kv >= 2:
                        transpose_out(c, kv - 2)
                    weighted(c, kv - 1)
                transpose_out(c, KVH - 2)
                weighted(c, KVH - 1)
                transpose_out(c, KVH - 1)
                if ahead:
                    transpose_qk(c + 1)
                project_out(c, ahead)

            pe.wait_ge(w_ready, KD)
            pe.wait_ge(masks_ready, 2)
            project(0)
            transpose_qk(0)
            turns(pe, turn)

        @block.vector
        def _(dve):
            v = nc.vector
            chain = Chain(dve, dve_seq)

            def scale_x(c):
                src = chunk(c)
                for t in range(TPC):
                    chain.do(v.bn_stats(bn[:, t, :], src[:, t, :]))
                chain.sync()
                for t in range(TPC):
                    chain.do(v.bn_aggr(mv[:, t, :], bn[:, t, :]))
                chain.sync()
                chain.link(v.tensor_tensor(var[:, :], mv[:, :, 0], mv[:, :, 0], ALU.mult))
                chain.link(v.scalar_tensor_tensor(var[:, :], var[:, :], RMS_EPS, mv[:, :, 1], ALU.add, ALU.add))
                rsqrt(nc, chain, rms[:, :], var[:, :], s1[:, :], s2[:, :])
                dve.wait_ge(xT_done, c * 2)
                for t in range(TPC - 1):
                    chain.do(v.tensor_scalar(xs[:, t, :], src[:, t, :], rms[:, t:t + 1], None, ALU.mult))
                chain.sync()
                v.tensor_scalar(xs[:, TPC - 1, :], src[:, TPC - 1, :], rms[:, TPC - 1:TPC], None,
                                ALU.mult).then_inc(xs_ready, 1)

            def rope(c):
                dve.wait_ge(qkv_copied, c * (2 * TPC) + 2 * TPC)
                shape = [P, TPC, NQK, HD // 2]
                cos = w("cos")[:, bass.ds(c * (TPC * HD), TPC * HD)].rearrange("p (t e) -> p t e", t=TPC)
                sin = w("sin")[:, bass.ds(c * (TPC * HD), TPC * HD)].rearrange("p (t e) -> p t e", t=TPC)
                as4 = lambda a: a[:, :].rearrange("p (t h e) -> p t h e", t=TPC, h=NQK)
                chain.do(v.tensor_tensor(as4(t1), as4(qk), cos.unsqueeze(2).to_broadcast([P, TPC, NQK, HD]), ALU.mult))
                for e in range(2):
                    chain.do(v.tensor_tensor(as4(t2)[:, :, :, e::2], as4(qk)[:, :, :, 1 - e::2],
                                             sin[:, :, e::2].unsqueeze(2).to_broadcast(shape), ALU.mult))
                chain.sync()
                chain.link(v.tensor_tensor(t1[:, :], t1[:, :], t2[:, :], ALU.add))

            def norm(c):
                chain.link(v.tensor_tensor(t2[:, :], t1[:, :], t1[:, :], ALU.mult))
                chain.link(v.tensor_reduce(ss[:, :], t2[:, :].rearrange("p (h e) -> p h e", e=HD), AX, ALU.add))
                chain.link(v.tensor_scalar(ss[:, :], ss[:, :], 1.0 / HD, RMS_EPS, ALU.mult, ALU.add))
                rsqrt(nc, chain, rs[:, :], ss[:, :], n1[:, :], n2[:, :])
                src = t1[:, :].rearrange("p (t h e) -> p t h e", t=TPC, h=NQK)
                scale = rs[:, :].rearrange("p (t h) -> p t h", t=TPC)
                for dst, h0, h1 in ((qn, 0, H), (kn, H, NQK)):
                    chain.do(v.tensor_tensor(dst[:, :, :].rearrange("p (t h) e -> p t h e", t=TPC), src[:, :, h0:h1, :],
                                             scale[:, :, h0:h1].unsqueeze(3).to_broadcast([P, TPC, h1 - h0, HD]), ALU.mult))
                chain.sync()

            def split(c, part):
                q0, q1 = ((0, 3), (3, 6), (6, 8))[part]
                k0, k1 = ((0, 8), (1, 8), (2, 6))[part]
                nk = len(range(k0, k1, 3))
                if part == 0:
                    dve.wait_ge(lay_done, c * LAYS)
                chain.do(v.tensor_copy(qs[:, :, q0:q1, :], qn[:, :, :].unsqueeze(2).to_broadcast([P, TPC * H, q1 - q0, HD])))
                kc = v.tensor_copy(ks[:, :, k0:k1:3, :], kn[:, :, :].unsqueeze(2).to_broadcast([P, TPC * KVH, nk, HD]))
                if part == 2:
                    chain.sync()
                    kc.then_inc(split_ready, 1)
                    return
                chain.link(kc)
                chain.do(v.tensor_tensor(qn[:, :, :], qn[:, :, :], qs[:, :, q0, :], ALU.subtract))
                chain.link(v.tensor_tensor(kn[:, :, :], kn[:, :, :], ks[:, :, k0, :], ALU.subtract))

            def lay(c):
                for n in range(0, LAYS, 2):
                    dve.wait_ge(lay_done, c * LAYS + (n + 1))
                    if n == 2 * TPC:
                        dve.wait_ge(k_moved, c)
                    dst, src = lay_views(n)
                    v.tensor_copy(dst, src).then_inc(lay_dve, 1)

            def normalise_out(c, kv):
                dve.wait_ge(oT_done, c * KVH + (kv + 1))
                dve.wait_ge(aT_done, c * 2)
                o = bank_p[:, :].rearrange("p (m e) -> p m e", e=VW)
                chain.link(v.reciprocal(den[:, :], o[:, :, HD]))
                dst = attn[:, :, kv * GQ * HD:(kv + 1) * GQ * HD]
                v.tensor_tensor(dst.rearrange("p t (h e) -> p t h e", h=GQ),
                                o[:, :, 0:HD].rearrange("p (t h) e -> p t h e", t=TPC),
                                den[:, :].rearrange("p (t h) -> p t h", t=TPC).unsqueeze(3).to_broadcast([P, TPC, GQ, HD]),
                                ALU.mult).then_inc(o_normed, 1)

            def add_proj(c):
                dve.wait_ge(xr_added, c + 1)
                for p in range(2):
                    dve.wait_ge(proj_done, c * 2 + (p + 1))
                    dst = chunk(c)[:, 2 * p:2 * p + 2, :]
                    v.tensor_tensor(dst, dst, sbank[4 + p].rearrange("p (t d) -> p t d", t=2), ALU.add).then_inc(added, 1)

            def turn(c, ahead, far):
                if ahead:
                    rope(c + 1)
                    norm(c + 1)
                    normalise_out(c, 0)
                    split(c + 1, 0)
                    normalise_out(c, 1)
                    split(c + 1, 1)
                    normalise_out(c, 2)
                    split(c + 1, 2)
                    normalise_out(c, 3)
                    lay(c + 1)
                else:
                    for kv in range(KVH):
                        normalise_out(c, kv)
                add_proj(c)
                if far:
                    scale_x(c + 2)
                if ahead:
                    chain.restart()

            dve.wait_ge(g.later_in["wb"], 16)
            for k in range(KD):
                v.tensor_scalar(wqkv[:, k, :], w("wqkv", k), w("norm2")[:, k:k + 1], None, ALU.mult).then_inc(w_ready, 1)
            scale_x(0)
            rope(0)
            norm(0)
            for part in range(3):
                split(0, part)
            lay(0)
            scale_x(1)
            chain.restart()
            turns(dve, turn)


def tree_ffn(nc, g, tag, first, store):
    ctx = ExitStack()
    with ctx:
        def sb(name, shape, dt=F32):
            return ctx.enter_context(nc.sbuf_tensor(f"{tag}_{name}", shape, dt))

        def sem(name):
            return ctx.enter_context(nc.semaphore(f"{tag}_{name}"))

        x, w = g.x, piece(g.later["wc"], PACKS["wc"][0])
        DEPTH = 8
        xs = sb("xs", [P, TPC, D])
        xT = sb("xT", [P, TPC, KD, P])
        gate = sb("gate", [P, TPC, D])
        leaf = [sb(f"leaf{i}", [P, TPC, D]) for i in range(2)]
        leafT = sb("leafT", [P, TPC, KD, P])
        bn, mv = sb("bn", [P, TPC, 6]), sb("mv", [P, TPC, 2])
        var, rstd, s1, s2 = (sb(n, [P, TPC]) for n in ("var", "rstd", "s1", "s2"))

        def banks(name):
            return [ctx.enter_context(nc.psum_tensor(f"{tag}_{name}{i}", [P, 512], F32)) for i in range(2)]

        bank_x, bank_g, bank_l, bank_o = banks("bank_x"), banks("bank_g"), banks("bank_l"), banks("bank_o")
        dve_seq, w_prod, w_ready = sem("dve_seq"), sem("w_prod"), sem("w_ready")
        xs_ready, biased = sem("xs_ready"), sem("biased")
        xT_done, xT_copied, logits_done, gates_ready = sem("xT_done"), sem("xT_copied"), sem("logits_done"), sem("gates_ready")
        leaf_ready, leafT_done, leafT_copied = sem("leaf_ready"), sem("leafT_done"), sem("leafT_copied")
        out_done, added, stored = sem("out_done"), sem("added"), g.stored

        def chunk(c):
            return x[:, bass.ds(c * TPC, TPC), :]

        def turns(eng, body):
            body(0, True, True)
            with eng.Fori(1, NCH - 2) as c:
                body(c, True, True)
            body(NCH - 2, True, False)
            body(NCH - 1, False, False)

        block = ctx.enter_context(nc.Block())

        if store:
            @block.sync
            def _(sp):
                with sp.Fori(0, NCH) as c:
                    sp.wait_ge(added, c * 2 + 2)
                    sp.dma_start(g.out[:, bass.ds(c * TPC, TPC), :], chunk(c)).then_inc(stored, 16)
                sp.wait_ge(stored, 16 * NCH)

        @block.gpsimd
        def _(pool):
            pool.wait_ge(g.later_in["wd"], 16)
            with pool.Fori(0, NCH) as c:
                pool.wait_ge(xs_ready, c + 1)
                nc.gpsimd.tensor_tensor(chunk(c), chunk(c), piece(g.later["wd"], PACKS["wd"][0])("bias").unsqueeze(1).to_broadcast([P, TPC, D]),
                                        ALU.add).then_inc(biased, 1)

        @block.scalar
        def _(act):
            def copy(out, in_):
                return nc.scalar.activation(out, in_, ACT.Copy)

            def gates(c):
                for p in range(2):
                    act.wait_ge(xT_done, c * 2 + (p + 1))
                    if p == 0:
                        act.wait_ge(logits_done, c * 2)
                    copy(xT[:, 2 * p:2 * p + 2, :, :].rearrange("p t k n -> p (t k n)"), bank_x[p][:, :]).then_inc(xT_copied, 1)
                act.wait_ge(leaf_ready, c)
                for p in range(2):
                    act.wait_ge(logits_done, c * 2 + (p + 1))
                    nc.scalar.activation(gate[:, 2 * p:2 * p + 2, :].rearrange("p t n -> p (t n)"), bank_g[p][:, :],
                                         ACT.Sigmoid).then_inc(gates_ready, 1)

            def turn(c, ahead, far):
                if ahead:
                    gates(c + 1)
                for p in range(2):
                    act.wait_ge(leafT_done, c * 2 + (p + 1))
                    if p == 0:
                        act.wait_ge(out_done, c * 2)
                    copy(leafT[:, 2 * p:2 * p + 2, :, :].rearrange("p t k n -> p (t k n)"), bank_l[p][:, :]).then_inc(leafT_copied, 1)

            gates(0)
            turns(act, turn)

        @block.tensor
        def _(pe):
            mm, tr = nc.tensor.matmul, nc.tensor.transpose

            def transposed(src, banks, done):
                for p in range(2):
                    for t in range(2 * p, 2 * p + 2):
                        for k in range(KD):
                            at = ((t % 2) * KD + k) * P
                            last = tr(banks[p][:, at:at + P], src[:, t, k * P:(k + 1) * P], g.identf[:, :])
                    last.then_inc(done, 1)

            def product(src, weight, banks, done, ready, c):
                for p in range(2):
                    pe.wait_ge(ready, c * 2 + (p + 1))
                    for t in range(2 * p, 2 * p + 2):
                        for k in range(KD):
                            last = mm(banks[p][:, (t % 2) * D:(t % 2 + 1) * D], src[:, t, k, :], weight[:, k, :],
                                      start=(k == 0), stop=(k == KD - 1))
                    last.then_inc(done, 1)

            def logits(c):
                pe.wait_ge(xs_ready, c + 1)
                transposed(xs, bank_x, xT_done)
                pe.wait_ge(gates_ready, c * 2)
                product(xT, g.w_gate, bank_g, logits_done, xT_copied, c)

            def turn(c, ahead, far):
                if ahead:
                    logits(c + 1)
                pe.wait_ge(leaf_ready, c + 1)
                transposed(leaf[DEPTH % 2], bank_l, leafT_done)
                pe.wait_ge(added, c * 2)
                product(leafT, g.w_out, bank_o, out_done, leafT_copied, c)

            if first:
                pe.wait_ge(g.later_in["wc"], 16)
                for banks_, a, b in ((bank_g, "wq", "routersT"), (bank_o, "valuesT", "woutT")):
                    for m in range(KD):
                        for k in range(KD):
                            last = mm(banks_[m][:, 0:D], w(a, k)[:, m * P:(m + 1) * P], w(b, k), start=(k == 0), stop=(k == KD - 1))
                        last.then_inc(w_prod, 1)
                pe.wait_ge(w_ready, 2 * KD)
            logits(0)
            turns(pe, turn)

        @block.vector
        def _(dve):
            v = nc.vector
            chain = Chain(dve, dve_seq)

            def normalise(c):
                src = chunk(c)
                for t in range(TPC):
                    chain.do(v.bn_stats(bn[:, t, :], src[:, t, :]))
                chain.sync()
                for t in range(TPC):
                    chain.do(v.bn_aggr(mv[:, t, :], bn[:, t, :]))
                chain.sync()
                chain.link(v.tensor_scalar(var[:, :], mv[:, :, 1], LN_EPS, None, ALU.add))
                rsqrt(nc, chain, rstd[:, :], var[:, :], s1[:, :], s2[:, :])
                dve.wait_ge(xT_done, c * 2)
                for t in range(TPC):
                    last = v.tensor_scalar(xs[:, t, :], src[:, t, :], mv[:, t, 0:1], rstd[:, t:t + 1], ALU.subtract, ALU.mult)
                    if t < TPC - 1:
                        chain.do(last)
                last.then_inc(xs_ready, 1)
                chain.sync()

            def leaves(c):
                dve.wait_ge(gates_ready, c * 2 + 2)
                dve.wait_ge(leafT_done, c * 2)
                chain.do(v.tensor_copy(leaf[1][:, :, 1:2], gate[:, :, 0:1]))
                chain.link(v.tensor_scalar(leaf[1][:, :, 0:1], gate[:, :, 0:1], -1.0, 1.0, ALU.mult, ALU.add))
                for level in range(1, DEPTH):
                    n = 2 ** level
                    a, b = leaf[level % 2], leaf[(level + 1) % 2]
                    chain.link(v.tensor_tensor(b[:, :, 1:2 * n:2], a[:, :, 0:n], gate[:, :, n - 1:2 * n - 1], ALU.mult))
                    last = v.tensor_tensor(b[:, :, 0:2 * n:2], a[:, :, 0:n], b[:, :, 1:2 * n:2], ALU.subtract)
                    if level < DEPTH - 1:
                        chain.link(last)
                last.then_inc(leaf_ready, 1)

            def add_out(c):
                dve.wait_ge(biased, c + 1)
                for p in range(2):
                    dve.wait_ge(out_done, c * 2 + (p + 1))
                    dst = chunk(c)[:, 2 * p:2 * p + 2, :]
                    v.tensor_tensor(dst, dst, bank_o[p][:, :].rearrange("p (t d) -> p t d", t=2), ALU.add).then_inc(added, 1)

            def turn(c, ahead, far):
                leaves(c)
                if far:
                    normalise(c + 2)
                add_out(c)
                if ahead:
                    chain.sync()
                    chain.restart()

            if first:
                for m, (banks_, dst) in enumerate(((bank_g, g.w_gate), (bank_o, g.w_out))):
                    for k in range(KD):
                        dve.wait_ge(w_prod, m * KD + k + 1)
                        v.tensor_copy(dst[:, k, :], banks_[k][:, 0:D]).then_inc(w_ready, 1)
            normalise(0)
            normalise(1)
            chain.restart()
            turns(dve, turn)


def mamba_norms(nc, g):
    ctx = ExitStack()
    with ctx:
        def sb(name, shape, dt=F32):
            return ctx.enter_context(nc.sbuf_tensor("mn_" + name, shape, dt))

        def sem(name):
            return ctx.enter_context(nc.semaphore("mn_" + name))

        x, w = g.x, piece(g.later["wd"], PACKS["wd"][0])
        xs = sb("xs", [P, 2, TPC, D])
        bn, mv = sb("bn", [P, NT, 6]), sb("mv", [P, NT, 2])
        var, rln, rln2, s1, s2 = (sb(n, [P, NT]) for n in ("var", "rln", "rln2", "s1", "s2"))
        sT = sb("sT", [P, 2, KD, CH])
        obank = [[ctx.enter_context(nc.psum_tensor(f"mn_obank{i}{p}", [P, 2 * D], F32)) for p in range(2)] for i in range(2)]
        bank = [[ctx.enter_context(nc.psum_tensor(f"mn_bank{i}{k}", [P, CH], F32)) for k in range(KD)] for i in range(2)]
        dve_seq, xs_ready, xT_done, xT_copied, biased = (sem("dve_seq"), sem("xs_ready"), sem("xT_done"),
                                                         sem("xT_copied"), sem("biased"))
        h_copied, out_done, added = sem("h_copied"), sem("out_done"), sem("added")
        block = ctx.enter_context(nc.Block())

        def pairs(eng, body):
            for b in range(2):
                body(b, b)
            with eng.Fori(1, NCH // 2) as i:
                for b in range(2):
                    body(i * 2 + b, b)

        @block.gpsimd
        def _(pool):
            def turn(c, b):
                pool.wait_ge(xs_ready, c + 1)
                nc.gpsimd.tensor_tensor(x[:, bass.ds(c * TPC, TPC), :], x[:, bass.ds(c * TPC, TPC), :],
                                        w("po_b").unsqueeze(1).to_broadcast([P, TPC, D]), ALU.add).then_inc(biased, 1)
            pairs(pool, turn)

        @block.scalar
        def _(act):
            def turn(c, b):
                if not isinstance(c, int):
                    act.wait_ge(out_done, c * 2 - 2)
                for k in range(KD):
                    act.wait_ge(xT_done, c * KD + (k + 1))
                    nc.scalar.activation(sT[:, b, k, :], bank[b][k][:, :], ACT.Identity,
                                         scale=w("ln_g")[:, k:k + 1], bias=w("ln_b")[:, k:k + 1]).then_inc(xT_copied, 1)
                act.wait_ge(xT_copied, c * KD + 1)
                nc.scalar.activation(g.hT[:, bass.ds(c * CH, CH)], sT[:, b, 0, :], ACT.Copy).then_inc(h_copied, 1)
            pairs(act, turn)

        @block.tensor
        def _(pe):
            def transposes(c, b):
                pe.wait_ge(xs_ready, c + 1)
                for k in range(KD):
                    if not isinstance(c, int):
                        pe.wait_ge(xT_copied, c * KD + (k + 1 - 2 * KD))
                    for t in range(TPC):
                        last = nc.tensor.transpose(bank[b][k][:, t * P:(t + 1) * P], xs[:, b, t, k * P:(k + 1) * P], g.identf[:, :])
                    last.then_inc(xT_done, 1)

            def products(c, b):
                pe.wait_ge(xT_copied, c * KD + KD)
                for p in range(2):
                    if not isinstance(c, int):
                        pe.wait_ge(added, c * 2 + (p + 1 - 4))
                    for t in range(2):
                        for k in range(KD):
                            rows = sT[:, b, k, (2 * p + t) * P:(2 * p + t + 1) * P]
                            nc.tensor.matmul(obank[b][p][:, t * D:(t + 1) * D], rows, w("po_WT", k),
                                             start=(t == 0 and k == 0), stop=False, skip_group_check=True)
                            last = nc.tensor.matmul(obank[b][p][:, t * D + k * P:t * D + (k + 1) * P], rows, g.identf[:, :],
                                                    start=False, stop=True, skip_group_check=True)
                    last.then_inc(out_done, 1)

            def turn(c, b):
                transposes(c, b)
                products(c, b)
            pairs(pe, turn)

        @block.vector
        def _(dve):
            v = nc.vector
            chain = Chain(dve, dve_seq)

            def add_out(c):
                dve.wait_ge(biased, c + 1)
                for p in range(2):
                    dve.wait_ge(out_done, c * 2 + (p + 1))
                    dst = x[:, c * TPC + 2 * p:c * TPC + 2 * p + 2, :]
                    v.tensor_tensor(dst, dst, obank[c % 2][p][:, :].rearrange("p (t d) -> p t d", t=2), ALU.add).then_inc(added, 1)

            dve.wait_ge(g.later_in["wd"], 16)
            for i in range(NT):
                chain.do(v.bn_stats(bn[:, i, :], x[:, i, :]))
            chain.sync()
            for i in range(NT):
                chain.do(v.bn_aggr(mv[:, i, :], bn[:, i, :]))
            chain.sync()
            chain.link(v.tensor_scalar(var[:, :], mv[:, :, 1], LN_EPS, None, ALU.add))
            rsqrt(nc, chain, rln[:, :], var[:, :], s1[:, :], s2[:, :])
            chain.link(v.tensor_tensor(var[:, :], rln[:, :], rln[:, :], ALU.mult))
            chain.link(v.tensor_tensor(var[:, :], var[:, :], mv[:, :, 1], ALU.mult))
            chain.link(v.tensor_scalar(var[:, :], var[:, :], MAMBA_EPS, None, ALU.add))
            rsqrt(nc, chain, rln2[:, :], var[:, :], s1[:, :], s2[:, :])
            chain.link(v.tensor_tensor(rln[:, :], rln[:, :], rln2[:, :], ALU.mult))
            chain.restart()
            for c in range(NCH):
                if c >= 2:
                    dve.wait_ge(xT_done, KD * (c - 1))
                    add_out(c - 2)
                for t in range(TPC):
                    i = c * TPC + t
                    last = v.tensor_scalar(xs[:, c % 2, t, :], x[:, i, :], mv[:, i, 0:1], rln[:, i:i + 1], ALU.subtract, ALU.mult)
                    if t < TPC - 1:
                        chain.do(last)
                last.then_inc(xs_ready, 1)
            for c in (NCH - 2, NCH - 1):
                add_out(c)


def mamba_layers(nc, g):
    BCR = 2 * NS
    ctx = ExitStack()
    with ctx:
        def sb(name, shape, dt=F32):
            return ctx.enter_context(nc.sbuf_tensor("mb_" + name, shape, dt))

        def sem(name):
            return ctx.enter_context(nc.semaphore("mb_" + name))

        w = piece(g.later["wd"], PACKS["wd"][0])
        hT = g.hT
        decay, decay_neg = (sb(n, [P, NL * 2 * NS]) for n in ("decay", "decay_neg"))
        mean_w, zeros, eps = sb("mean_w", [P, P]), sb("zeros", [P, 2 * TAPS]), sb("eps", [P, 1])
        pick = sb("pick", [3 * BCR, BCR], BF16)
        hn = sb("hn", [P, CH])
        xpad = sb("xpad", [P, 2, TAPS - 1 + CH])
        conv = sb("conv", [P, 2, CH])
        xc, zs = sb("xc", [P, 2, 2, CH]), sb("zs", [P, 2, 2, CH])
        delta, u = sb("delta", [P, 2, 2, CH]), sb("u", [P, 2, 2, CH])
        proj = sb("proj", [3 * BCR + DTR, CH])
        bc = sb("bc", [3 * BCR, 2, CH], BF16)
        rest = sb("rest", [2 * BCR, CH])
        ea, lg, rl, w1 = (sb(n, [P, 2, CH]) for n in ("ea", "lg", "rl", "w1"))
        yz, zraw = sb("yz", [P, 2, CH]), sb("zraw", [P, 2, CH])
        RB, RX, RH, RC = 4, 4, 4, 4
        AHEAD = RB - 1
        bsb = sb("bsb", [P, RB, CH])
        dbx, hs, hc = sb("dbx", [P, RX, 2, CH]), sb("hs", [P, RH, 2, CH]), sb("hc", [P, RC, 2, CH])
        carry = sb("carry", [P, NS, 2])

        def bank(name):
            return ctx.enter_context(nc.psum_tensor("mb_" + name, [P, CH], F32))

        ybank, abank, fbank = ([bank(f"{n}{i}") for i in range(2)] for n in ("y", "a", "f"))
        bbank, cbank = bank("b"), bank("c")

        const_seq, consts, inw_ready = sem("const_seq"), sem("consts"), sem("inw_ready")
        w_ready, decay_ready = sem("w_ready"), sem("decay_ready")
        sq_ready, ms_done, ln_done, rms_ready, hn_ready = (sem(n) for n in ("sq_ready", "ms_done", "ln_done", "rms_ready", "hn_ready"))
        x_done, z_done, x_copied, z_copied = sem("x_done"), sem("z_done"), sem("x_copied"), sem("z_copied")
        tail_moved, conv_seq, conv_done = sem("tail_moved"), sem("conv_seq"), [sem(f"conv_done{i}") for i in range(2)]
        xc_ready, z_ready = sem("xc_ready"), sem("z_ready")
        xp_done, p_copied, bc1, split_seq, bc_ready = (sem(n) for n in ("xp_done", "p_copied", "bc1", "split_seq", "bc_ready"))
        dt_done, dt_read = sem("dt_done"), sem("dt_read")
        e_ready, l_ready, w1_ready, soft_seq, delta_ready, u_ready = (
            sem(n) for n in ("e_ready", "l_ready", "w1_ready", "soft_seq", "delta_ready", "u_ready"))
        b_done, b_copied, c_done, dbx_done, hc_done, y_acc, carried = (
            sem(n) for n in ("b_done", "b_copied", "c_done", "dbx_done", "hc_done", "y_acc", "carried"))
        da_done, scan_done = sem("da_done"), sem("scan_done")
        y_read, yz_ready, mo_done, h_added = (sem(n) for n in ("y_read", "yz_ready", "mo_done", "h_added"))
        HS = 2 * NS

        def slab(ap, c):
            return ap[:, bass.ds(c * CH, CH)]

        def turns(eng, first, body, last):
            def chunk(l, c, b):
                if isinstance(c, int):
                    l, c = l + c // NCH, c % NCH
                    if l >= NL:
                        return None
                return (c + l * NCH, l, c, b)

            def turn(l, c, b):
                before = (c + (l * NCH - 1), None, None, 1 - b) if not isinstance(c, int) else \
                    (l * NCH + c - 1, (l * NCH + c - 1) // NCH, (c - 1) % NCH, 1 - b) if l + c else None
                if before and not isinstance(c, int):
                    before = (before[0], l, c - 1, 1 - b)
                body(chunk(l, c, b), before, chunk(l, c + 1, 1 - b), chunk(l, c + 2, b))

            first(chunk(0, 0, 0), chunk(0, 1, 1))
            for l in range(NL):
                for c in range(2):
                    turn(l, c, c)
                with eng.Fori(1, NCH // 2 - 1) as i:
                    for b in range(2):
                        turn(l, i * 2 + b, b)
                for c in (NCH - 2, NCH - 1):
                    turn(l, c, c % 2)
            last(chunk(NL - 1, NCH - 1, 1))

        block = ctx.enter_context(nc.Block())

        @block.gpsimd
        def _(pool):
            gp = nc.gpsimd
            setup = Chain(pool, const_seq)
            for t, val in ((mean_w, 1.0 / P), (zeros, 0.0), (eps, MAMBA_EPS)):
                gp.memset(t[:, :], val).then_inc(consts, 1)
            gp.memset(carry[:, :, :], 0.0).then_inc(consts, 1)
            setup.link(gp.memset(pick[:, :], 0.0))
            for q in range(3):
                ins = gp.affine_select(out=pick[:, :], in_=pick[:, :], compare_op=ALU.not_equal, fill=1.0, base=-q * BCR,
                                       pattern=[[-1, BCR]], channel_multiplier=1)
                if q < 2:
                    setup.link(ins)
            ins.then_inc(consts, 1)
            pool.wait_ge(consts, 5)

            def split(f, b):
                pool.wait_ge(bc1, f + 1)
                gp.tensor_tensor(rest[:, :], proj[0:2 * BCR, :], bc[0:2 * BCR, b, :], ALU.subtract).then_inc(split_seq, 1)
                pool.wait_ge(split_seq, f * 2 + 1)
                gp.tensor_tensor(bc[0:2 * BCR, b, :], rest[:, :], g.zero[0:2 * BCR, 0:1].to_broadcast([2 * BCR, CH]),
                                 ALU.add).then_inc(split_seq, 1)
                pool.wait_ge(split_seq, f * 2 + 2)
                gp.tensor_tensor(bc[0:BCR, b, :], rest[0:BCR, :], bc[0:BCR, b, :], ALU.subtract).then_inc(bc_ready, 1)

            def softplus_1(f):
                pool.wait_ge(w1_ready, f + 1)
                gp.tensor_tensor(w1[:, :, :], ea[:, :, :], w1[:, :, :], ALU.subtract).then_inc(soft_seq, 1)

            def softplus_2(f):
                pool.wait_ge(soft_seq, f * 2 + 1)
                pool.wait_ge(l_ready, f + 1)
                gp.tensor_tensor(w1[:, :, :], w1[:, :, :], lg[:, :, :], ALU.add).then_inc(soft_seq, 1)

            def softplus_3(f, b, m):
                pool.wait_ge(da_done, m * HS)
                pool.wait_ge(soft_seq, f * 2 + 2)
                gp.tensor_tensor(delta[:, b, :, :], w1[:, :, :], rl[:, :, :], ALU.add).then_inc(delta_ready, 1)

            def first(one, two):
                split(0, 0)
                softplus_1(0)
                softplus_2(0)
                softplus_3(0, 0, 0)

            def body(now, before, nxt, far):
                m, l, c, b = now
                pool.wait_ge(u_ready, m + 1)
                for n in range(NS):
                    pool.wait_ge(b_copied, m * NS + (n + 1))
                    if before or n >= RX:
                        pool.wait_ge(scan_done, m * HS + 2 * (n - RX + 1))
                    gp.tensor_tensor(dbx[:, n % RX, :, :], u[:, b, :, :],
                                     bsb[:, n % RB, :].unsqueeze(1).to_broadcast([P, 2, CH]), ALU.mult).then_inc(dbx_done, 1)
                    if nxt:
                        f, _, _, fb = nxt
                        if n == 7:
                            split(f, fb)
                        if n == 12:
                            softplus_1(f)
                        if n == 13:
                            softplus_2(f)
                        if n == 14:
                            softplus_3(f, fb, m)

            turns(pool, first, body, lambda end: None)

        @block.scalar
        def _(act):
            def fn(out, in_, func=ACT.Copy, **kw):
                return nc.scalar.activation(out, in_, func, **kw)

            def exp_ln_tables():
                nc.scalar.preload_act_table_set("natural_log_exp_and_others")

            def square(f, l, c):
                if l:
                    act.wait_ge(h_added, c + 1)
                act.wait_ge(z_done, f * 2)
                fn(hn[:, :], slab(hT, c), ACT.Square).then_inc(sq_ready, 1)

            def rms(f):
                act.wait_ge(ms_done, f + 1)
                fn(fbank[1][:, :], fbank[1][:, :], ACT.Ln, bias=eps[:, 0:1]).then_inc(ln_done, 1)
                act.wait_ge(ln_done, f + 1)
                fn(fbank[1][:, :], fbank[1][:, :], ACT.Exp, scale=-0.5).then_inc(rms_ready, 1)

            def move_tail(f, c):
                for done in conv_done:
                    act.wait_ge(done, f)
                src = zeros[:, 0:2 * (TAPS - 1)].rearrange("p (h t) -> p h t", h=2) if isinstance(c, int) and c == 0 \
                    else xpad[:, :, CH:CH + TAPS - 1]
                fn(xpad[:, :, 0:TAPS - 1], src).then_inc(tail_moved, 1)

            def copy_x(f, half):
                if half == 0:
                    act.wait_ge(tail_moved, f + 1)
                act.wait_ge(x_done, f * 2 + (half + 1))
                fn(xpad[:, half, TAPS - 1:], fbank[1][:, :]).then_inc(x_copied, 1)

            def copy_z(f, half):
                act.wait_ge(z_done, f * 2 + (half + 1))
                if half == 0:
                    act.wait_ge(z_ready, f)
                fn(zraw[:, half, :], fbank[1][:, :]).then_inc(z_copied, 1)

            def silus(f, l, b, before):
                if before:
                    act.wait_ge(yz_ready, before[0] + 1)
                for half in range(2):
                    act.wait_ge(conv_done[half], f + 1)
                    fn(xc[:, b, half, :], conv[:, half, :], ACT.Silu,
                       bias=w("conv_b", l)[:, half:half + 1]).then_inc(xc_ready, 1)
                act.wait_ge(z_copied, f * 2 + 2)
                fn(zs[:, b, :, :], zraw[:, :, :], ACT.Silu).then_inc(z_ready, 1)
                exp_ln_tables()

            def project(f, b, before):
                act.wait_ge(xp_done, f + 1)
                act.wait_ge(bc_ready, f)
                fn(proj[:, :], fbank[0][0:3 * BCR + DTR, :]).then_inc(p_copied, 1)
                act.wait_ge(p_copied, f + 1)
                if before:
                    act.wait_ge(c_done, (before[0] + 1) * NS)
                fn(bc[:, b, :], proj[0:3 * BCR, :]).then_inc(bc1, 1)

            def abs_relu(f, l, half):
                act.wait_ge(dt_done, f * 2 + (half + 1))
                if half == 0:
                    act.wait_ge(delta_ready, f)
                bias = w("dt_b", l)[:, half:half + 1]
                fn(ea[:, half, :], fbank[0][:, :], ACT.Abs, bias=bias).then_inc(dt_read, 1)
                fn(rl[:, half, :], fbank[0][:, :], ACT.Relu, bias=bias).then_inc(dt_read, 1)

            def exp_e(f):
                act.wait_ge(dt_read, f * 4 + 4)
                fn(ea[:, :, :], ea[:, :, :], ACT.Exp, scale=-1.0).then_inc(e_ready, 1)

            def ln_e(f):
                act.wait_ge(e_ready, f + 1)
                fn(lg[:, :, :], ea[:, :, :], ACT.Ln, bias=1.0).then_inc(l_ready, 1)

            def copy_b(m, n, fresh):
                act.wait_ge(b_done, m * NS + (n + 1))
                if not fresh:
                    act.wait_ge(dbx_done, m * NS + (n - RB + 1))
                fn(bsb[:, n % RB, :], bbank[:, :]).then_inc(b_copied, 1)

            def carry_on(m, n, end):
                act.wait_ge(scan_done, m * HS + 2 * (n + 1))
                src = zeros[:, 0:2] if end else hs[:, n % RH, :, CH - 1]
                fn(carry[:, n, :], src).then_inc(carried, 1)

            def first(one, two):
                exp_ln_tables()
                act.wait_ge(g.later_in["wd"], 16)
                fn(decay[:, :], w("A_log"), ACT.Exp).then_inc(w_ready, 1)
                act.wait_ge(consts, 5)
                for f, l, c, b in (one, two):
                    square(f, l, c)
                    rms(f)
                    move_tail(f, c)
                    for half in range(2):
                        copy_x(f, half)
                    for half in range(2):
                        copy_z(f, half)
                    if f == 0:
                        silus(f, l, b, None)
                        project(f, b, None)
                        for half in range(2):
                            abs_relu(f, l, half)
                        exp_e(f)
                        ln_e(f)
                for n in range(AHEAD - 1):
                    copy_b(0, n, True)
                act.wait_ge(decay_ready, 1)

            def body(now, before, nxt, far):
                m, l, c, b = now
                act.wait_ge(delta_ready, m + 1)
                for n in range(NS):
                    for half in range(2):
                        s = 2 * n + half
                        if before or s >= 2:
                            act.wait_ge(scan_done, m * HS + (s - 1))
                        at = (l * 2 + half) * NS + n
                        fn(abank[half][:, :], delta[:, b, half, :], ACT.Exp, scale=decay_neg[:, at:at + 1]).then_inc(da_done, 1)
                    if n:
                        carry_on(m, n - 1, nxt is None or nxt[1] != l)
                    elif before:
                        carry_on(before[0], NS - 1, before[1] != l)
                    k = n + AHEAD - 1
                    if k < NS:
                        copy_b(m, k, k < RB and not before)
                    elif nxt:
                        copy_b(nxt[0], k - NS, False)
                    if nxt:
                        f, fl, fc, fb = nxt
                        if n == 5:
                            project(f, fb, before)
                        if n in (7, 9):
                            abs_relu(f, fl, (n - 7) // 2)
                        if n == 10:
                            exp_e(f)
                        if n == 11:
                            ln_e(f)
                    if far:
                        f, fl, fc, fb = far
                        if n == 1:
                            square(f, fl, fc)
                        if n == 6:
                            rms(f)
                        if n == 8:
                            move_tail(f, fc)
                        if n in (9, 11):
                            copy_x(f, (n - 9) // 2)
                        if n in (13, 15):
                            copy_z(f, (n - 13) // 2)
                    if nxt and n == 2:
                        silus(nxt[0], nxt[1], nxt[3], before)

            turns(act, first, body, lambda end: None)

        @block.tensor
        def _(pe):
            mm = nc.tensor.matmul

            def mean_sq(f):
                pe.wait_ge(sq_ready, f + 1)
                if not isinstance(f, int) or f:
                    pe.wait_ge(z_copied, f * 2)
                mm(fbank[1][:, :], mean_w[:, :], hn[:, :], start=True, stop=True).then_inc(ms_done, 1)

            def in_proj(f, l, e):
                if e == 0:
                    pe.wait_ge(hn_ready, f + 1)
                elif e < 3:
                    pe.wait_ge(x_copied, f * 2 + e)
                else:
                    pe.wait_ge(z_copied, f * 2 + 1)
                mm(fbank[1][:, :], w("in_WT", l)[:, e * P:(e + 1) * P], hn[:, :], start=True, stop=True).then_inc((x_done, z_done)[e // 2], 1)

            def x_proj(f, l, b):
                if not isinstance(f, int) or f:
                    pe.wait_ge(dt_read, f * 4)
                pe.wait_ge(xc_ready, f * 2 + 2)
                for half in range(2):
                    last = mm(fbank[0][0:3 * BCR + DTR, :], w("xp_WT", l * 2 + half), xc[:, b, half, :], start=(half == 0), stop=(half == 1))
                last.then_inc(xp_done, 1)

            def dt_proj(f, l, half):
                if half == 0:
                    pe.wait_ge(p_copied, f + 1)
                else:
                    pe.wait_ge(dt_read, f * 4 + 2)
                at = 3 * BCR
                mm(fbank[0][:, :], w("dt_WT", l)[at:at + DTR, half * P:(half + 1) * P], proj[at:at + DTR, :],
                   start=True, stop=True).then_inc(dt_done, 1)

            def mo_proj(m, l):
                pe.wait_ge(yz_ready, m + 1)
                for half in range(2):
                    last = mm(ybank[0][:, :], w("mo_WT", l * 2 + half), yz[:, half, :], start=(half == 0), stop=(half == 1))
                last.then_inc(mo_done, 1)

            def rows_b(m, b, n, fresh=False):
                if not fresh:
                    pe.wait_ge(b_copied, m * NS + n)
                mm(bbank[:, :], pick[:, n:n + 1].to_broadcast([3 * BCR, P]), bc[:, b, :], start=True, stop=True).then_inc(b_done, 1)

            def rows_c(m, b, n, fresh):
                if not fresh:
                    pe.wait_ge(hc_done, m * NS + n)
                mm(cbank[:, :], pick[:, NS + n:NS + n + 1].to_broadcast([3 * BCR, P]), bc[:, b, :],
                   start=True, stop=True).then_inc(c_done, 1)

            def add_state(m, n):
                pe.wait_ge(hc_done, m * NS + (n + 1))
                for half in range(2):
                    last = mm(ybank[half][:, :], g.identf[:, :], hc[:, n % RC, half, :], start=(n == 0), stop=(n == NS - 1))
                last.then_inc(y_acc, 1)

            def first(one, two):
                pe.wait_ge(consts, 5)
                pe.wait_ge(inw_ready, NL)
                for f, l, c, b in (one, two):
                    mean_sq(f)
                    for e in range(4):
                        in_proj(f, l, e)
                    if f == 0:
                        x_proj(f, l, b)
                        for half in range(2):
                            dt_proj(f, l, half)
                pe.wait_ge(bc_ready, 1)
                for n in range(AHEAD):
                    rows_b(0, 0, n, n == 0)

            def body(now, before, nxt, far):
                m, l, c, b = now
                for n in range(NS):
                    if n + AHEAD < NS:
                        rows_b(m, b, n + AHEAD)
                    elif nxt:
                        if n + AHEAD == NS:
                            pe.wait_ge(bc_ready, nxt[0] + 1)
                        rows_b(nxt[0], nxt[3], n + AHEAD - NS)
                    rows_c(m, b, n, n == 0 and not before)
                    if n == 1 and before:
                        pe.wait_ge(h_added, m)
                    if n:
                        add_state(m, n - 1)
                    elif before:
                        add_state(before[0], NS - 1)
                    if far and n == 4:
                        mean_sq(far[0])
                    if n == 0 and before:
                        mo_proj(before[0], before[1])
                    if nxt:
                        f, fl, fc, fb = nxt
                        if n == 3:
                            x_proj(f, fl, fb)
                        if n in (5, 7):
                            dt_proj(f, fl, (n - 5) // 2)
                    if far and n in (7, 9, 11, 13):
                        in_proj(far[0], far[1], (n - 7) // 2)

            def last(end):
                m, l, c, b = end
                add_state(m, NS - 1)
                mo_proj(m, l)

            turns(pe, first, body, last)

        @block.vector
        def _(dve):
            v = nc.vector

            def normed(f, l, c):
                dve.wait_ge(rms_ready, f + 1)
                if l:
                    dve.wait_ge(h_added, c + 1)
                v.tensor_tensor(hn[:, :], slab(hT, c), fbank[1][:, :], ALU.mult).then_inc(hn_ready, 1)

            def convolve(f, l, k):
                if k == 0:
                    dve.wait_ge(x_copied, f * 2 + 2)
                    dve.wait_ge(xc_ready, f * 2)
                for half in range(2):
                    tap = w("conv_w", l)[:, half * TAPS + k:half * TAPS + k + 1]
                    src = xpad[:, half, k:k + CH]
                    if k == 0:
                        ins = v.tensor_scalar(conv[:, half, :], src, tap, None, ALU.mult)
                    else:
                        dve.wait_ge(conv_seq, f * 6 + (2 * k + half - 1))
                        ins = v.scalar_tensor_tensor(conv[:, half, :], src, tap, conv[:, half, :], ALU.mult, ALU.add)
                    ins.then_inc(conv_done[half] if k == TAPS - 1 else conv_seq, 1)

            def one_plus(f):
                dve.wait_ge(e_ready, f + 1)
                dve.wait_ge(delta_ready, f)
                v.tensor_scalar(w1[:, :, :], ea[:, :, :], 1.0, -1.0, ALU.add, ALU.add).then_inc(w1_ready, 1)

            def inputs(f, b):
                dve.wait_ge(delta_ready, f + 1)
                dve.wait_ge(xc_ready, f * 2 + 2)
                v.tensor_tensor(u[:, b, :, :], delta[:, b, :, :], xc[:, b, :, :], ALU.mult).then_inc(u_ready, 1)

            def finish_y(m, l, b):
                dve.wait_ge(y_acc, m * NS + NS)
                for half in range(2):
                    v.scalar_tensor_tensor(yz[:, half, :], xc[:, b, half, :], w("Dp", l)[:, half:half + 1], ybank[half][:, :],
                                           ALU.mult, ALU.add).then_inc(y_read, 1)
                dve.wait_ge(y_read, m * 2 + 2)
                dve.wait_ge(z_ready, m + 1)
                v.tensor_tensor(yz[:, :, :], yz[:, :, :], zs[:, b, :, :], ALU.mult).then_inc(yz_ready, 1)

            def add_h(m, l, c):
                dve.wait_ge(mo_done, m + 1)
                v.tensor_tensor(slab(hT, c), slab(hT, c), ybank[0][:, :], ALU.add).then_inc(h_added, 1)

            def weighted(m, n):
                dve.wait_ge(scan_done, m * HS + 2 * (n + 1))
                dve.wait_ge(c_done, m * NS + (n + 1))
                if not isinstance(m, int) or m or n >= RC:
                    dve.wait_ge(y_acc, m * NS + (n - RC + 1))
                v.tensor_tensor(hc[:, n % RC, :, :], hs[:, n % RH, :, :], cbank[:, :].unsqueeze(1).to_broadcast([P, 2, CH]),
                                ALU.mult).then_inc(hc_done, 1)

            def first(one, two):
                dve.wait_ge(g.later_in["wd"], 16)
                for i in range(NL):
                    v.tensor_scalar(w("in_WT", i), w("in_WT", i), w("rms_w")[:, i:i + 1], None, ALU.mult).then_inc(inw_ready, 1)
                dve.wait_ge(w_ready, 1)
                v.tensor_scalar(decay_neg[:, :], decay[:, :], -1.0, None, ALU.mult).then_inc(decay_ready, 1)
                for f, l, c, b in (one, two):
                    normed(f, l, c)
                    for k in range(TAPS):
                        convolve(f, l, k)
                    if f == 0:
                        one_plus(f)
                        inputs(f, b)

            def body(now, before, nxt, far):
                m, l, c, b = now
                for n in range(NS):
                    if nxt and n == NS - 1:
                        inputs(nxt[0], nxt[3])
                    dve.wait_ge(dbx_done, m * NS + (n + 1))
                    if before or n >= RH:
                        dve.wait_ge(carried, m * NS + (n - RH + 1))
                    for half in range(2):
                        dve.wait_ge(da_done, m * HS + (2 * n + half + 1))
                        if before and n == NS - 1 and half == 0:
                            dve.wait_ge(carried, m * NS)
                        v.tensor_tensor_scan(hs[:, n % RH, half, :], abank[half][:, :], dbx[:, n % RX, half, :],
                                             carry[:, n, half:half + 1], ALU.mult, ALU.add).then_inc(scan_done, 1)
                    if before and n == 1:
                        finish_y(before[0], before[1], before[3])
                    if before and n == 2:
                        add_h(before[0], before[1], before[2])
                    if n:
                        weighted(m, n - 1)
                    elif before:
                        weighted(before[0], NS - 1)
                    if nxt:
                        f, fl, fc, fb = nxt
                        if n == 10:
                            one_plus(f)
                    if far:
                        f, fl, fc, fb = far
                        if n == 6:
                            normed(f, fl, fc)
                        if n >= NS - TAPS:
                            convolve(f, fl, n - (NS - TAPS))

            def last(end):
                m, l, c, b = end
                weighted(m, NS - 1)
                finish_y(m, l, b)
                add_h(m, l, c)

            turns(dve, first, body, last)


def mamba_out(nc, g):
    ctx = ExitStack()
    with ctx:
        def sem(name):
            return ctx.enter_context(nc.semaphore("mo_" + name))

        w = piece(g.later["wd"], PACKS["wd"][0])
        yT = ctx.enter_context(nc.sbuf_tensor("mo_yT", [P, 2, KD, CH], F32))
        pbank, tbank = ([[ctx.enter_context(nc.psum_tensor(f"mo_{n}{b}{k}", [P, CH], F32)) for k in range(KD)]
                         for b in range(2)] for n in ("p", "t"))
        po_done, y_ready, yT_done, added = sem("po_done"), sem("y_ready"), sem("yT_done"), sem("added")
        block = ctx.enter_context(nc.Block())

        def slab(ap, c):
            return ap[:, bass.ds(c * CH, CH)]

        def pairs(eng, body):
            for b in range(2):
                body(b, b, False)
            with eng.Fori(1, NCH // 2) as i:
                for b in range(2):
                    body(i * 2 + b, b, True)

        @block.scalar
        def _(act):
            def turn(c, b, again):
                if again:
                    act.wait_ge(yT_done, c * 2 - 2)
                for k in range(KD):
                    act.wait_ge(po_done, c * KD + (k + 1))
                    nc.scalar.activation(yT[:, b, k, :], pbank[b][k][:, :], ACT.Copy).then_inc(y_ready, 1)

            pairs(act, turn)

        @block.tensor
        def _(pe):
            def project(c, b, again):
                for k in range(KD):
                    if again:
                        pe.wait_ge(y_ready, c * KD + (k + 1 - 2 * KD))
                    nc.tensor.matmul(pbank[b][k][:, :], w("po_WT", KD - 1)[:, k * P:(k + 1) * P], slab(g.hT, c),
                                     start=True, stop=True).then_inc(po_done, 1)

            def back(c, b, again):
                pe.wait_ge(y_ready, c * KD + KD)
                for p in range(2):
                    if again:
                        pe.wait_ge(added, c * 2 + (p + 1 - 4))
                    for t in range(2):
                        for k in range(KD):
                            at = (2 * p + t) * P
                            last = nc.tensor.transpose(tbank[b][p][:, (t * KD + k) * P:(t * KD + k + 1) * P],
                                                       yT[:, b, k, at:at + P], g.identf[:, :])
                    last.then_inc(yT_done, 1)

            def turn(c, b, again):
                project(c, b, again)
                back(c, b, again)

            pairs(pe, turn)

        @block.vector
        def _(dve):
            v = nc.vector

            def turn(c, b, again):
                for p in range(2):
                    dve.wait_ge(yT_done, c * 2 + (p + 1))
                    dst = g.x[:, bass.ds(c * TPC + 2 * p, 2), :]
                    v.tensor_tensor(dst, dst, tbank[b][p][:, :].rearrange("p (t d) -> p t d", t=2), ALU.add).then_inc(added, 1)

            pairs(dve, turn)


def kernel(**inputs):
    import concourse.bacc as bacc
    from concourse.bass_utils import run_bass_kernel_spmd
    nc = bacc.Bacc("TRN2", target_bir_lowering=False, num_devices=1)
    arrays = lay_out(inputs)
    dram = {name: nc.dram_tensor("in_" + name, a.shape, mybir.dt.from_np(a.dtype), kind="ExternalInput").ap()
            for name, a in arrays.items()}
    out = nc.dram_tensor("out_x", (P, NT, D), F32, kind="ExternalOutput").ap()
    build(nc, dram, out)
    nc.compile()
    res = run_bass_kernel_spmd(nc, [{"in_" + name: a for name, a in arrays.items()}], core_ids=[0])
    return np.asarray(res.results[0]["out_x"]).transpose(1, 0, 2).reshape(1, S, D)
```

```python
from contextlib import ExitStack

import numpy as np

import concourse.bass as bass
from concourse import mybir

F32 = mybir.dt.float32
BF16 = mybir.dt.bfloat16
I32 = mybir.dt.int32
ACT = mybir.ActivationFunctionType
ALU = mybir.AluOpType
AX = mybir.AxisListType.X

P = 128
S, D = 4096, 256
NT = S // P
TPC = 4
CH = TPC * P
NCH = S // CH
KD = D // P
H, KVH, HD = 16, 4, 16
GQ = H // KVH
NQK = H + KVH
QKW, QKVW = NQK * HD, (NQK + KVH) * HD
LAT, WIN = 64, 64
TERMS = 8
VW = 32
NL, NS, DTR, TAPS = 2, 16, 8, 4
HALVES = 2
DI = HALVES * P
XPW = 3 * 2 * NS + DTR
LN_EPS, RMS_EPS, MAMBA_EPS = 1e-5, 1e-6, 1e-5
NEG = -30000.0
SCORE_SCALE = 1.0 / 4.0


class Tiles:
    pass


class Chain:

    def __init__(self, eng, sem):
        self.eng, self.sem, self.count = eng, sem, 0

    def do(self, ins):
        ins.then_inc(self.sem, 1)
        self.count += 1

    def sync(self):
        if self.count:
            self.eng.wait_ge(self.sem, self.count)

    def link(self, ins):
        self.do(ins)
        self.sync()

    def restart(self):
        self.eng.sem_clear(self.sem)
        self.count = 0


def rsqrt(nc, *parts):
    v = nc.vector
    for chain, y, x, half, tmp in parts:
        chain.sync()
        chain.do(v.tensor_scalar(half, x, -0.5, None, ALU.mult))
        chain.do(v.tensor_single_scalar(tmp.bitcast(I32), x.bitcast(I32), 1, ALU.logical_shift_right))
    for chain, y, x, half, tmp in parts:
        chain.sync()
        chain.do(v.tensor_scalar(y.bitcast(I32), tmp.bitcast(I32), -1.0, float(0x5F3759DF), ALU.mult, ALU.add))
    for _ in range(3):
        for chain, y, x, half, tmp in parts:
            chain.sync()
            chain.do(v.tensor_tensor(tmp, y, y, ALU.mult))
        for chain, y, x, half, tmp in parts:
            chain.sync()
            chain.do(v.tensor_tensor(tmp, tmp, half, ALU.mult))
        for chain, y, x, half, tmp in parts:
            chain.sync()
            chain.do(v.scalar_tensor_tensor(y, tmp, 1.5, y, ALU.add, ALU.mult))
    for chain, *_ in parts:
        chain.sync()


def pair_swap(ap):
    return ap.rearrange("p h (e t) -> p h e t", t=2)[:, :, :, ::-1]


def heads(ap, n):
    return ap.rearrange("p (h e) -> p h e", h=n)


def spread(ap, n):
    return ap.unsqueeze(2).to_broadcast([P, n, HD])


def rope_norm_split(nc, tiles, split_ready):
    v = nc.vector
    for chain, b, qkv, cos, sin in tiles:
        qk, t1, t2 = (heads(t[:, :], NQK) for t in (qkv, b.t1, b.t2))
        cosb = cos.unsqueeze(1).to_broadcast([P, NQK, HD])
        sinb = sin.rearrange("p (e t) -> p e t", t=2).unsqueeze(1).to_broadcast([P, NQK, HD // 2, 2])
        chain.do(v.tensor_tensor(t1, qk, cosb, ALU.mult))
        chain.do(v.tensor_tensor(t2.rearrange("p h (e t) -> p h e t", t=2), pair_swap(qk), sinb, ALU.mult))
    for chain, b, *_ in tiles:
        chain.sync()
        chain.do(v.tensor_tensor(b.t1[:, :], b.t1[:, :], b.t2[:, :], ALU.add))
    for chain, b, *_ in tiles:
        chain.sync()
        chain.do(v.tensor_tensor(b.t2[:, :], b.t1[:, :], b.t1[:, :], ALU.mult))
    for chain, b, *_ in tiles:
        chain.sync()
        chain.do(v.tensor_reduce(b.ss[:, :], heads(b.t2[:, :], NQK), AX, ALU.add))
    for chain, b, *_ in tiles:
        chain.sync()
        chain.do(v.tensor_scalar(b.ss[:, :], b.ss[:, :], 1.0 / HD, RMS_EPS, ALU.mult, ALU.add))
    rsqrt(nc, *((chain, b.rs[:, :], b.ss[:, :], b.n1[:, :], b.n2[:, :]) for chain, b, *_ in tiles))
    for chain, b, *_ in tiles:
        t1 = heads(b.t1[:, :], NQK)
        chain.do(v.tensor_tensor(t1, t1, spread(b.rs[:, :], NQK), ALU.mult))
    for part in range(3):
        q0, q1 = ((0, 3), (3, 6), (6, 8))[part]
        k0, k1 = ((0, 8), (1, 8), (2, 6))[part]
        nk = len(range(k0, k1, 3))
        for chain, b, *_ in tiles:
            t1 = heads(b.t1[:, :], NQK)
            q, k = t1[:, 0:H, :], t1[:, H:NQK, :]
            qs = b.qs[:, :].rearrange("p (h r e) -> p h r e", h=H, r=TERMS)
            ks = b.ks[:, :].rearrange("p (h r e) -> p h r e", h=KVH, r=TERMS)
            chain.sync()
            chain.do(v.tensor_copy(qs[:, :, q0:q1, :], q.unsqueeze(2).to_broadcast([P, H, q1 - q0, HD])))
            last = v.tensor_copy(ks[:, :, k0:k1:3, :], k.unsqueeze(2).to_broadcast([P, KVH, nk, HD]))
            if part == 2:
                last.then_inc(split_ready, 1)
            else:
                chain.do(last)
        if part < 2:
            for chain, b, *_ in tiles:
                t1 = heads(b.t1[:, :], NQK)
                q, k = t1[:, 0:H, :], t1[:, H:NQK, :]
                qs = b.qs[:, :].rearrange("p (h r e) -> p h r e", h=H, r=TERMS)
                ks = b.ks[:, :].rearrange("p (h r e) -> p h r e", h=KVH, r=TERMS)
                chain.sync()
                chain.do(v.tensor_tensor(q, q, qs[:, :, q0, :], ALU.subtract))
                chain.do(v.tensor_tensor(k, k, ks[:, :, k0, :], ALU.subtract))


def global_attention(nc, g, dram):
    ctx = ExitStack()
    with ctx:
        def sb(name, shape, dt=F32):
            return ctx.enter_context(nc.sbuf_tensor(name, shape, dt))

        def pb(name, shape):
            return ctx.enter_context(nc.psum_tensor(name, shape, F32))

        def sem(name):
            return ctx.enter_context(nc.semaphore(name))

        x = g.x
        w = g.wa_col
        kT = sb("ga_kT", [P, NCH * KVH * CH], BF16)
        qT = sb("ga_qT", [P, 2, H, CH], BF16)
        vals = sb("ga_vals", [P, NCH, KVH, TPC, HD])
        probs = sb("ga_probs", [P, 2, 2, 2 * CH])
        wqkv = sb("ga_wqkv", [P, KD, QKVW])
        xnT = sb("ga_xnT", [P, 2, KD, P])
        tile_bufs = []
        for i in range(2):
            b = Tiles()
            b.qkv, b.t1, b.t2 = (sb(f"ga_{n}{i}", [P, QKW]) for n in ("qkv", "t1", "t2"))
            b.ss, b.rs, b.n1, b.n2 = (sb(f"ga_{n}{i}", [P, NQK]) for n in ("ss", "rs", "n1", "n2"))
            b.qs, b.ks = sb(f"ga_qs{i}", [P, H * P], BF16), sb(f"ga_ks{i}", [P, KVH * P], BF16)
            tile_bufs.append(b)
        b = tile_bufs[0]
        pair_qkv = [[b.qkv for b in tile_bufs], [sb(f"ga_qkv{i}", [P, QKW]) for i in (2, 3)]]
        bn = sb("ga_bn", [P, NT, 6])
        mv = sb("ga_mv", [P, NT, 2])
        var = sb("ga_var", [P, NT])
        rln = sb("ga_rln", [P, NT])
        rms = sb("ga_rms", [P, NT])
        st1 = sb("ga_st1", [P, NT])
        st2 = sb("ga_st2", [P, NT])
        v_diag = sb("ga_v_diag", [P, 3, VW])
        v_ab = sb("ga_v_ab", [P, 2, VW])
        v_cd = sb("ga_v_cd", [P, 2, VW])
        oT = sb("ga_oT", [P, CH])
        den = sb("ga_den", [P, H])
        attn = sb("ga_attn", [P, 2, TPC, D])
        attnT = sb("ga_attnT", [P, KD, P])

        score = [pb(f"ga_score{i}", [P, 2 * CH]) for i in range(2)]
        out_acc = pb("ga_out_acc", [P, CH])
        bank_a = pb("ga_bank_a", [P, 512])
        bank_b = pb("ga_bank_b", [P, 512])
        bank_c = pb("ga_bank_c", [P, 512])

        x_in = [sem(f"ga_x_in{c}") for c in range(NCH)]
        w_in = sem("ga_w_in")
        v_const = sem("ga_v_const")
        w_prod, w_ready = sem("ga_w_prod"), sem("ga_w_ready")
        dve_seq, dve_seq1 = sem("ga_dve_seq"), sem("ga_dve_seq1")
        xn_ready, xT_done, xT_copied = sem("ga_xn_ready"), sem("ga_xT_done"), sem("ga_xT_copied")
        qkv_done, qkv_copied = sem("ga_qkv_done"), sem("ga_qkv_copied")
        split_ready = sem("ga_split_ready")
        qa_done, qb_done, kk_done = sem("ga_qa_done"), sem("ga_qb_done"), sem("ga_kk_done")
        qa_copied, qb_copied, kk_copied = sem("ga_qa_copied"), sem("ga_qb_copied"), sem("ga_kk_copied")
        scores_done, exp_done, kb_done = sem("ga_scores_done"), sem("ga_exp_done"), sem("ga_kb_done")
        vd_staged, vab_staged, vcd_staged = sem("ga_vd_staged"), sem("ga_vab_staged"), sem("ga_vcd_staged")
        o_copied, oT_done, o_normed = sem("ga_o_copied"), sem("ga_oT_done"), sem("ga_o_normed")
        aT_done, aT_copied, proj_done, proj_added = (sem("ga_aT_done"), sem("ga_aT_copied"),
                                                     sem("ga_proj_done"), sem("ga_proj_added"))

        NG = NCH * KVH
        LEAD = 5
        READY = 2 * TPC
        pair_banks = [score[i][:, h * 512:(h + 1) * 512] for i in range(2) for h in range(2)]
        first_kb = [0]
        for n in range(NG):
            first_kb.append(first_kb[-1] + TPC + TPC * (n // KVH))

        def kcols(c, kv, j):
            return ((c * KVH + kv) * TPC + j) * P

        block = ctx.enter_context(nc.Block())

        @block.sync
        def _(sp):
            sp.dma_start(g.wa[:, :], dram["wa"]).then_inc(w_in, 16)
            for c in range(NCH):
                sp.dma_start(x[:, c * TPC:(c + 1) * TPC, :], dram["x"][:, c * TPC:(c + 1) * TPC, :]).then_inc(x_in[c], 16)
            for name in ("wb", "wc", "wd"):
                sp.dma_start(g.later[name][:, :], dram[name]).then_inc(g.later_in[name], 16)

        @block.gpsimd
        def _(pool):
            def copy(out, in_):
                zero = g.zero[:, 0:1]
                for _ in in_.shape[2:]:
                    zero = zero.unsqueeze(2)
                return nc.gpsimd.tensor_tensor(out, in_, zero.to_broadcast(list(in_.shape)), ALU.add)

            make_constants(nc, pool, g)
            for t in (v_diag, v_ab, v_cd):
                nc.gpsimd.memset(t[:, :, :], 0.0).then_inc(v_const, 1)
            pool.wait_ge(v_const, 3)
            for t in (v_diag, v_ab, v_cd):
                nc.gpsimd.memset(t[:, :, HD:HD + 1], 1.0).then_inc(v_const, 1)
            pool.wait_ge(v_const, 6)
            for n in range(NG):
                c, kv = divmod(n, KVH)
                pool.wait_ge(qkv_copied, 2 * TPC * (c + 1))
                if n:
                    pool.wait_ge(kb_done, first_kb[n - 1] + 3)
                copy(v_diag[:, :, 0:HD], vals[:, c, kv, 1:TPC, :]).then_inc(vd_staged, 1)
                if n:
                    pool.wait_ge(kb_done, first_kb[n])
                copy(v_cd[:, 1, 0:HD], vals[:, c, kv, 0, :]).then_inc(vcd_staged, 1)
                if c:
                    with pool.Fori(0, c) as q:
                        row = vals[:, bass.ds(q, 1), kv, :, :]
                        pool.wait_ge(kb_done, q * TPC + (first_kb[n] + 2))
                        copy(v_ab[:, :, 0:HD], row[:, 0, 0:2, :]).then_inc(vab_staged, 1)
                        pool.wait_ge(kb_done, q * TPC + (first_kb[n] + TPC))
                        copy(v_cd[:, :, 0:HD], row[:, 0, 2:4, :]).then_inc(vcd_staged, 1)

        @block.scalar
        def _(act):
            def copy(out, in_, scale=1.0):
                return nc.scalar.activation(out, in_, ACT.Copy, scale=scale)

            def copy_pair(p):
                act.wait_ge(xT_done, 2 * p + 2)
                if p:
                    act.wait_ge(qkv_done, 2 * p)
                copy(xnT[:, :, :, :].rearrange("p t k n -> p (t k n)"), bank_b[:, :]).then_inc(xT_copied, 2)
                act.wait_ge(xn_ready, 1)
                if p >= 2:
                    act.wait_ge(split_ready, 2 * p - 2)
                for t in range(2):
                    i = 2 * p + t
                    act.wait_ge(qkv_done, i + 1)
                    bank = (bank_a, bank_c)[t]
                    copy(pair_qkv[p % 2][t][:, :], bank[:, 0:QKW], rms[:, i:i + 1]).then_inc(qkv_copied, 1)
                    copy(vals[:, i // TPC, :, i % TPC, :], heads(bank[:, QKW:QKVW], KVH),
                         rms[:, i:i + 1]).then_inc(qkv_copied, 1)

            def lay_pair(p):
                for t in range(2):
                    i = 2 * p + t
                    t0 = (i % TPC) * P
                    for half in range(2):
                        act.wait_ge((qa_done, qb_done)[half], i + 1)
                        copy(qT[:, i // TPC, 8 * half:8 * half + 8, t0:t0 + P],
                             pair_banks[2 * t + half].bitcast(BF16).rearrange("p (h t) -> p h t", h=8)).then_inc(
                                 (qa_copied, qb_copied)[half], 1)
                act.wait_ge(kk_done, 2 * p + 2)
                c, j = divmod(2 * p, TPC)
                dst = kT[:, kcols(c, 0, 0):kcols(c + 1, 0, 0)].rearrange("p (h t) -> p h t", h=KVH)
                copy(dst[:, :, j * P:(j + 2) * P].rearrange("p h (t n) -> p t h n", t=2),
                     out_acc[:, :].bitcast(BF16).rearrange("p (t h n) -> p t h n", t=2, h=KVH)).then_inc(kk_copied, 2)

            copy_pair(0)
            for p in range(READY // 2):
                if p + 1 < READY // 2:
                    copy_pair(p + 1)
                lay_pair(p)
            for n in range(NG):
                c = n // KVH
                k0 = first_kb[n]
                for j in range(TPC):
                    for pr in range(2):
                        width = (j + 1) * P
                        act.wait_ge(scores_done, 2 * (k0 + j) + pr + 1)
                        if k0 + j >= 2:
                            act.wait_ge(kb_done, k0 + j - 1)
                        src = score[pr][:, :].rearrange("p (h q) -> p h q", h=2)[:, :, 0:width]
                        dst = probs[:, j % 2, pr, :].rearrange("p (h q) -> p h q", h=2)[:, :, 0:width]
                        nc.scalar.activation(dst, src, ACT.Exp, scale=SCORE_SCALE).then_inc(exp_done, 1)
                if c:
                    with act.Fori(0, c) as q:
                        for j in range(TPC):
                            for pr in range(2):
                                act.wait_ge(scores_done, q * (2 * TPC) + (2 * (k0 + TPC + j) + pr + 1))
                                if pr == 0:
                                    act.wait_ge(kb_done, q * TPC + (k0 + TPC + j - 1))
                                nc.scalar.activation(probs[:, j % 2, pr, :], score[pr][:, :], ACT.Exp,
                                                     scale=SCORE_SCALE).then_inc(exp_done, 1)

        @block.tensor
        def _(pe):
            mm, tr = nc.tensor.matmul, nc.tensor.transpose
            identf, identb = g.identf, g.identb

            pe.wait_ge(w_in, 16)
            for k in range(KD):
                last = mm(bank_a[:, k * P:(k + 1) * P], w("kv_downT")[0:LAT, k * P:(k + 1) * P],
                          w("kv_up")[0:LAT, :], start=True, stop=True)
            last.then_inc(w_prod, 1)

            def transpose_x(i):
                pe.wait_ge(xn_ready, i + 1)
                pe.wait_ge(g.ident_ready, 1)
                for k in range(KD):
                    last = tr(bank_b[:, k * P:(k + 1) * P], x[:, i, k * P:(k + 1) * P], identf[:, :])
                last.then_inc(xT_done, 1)

            def project_qkv(i):
                pe.wait_ge(xT_copied, i + 1)
                pe.wait_ge(w_ready, 4)
                for k in range(KD):
                    last = mm(bank_a[:, 0:QKVW], xnT[:, 0, k, :], wqkv[:, k, :], start=(k == 0), stop=(k == KD - 1))
                last.then_inc(qkv_done, 1)

            def transpose_heads(i, bank, src, h0, nh, done):
                for h in range(nh):
                    last = tr(bank.bitcast(BF16)[:, h * P:(h + 1) * P], src[:, (h0 + h) * P:(h0 + h + 1) * P],
                              identb[:, :])
                last.then_inc(done, 1)

            def transpose_qa(i):
                pe.wait_ge(split_ready, i + 1)
                transpose_heads(i, bank_a[:, :], b.qs, 0, 8, qa_done)

            def transpose_qb(i):
                if i >= LEAD + KVH:
                    pe.wait_ge(proj_added, i - (LEAD - 1) - KVH)
                transpose_heads(i, bank_b[:, :], b.qs, 8, 8, qb_done)

            def transpose_k(i):
                pe.wait_ge(qa_copied, i + 1)
                transpose_heads(i, bank_a[:, :], b.ks, 0, KVH, kk_done)

            def scores(n, pr, kcol, wait_unit, j=None):
                if wait_unit is not None:
                    pe.wait_ge(exp_done, wait_unit)
                c, kv = divmod(n, KVH)
                q0 = 0 if j is None else j * P
                for a in range(2):
                    dst = score[pr][:, a * CH:a * CH + CH - q0]
                    last = mm(dst, kcol, qT[:, c % 2, kv * GQ + 2 * pr + a, q0:CH], start=True, stop=j is None)
                    if j is not None:
                        last = mm(dst[:, 0:P], identb[:, :], g.causal[:, :], start=False, stop=True)
                last.then_inc(scores_done, 1)

            def diag_scores(n, s):
                k = first_kb[n] + s
                c, kv = divmod(n, KVH)
                if s == 0 and kv == 0:
                    pe.wait_ge(qb_copied, TPC * (c + 1))
                    pe.wait_ge(kk_copied, TPC * (c + 1))
                at = kcols(c, kv, TPC - 1 - s)
                for pr in range(2):
                    scores(n, pr, kT[:, at:at + P], 2 * k + pr - 1 if k else None, TPC - 1 - s)

            def weighted(rows, slot, q0, first=False, last=False):
                for h in range(GQ):
                    out = mm(out_acc[h * VW:(h + 1) * VW, q0:CH], rows,
                             probs[:, slot, h // 2, (h % 2) * CH:(h % 2) * CH + CH - q0],
                             start=first, stop=last, skip_group_check=True)
                out.then_inc(kb_done, 1)

            def transpose_out(n):
                pe.wait_ge(o_copied, n + 1)
                if n >= KVH:
                    pe.wait_ge(aT_copied, n - KVH + 1)
                for t in range(TPC):
                    last = tr(bank_c[:, t * P:(t + 1) * P], oT[:, t * P:(t + 1) * P], identf[:, :])
                last.then_inc(oT_done, 1)

            def transpose_attn(i):
                pe.wait_ge(o_normed, min(i + KVH, NG))
                if i > NT - TPC:
                    pe.wait_ge(aT_copied, i)
                for k in range(KD):
                    last = tr(bank_c[:, k * P:(k + 1) * P], attn[:, (i // TPC) % 2, i % TPC, k * P:(k + 1) * P],
                              identf[:, :])
                last.then_inc(aT_done, 1)

            def project_out(i):
                pe.wait_ge(aT_copied, i + 1)
                pe.wait_ge(qb_copied, min(i + KVH + LEAD, NT))
                if i:
                    pe.wait_ge(proj_added, i)
                for k in range(KD):
                    last = mm(bank_b[:, 0:D], attnT[:, k, :], w("wo", k), start=(k == 0), stop=(k == KD - 1))
                last.then_inc(proj_done, 1)

            def front_pair(p):
                if p:
                    pe.wait_ge(xT_copied, 2 * p)
                for t in range(2):
                    i = 2 * p + t
                    pe.wait_ge(xn_ready, i + 1)
                    for k in range(KD):
                        last = tr(bank_b[:, (t * KD + k) * P:(t * KD + k + 1) * P], x[:, i, k * P:(k + 1) * P], identf[:, :])
                last.then_inc(xT_done, 2)
                pe.wait_ge(xT_copied, 2 * p + 2)
                if p:
                    pe.wait_ge(qkv_copied, 4 * p)
                for t in range(2):
                    for k in range(KD):
                        last = mm((bank_a, bank_c)[t][:, 0:QKVW], xnT[:, t, k, :], wqkv[:, k, :], start=(k == 0), stop=(k == KD - 1))
                    last.then_inc(qkv_done, 1)

            def transpose_pair(p):
                for t in range(2):
                    i = 2 * p + t
                    pe.wait_ge(split_ready, i + 1)
                    if p:
                        pe.wait_ge((qa_copied, qb_copied)[0], i - 1)
                        pe.wait_ge((qa_copied, qb_copied)[1], i - 1)
                    transpose_heads(i, pair_banks[2 * t], tile_bufs[t].qs, 0, 8, qa_done)
                    transpose_heads(i, pair_banks[2 * t + 1], tile_bufs[t].qs, 8, 8, qb_done)
                if p:
                    pe.wait_ge(kk_copied, 2 * p)
                for t in range(2):
                    for h in range(KVH):
                        at = (t * KVH + h) * P
                        last = tr(out_acc[:, :].bitcast(BF16)[:, at:at + P], tile_bufs[t].ks[:, h * P:(h + 1) * P], identb[:, :])
                last.then_inc(kk_done, 2)

            pe.wait_ge(w_ready, 4)
            pe.wait_ge(g.ident_ready, 1)
            front_pair(0)
            for p in range(READY // 2):
                if p + 1 < READY // 2:
                    front_pair(p + 1)
                transpose_pair(p)
            for copied in (qa_copied, qb_copied, kk_copied):
                pe.wait_ge(copied, READY)
            diag_scores(0, 0)
            quads = 0
            for n in range(NG):
                c = n // KVH
                late, ahead = n + LEAD - 1, n + LEAD
                if READY <= late < NT:
                    transpose_qa(late)
                diag_scores(n, 1)
                if n:
                    transpose_out(n - 1)
                pe.wait_ge(vd_staged, n + 1)
                weighted(v_diag[:, 2, :], 0, 3 * P, first=True)
                if READY <= late < NT:
                    transpose_qb(late)
                diag_scores(n, 2)
                weighted(v_diag[:, 1, :], 1, 2 * P)
                if READY <= late < NT:
                    transpose_k(late)
                if READY <= ahead < NT:
                    pe.wait_ge(qb_copied, ahead)
                    transpose_x(ahead)
                diag_scores(n, 3)
                weighted(v_diag[:, 0, :], 0, P)
                if READY <= ahead < NT:
                    pe.wait_ge(kk_copied, ahead)
                    project_qkv(ahead)
                if c:
                    transpose_attn(n - KVH)
                    with pe.Fori(0, c) as q:
                        for j in range(TPC):
                            k = first_kb[n] + TPC + j
                            for pr in range(2):
                                scores(n, pr, kT[:, bass.ds(q * (KVH * CH) + kcols(0, n % KVH, j), P)],
                                       q * (2 * TPC) + (2 * k + pr - 1))
                            if j == 0:
                                pe.wait_ge(vcd_staged, q + (n + quads + 1))
                            if j == 1:
                                pe.wait_ge(vab_staged, q + (quads + 1))
                            if j == 3:
                                pe.wait_ge(vcd_staged, q + (n + quads + 2))
                            rows = (v_cd[:, 1, :], v_ab[:, 0, :], v_ab[:, 1, :], v_cd[:, 0, :])[j]
                            weighted(rows, (j + 1) % 2, 0)
                    quads += c
                    project_out(n - KVH)
                if n + 1 < NG:
                    diag_scores(n + 1, 0)
                else:
                    pe.wait_ge(exp_done, 2 * first_kb[NG])
                pe.wait_ge(vcd_staged, n + quads + 1)
                weighted(v_cd[:, 1, :], 1, 0, last=True)
            transpose_out(NG - 1)
            for i in range(NT - TPC, NT):
                transpose_attn(i)
                project_out(i)

        @block.vector
        def _(dve):
            chain, chain1 = Chain(dve, dve_seq), Chain(dve, dve_seq1)
            v = nc.vector

            def sums(c0, c1):
                for c in range(c0, c1):
                    dve.wait_ge(x_in[c], 16)
                    for i in range(c * TPC, (c + 1) * TPC):
                        chain.do(v.bn_stats(bn[:, i, :], x[:, i, :]))

            def stats(c0, c1):
                ts = slice(c0 * TPC, c1 * TPC)
                chain.sync()
                for i in range(c0 * TPC, c1 * TPC):
                    chain.do(v.bn_aggr(mv[:, i, :], bn[:, i, :]))
                chain.sync()
                chain.link(v.tensor_scalar(var[:, ts], mv[:, ts, 1], LN_EPS, None, ALU.add))
                rsqrt(nc, (chain, rln[:, ts], var[:, ts], st1[:, ts], st2[:, ts]))
                chain.link(v.tensor_tensor(var[:, ts], rln[:, ts], rln[:, ts], ALU.mult))
                chain.link(v.tensor_tensor(var[:, ts], var[:, ts], mv[:, ts, 1], ALU.mult))
                chain.link(v.tensor_scalar(var[:, ts], var[:, ts], RMS_EPS, None, ALU.add))
                rsqrt(nc, (chain, rms[:, ts], var[:, ts], st1[:, ts], st2[:, ts]))

            def normalise(i):
                v.tensor_scalar(x[:, i, :], x[:, i, :], mv[:, i, 0:1], rln[:, i:i + 1],
                                ALU.subtract, ALU.mult).then_inc(xn_ready, 1)

            def copy_xT(i):
                dve.wait_ge(xT_done, i + 1)
                if i:
                    dve.wait_ge(qkv_done, i)
                v.tensor_copy(xnT[:, 0, :, :], bank_b[:, 0:D].rearrange("p (k t) -> p k t", k=KD)).then_inc(xT_copied, 1)

            def copy_qkv(i):
                dve.wait_ge(qkv_done, i + 1)
                v.tensor_scalar(b.qkv[:, :], bank_a[:, 0:QKW], rms[:, i:i + 1], None, ALU.mult).then_inc(qkv_copied, 1)
                v.tensor_scalar(vals[:, i // TPC, :, i % TPC, :], heads(bank_a[:, QKW:QKVW], KVH), rms[:, i:i + 1],
                                None, ALU.mult).then_inc(qkv_copied, 1)

            def split(i):
                dve.wait_ge(qkv_copied, 2 * (i + 1))
                dve.wait_ge(kk_done, i)
                rope_norm_split(nc, [(chain, b, b.qkv, w("cos", i), w("sin", i))], split_ready)

            def split_pair(p):
                dve.wait_ge(qkv_copied, 4 * p + 4)
                if p:
                    dve.wait_ge(kk_done, 2 * p)
                rope_norm_split(nc, [((chain, chain1)[t], tile_bufs[t], pair_qkv[p % 2][t], w("cos", 2 * p + t), w("sin", 2 * p + t)) for t in range(2)],
                                split_ready)
                for c in (chain, chain1):
                    c.sync()

            def lay_q(i, bank, h0, done, copied):
                dve.wait_ge(done, i + 1)
                t0 = (i % TPC) * P
                v.tensor_copy(qT[:, (i // TPC) % 2, h0:h0 + 8, t0:t0 + P],
                              bank[:, :].bitcast(BF16)[:, 0:8 * P].rearrange("p (h t) -> p h t", h=8)).then_inc(copied, 1)

            def lay_k(i):
                dve.wait_ge(kk_done, i + 1)
                c, j = divmod(i, TPC)
                dst = kT[:, kcols(c, 0, 0):kcols(c + 1, 0, 0)].rearrange("p (h t) -> p h t", h=KVH)
                v.tensor_copy(dst[:, :, j * P:(j + 1) * P],
                              bank_a[:, :].bitcast(BF16)[:, 0:KVH * P].rearrange("p (h t) -> p h t", h=KVH)).then_inc(kk_copied, 1)

            def copy_out(n):
                dve.wait_ge(kb_done, first_kb[n + 1])
                if n:
                    dve.wait_ge(oT_done, n)
                v.tensor_copy(oT[:, :], out_acc[:, :]).then_inc(o_copied, 1)

            def normalise_out(n):
                c, kv = divmod(n, KVH)
                dve.wait_ge(oT_done, n + 1)
                if c >= 2:
                    dve.wait_ge(aT_done, TPC * (c - 1))
                o = bank_c[:, :].rearrange("p (m e) -> p m e", e=VW)
                chain.link(v.reciprocal(den[:, :], o[:, :, HD]))
                dst = attn[:, c % 2, :, kv * GQ * HD:(kv + 1) * GQ * HD]
                v.tensor_tensor(dst.rearrange("p t (h e) -> p t h e", h=GQ),
                                o[:, :, 0:HD].rearrange("p (t h) e -> p t h e", t=TPC),
                                den[:, :].rearrange("p (t h) -> p t h", t=TPC).unsqueeze(3).to_broadcast([P, TPC, GQ, HD]),
                                ALU.mult).then_inc(o_normed, 1)

            def copy_aT(i):
                dve.wait_ge(aT_done, i + 1)
                if i:
                    dve.wait_ge(proj_done, i)
                v.tensor_copy(attnT[:, :, :], bank_c[:, 0:D].rearrange("p (k t) -> p k t", k=KD)).then_inc(aT_copied, 1)

            def add_proj(i):
                dve.wait_ge(proj_done, i + 1)
                v.tensor_tensor(x[:, i, :], x[:, i, :], bank_b[:, 0:D], ALU.add).then_inc(proj_added, 1)

            dve.wait_ge(w_in, 16)
            dve.wait_ge(w_prod, 1)
            for k in range(KD):
                n1 = w("norm1")[:, k:k + 1]
                v.tensor_scalar(wqkv[:, k, 0:D], w("wq", k), n1, None, ALU.mult).then_inc(w_ready, 1)
                v.tensor_scalar(wqkv[:, k, D:QKVW], bank_a[:, k * P:(k + 1) * P], n1, None, ALU.mult).then_inc(w_ready, 1)
            sums(0, 2)
            stats(0, 2)
            for i in range(READY):
                normalise(i)
            for p in range(READY // 2):
                split_pair(p)
            for n in range(NG):
                late, ahead = n + LEAD - 1, n + LEAD
                if n:
                    copy_out(n - 1)
                if READY <= late < NT:
                    lay_q(late, bank_a, 0, qa_done, qa_copied)
                if n:
                    normalise_out(n - 1)
                if READY <= late < NT:
                    lay_q(late, bank_b, 8, qb_done, qb_copied)
                    lay_k(late)
                if READY <= ahead < NT:
                    copy_xT(ahead)
                    copy_qkv(ahead)
                if n >= KVH:
                    copy_aT(n - KVH)
                if n < 2:
                    sums(2 + 3 * n, 5 + 3 * n)
                if n == 2:
                    stats(2, NCH)
                if READY <= ahead < NT:
                    split(ahead)
                if READY <= ahead + 1 < NT:
                    normalise(ahead + 1)
                if n >= KVH:
                    add_proj(n - KVH)
            copy_out(NG - 1)
            normalise_out(NG - 1)
            for i in range(NT - TPC, NT):
                copy_aT(i)
                add_proj(i)


def make_constants(nc, pool, g):
    gp = nc.gpsimd
    steps = [0]

    def link(ins):
        steps[0] += 1
        ins.then_inc(g.const_seq, 1)
        pool.wait_ge(g.const_seq, steps[0])

    link(gp.memset(g.zero[:, :], 0.0))
    link(gp.memset(g.identf[:, :], 0.0))
    link(gp.affine_select(out=g.identf[:, :], in_=g.identf[:, :], compare_op=ALU.not_equal, fill=1.0, base=0,
                          pattern=[[-1, P]], channel_multiplier=1))
    link(gp.tensor_copy(g.identb[:, :], g.identf[:, :]))
    link(gp.memset(g.causal[:, :], 0.0))
    gp.affine_select(out=g.causal[:, :], in_=g.causal[:, :], compare_op=ALU.is_ge, fill=NEG, base=0,
                     pattern=[[1, P]], channel_multiplier=-1).then_inc(g.ident_ready, 1)
    pool.wait_ge(g.ident_ready, 1)


def pack(columns):
    at, out = 0, {}
    for name, n in columns:
        out[name] = (at, n)
        at += n
    return out, at


PACKS = {
    "wa": pack([("kv_downT", D), ("kv_up", 2 * KVH * HD), ("wq", KD * D), ("norm1", KD), ("wo", KD * D),
                ("cos", NT * HD), ("sin", NT * HD)]),
    "wb": pack([("wqkv", KD * QKVW), ("norm2", KD), ("wo", KD * D), ("cos", NT * HD), ("sin", NT * HD)]),
    "wc": pack([("wq", KD * D), ("routersT", KD * D), ("valuesT", KD * D), ("woutT", KD * D)]),
    "wd": pack([("bias", D), ("ln_g", KD), ("ln_b", KD), ("po_b", D), ("in_WT", NL * 2 * DI), ("rms_w", NL),
                ("conv_w", NL * HALVES * TAPS), ("conv_b", NL * HALVES), ("dt_b", NL * HALVES), ("Dp", NL * HALVES),
                ("A_log", NL * HALVES * NS), ("xp_WT", NL * HALVES * XPW), ("dt_WT", NL * DI), ("mo_WT", NL * HALVES * P),
                ("po_WT", KD * D)]),
}
PIECE = {"wq": D, "wo": D, "wqkv": QKVW, "cos": HD, "sin": HD, "routersT": D, "valuesT": D, "woutT": D,
         "in_WT": 2 * DI, "conv_w": HALVES * TAPS, "conv_b": HALVES, "dt_b": HALVES, "Dp": HALVES, "xp_WT": XPW,
         "dt_WT": DI, "mo_WT": P, "po_WT": D}


def piece(tile, table):
    def w(name, k=None):
        at, n = table[name]
        if k is not None:
            n = PIECE[name]
            at += k * n
        return tile[:, at:at + n]
    return w


def build(nc, dram, out, upto=9):
    with ExitStack() as ctx:
        early = ctx.enter_context(ExitStack())

        def sb(stack, name, shape, dt=F32):
            return stack.enter_context(nc.sbuf_tensor(name, shape, dt))

        def sem(name):
            return ctx.enter_context(nc.semaphore(name))

        g = Tiles()
        g.x = sb(ctx, "x", [P, NT, D])
        g.identf, g.identb = sb(ctx, "identf", [P, P]), sb(ctx, "identb", [P, P], BF16)
        g.zero = sb(ctx, "zero", [P, 1])
        g.bn = sb(ctx, "bn", [P, NT, 6])
        g.causal = sb(ctx, "causal", [P, P], BF16)
        g.w_gate, g.w_out = sb(ctx, "w_gate", [P, KD, D]), sb(ctx, "w_out", [P, KD, D])
        tiles = {name: sb(ctx if name == "wd" else early, name, [P, PACKS[name][1]]) for name in ("wd", "wa", "wb", "wc")}
        g.wa, g.later = tiles["wa"], tiles
        g.later_in = {name: sem(f"{name}_in") for name in ("wb", "wc", "wd")}
        g.wa_col = piece(g.wa, PACKS["wa"][0])
        g.tree_sems = {name: sem("tree_" + name) for name in (
            "dve_seq", "w_prod", "w_ready", "xs_ready", "biased", "xT_done", "xT_copied", "logits_done", "gates_ready",
            "leaf_ready", "leafT_done", "leafT_copied", "out_done", "added")}
        g.xr_in, g.stored = sem("xr_in"), sem("stored")
        g.const_seq, g.ident_ready = sem("const_seq"), sem("ident_ready")
        g.dram, g.out = dram, out

        global_attention(nc, g, dram)
        local_attention(nc, g, dram)
        tree_ffn(nc, g, "fa", True, False)
        early.close()
        with ExitStack() as late:
            g.hT = sb(late, "hT", [P, S])
            mamba_norms(nc, g)
            mamba_layers(nc, g)
            mamba_out(nc, g)
        tree_ffn(nc, g, "fb", False, True)


def rope_tables(base):
    inv = (np.float32(1.0) / np.float32(base) ** (np.arange(0, HD, 2, dtype=np.float32) / np.float32(HD))).astype(np.float32)
    ang = np.arange(S, dtype=np.float32)[:, None] * inv[None, :]
    cos, sin = np.cos(ang).astype(np.float32), np.sin(ang).astype(np.float32)
    cos2 = np.repeat(cos, 2, axis=1)
    sin2 = np.stack([-sin, sin], axis=2).reshape(S, HD)
    return [np.ascontiguousarray(t.reshape(NT, P, HD).transpose(1, 0, 2).reshape(P, NT * HD)) for t in (cos2, sin2)]


def lay_out(inputs):
    a = {k: np.asarray(v) for k, v in inputs.items()}

    def rows(m):
        return m.reshape(-1, P, m.shape[1]).transpose(1, 0, 2).reshape(P, -1)

    def pad(m):
        return np.concatenate([m, np.zeros((P - m.shape[0], m.shape[1]), m.dtype)], axis=0)

    def cols(v):
        return v.reshape(-1, P).T

    def everywhere(v):
        return np.broadcast_to(v[None, :], (P, v.shape[0]))

    ga, la, ff, mb = "L0_attn_a_g_", "L0_attn_a_l_", "L0_ffn_", "L0_attn_b_"
    halves = rows

    def layers(f):
        return np.concatenate([f(l) for l in range(NL)], axis=1)

    def xp_rows(l):
        m = a[mb + "xp_W"][l].T
        bc = m[:, DTR:]
        return rows(np.concatenate([bc, bc, bc, m[:, 0:DTR]], axis=1))

    def dt_rows(l):
        m = np.zeros((P, DI), np.float32)
        m[XPW - DTR:XPW] = a[mb + "dt_W"][l].T
        return m

    cg, sg = rope_tables(1000000.0)
    cl, sl = rope_tables(10000.0)
    parts = {
        "wa": dict(kv_downT=pad(a[ga + "kv_down"].T), kv_up=pad(np.concatenate([a[ga + "k_up"], a[ga + "v_up"]], axis=1)),
                   wq=rows(a[ga + "wq"]), norm1=cols(a["L0_attn_a_norm1_w"]), wo=rows(a[ga + "wo"]), cos=cg, sin=sg),
        "wb": dict(wqkv=rows(np.concatenate([a[la + "wq"], a[la + "wk"], a[la + "wv"]], axis=1)),
                   norm2=cols(a["L0_attn_a_norm2_w"]), wo=rows(a[la + "wo"]), cos=cl, sin=sl),
        "wc": dict(wq=rows(a[ff + "Wq"]),
                   routersT=rows(np.concatenate([a[ff + "routers"].T, np.zeros((D, 1), np.float32)], axis=1)),
                   valuesT=rows(a[ff + "leaf_values"].T), woutT=rows(a[ff + "Wout_w"].T)),
        "wd": dict(bias=everywhere(a[ff + "Wout_b"]), ln_g=cols(a[mb + "ln_g"]), ln_b=cols(a[mb + "ln_b"]),
                   po_b=everywhere(a[mb + "po_b"]), in_WT=layers(lambda l: a[mb + "in_W"][l].T),
                   rms_w=a[mb + "rms_w"].T, conv_w=layers(lambda l: halves(a[mb + "conv_w"][l, :, 0, :])),
                   conv_b=layers(lambda l: cols(a[mb + "conv_b"][l])), dt_b=layers(lambda l: cols(a[mb + "dt_b"][l])),
                   Dp=layers(lambda l: cols(a[mb + "Dp"][l])), A_log=layers(lambda l: halves(a[mb + "A_log"][l])),
                   xp_WT=layers(xp_rows), dt_WT=layers(dt_rows), mo_WT=layers(lambda l: rows(a[mb + "mo_W"][l].T)),
                   po_WT=rows(a[mb + "po_W"].T)),
    }
    arrays = {"x": np.ascontiguousarray(a["L0_attn_a_hidden"].reshape(NT, P, D).transpose(1, 0, 2))}
    for name, (table, width) in PACKS.items():
        whole = np.concatenate([parts[name][n] for n in table], axis=1)
        assert whole.shape == (P, width), (name, whole.shape, width)
        arrays[name] = np.ascontiguousarray(whole)
    return arrays


def local_attention(nc, g, dram):
    ctx = ExitStack()
    with ctx:
        def sb(name, shape, dt=F32):
            return ctx.enter_context(nc.sbuf_tensor("la_" + name, shape, dt))

        def sem(name):
            return ctx.enter_context(nc.semaphore("la_" + name))

        x, w = g.x, piece(g.later["wb"], PACKS["wb"][0])
        HALF = H // 2
        PW = WIN
        UNIT = 2 * CH + 2 * TPC * PW
        LAYS = 2 * TPC + 2
        wqkv = sb("wqkv", [P, KD, QKVW])
        xs = sb("xs", [P, TPC, D])
        xT = sb("xT", [P, TPC, KD, P])
        xr = sb("xr", [P, TPC, D])
        qk = sb("qk", [P, TPC * QKW])
        t1, t2 = sb("t1", [P, TPC * QKW]), sb("t2", [P, TPC * QKW])
        ss, rs, n1, n2 = (sb(n, [P, TPC * NQK]) for n in ("ss", "rs", "n1", "n2"))
        qn, kn = sb("qn", [P, TPC * H, HD]), sb("kn", [P, TPC * KVH, HD])
        qs, ks = sb("qs", [P, TPC * H, TERMS, HD], BF16), sb("ks", [P, TPC * KVH, TERMS, HD], BF16)
        qT = sb("qT", [P, H, CH], BF16)
        kT = sb("kT", [P, KVH, P + CH], BF16)
        vnew = sb("vnew", [P, TPC, KVH, HD])
        vals = sb("vals", [P, TPC + 1, KVH, VW])
        probs = sb("probs", [P, 2, 2, UNIT])
        oT = sb("oT", [P, CH])
        den = sb("den", [P, H])
        attn = sb("attn", [P, TPC, D])
        attnT = sb("attnT", [P, TPC, KD, P])
        bn, mv = sb("bn", [P, NT, 6]), sb("mv", [P, NT, 2])
        var, rms, s1, s2 = (sb(n, [P, NT]) for n in ("var", "rms", "s1", "s2"))
        band = sb("band", [P, P], BF16)
        before = sb("before", [P, PW], BF16)

        score = [ctx.enter_context(nc.psum_tensor(f"la_score{i}", [P, UNIT], F32)) for i in range(2)]
        out_acc = ctx.enter_context(nc.psum_tensor("la_out_acc", [P, CH], F32))
        bank_p = ctx.enter_context(nc.psum_tensor("la_bank_p", [P, 512], F32))
        sbank = [score[i // 3][:, (i % 3) * 512:(i % 3 + 1) * 512] for i in range(6)]

        dve_seq, pool_seq, masks_ready, w_ready = sem("dve_seq"), sem("pool_seq"), sem("masks_ready"), sem("w_ready")
        xr_in, xr_added, xs_ready = g.xr_in, sem("xr_added"), sem("xs_ready")
        xT_done, xT_copied = sem("xT_done"), sem("xT_copied")
        qkv_done, qkv_copied, split_ready = sem("qkv_done"), sem("qkv_copied"), sem("split_ready")
        lay_done, lay_dve, lay_act = sem("lay_done"), sem("lay_dve"), sem("lay_act")
        k_moved, vals_ready = sem("k_moved"), sem("vals_ready")
        scores_done, exp_done, pv_done = sem("scores_done"), sem("exp_done"), sem("pv_done")
        o_copied, oT_done, o_normed = sem("o_copied"), sem("oT_done"), sem("o_normed")
        aT_done, aT_copied, proj_done, added = sem("aT_done"), sem("aT_copied"), sem("proj_done"), sem("added")

        def chunk(c):
            return x[:, bass.ds(c * TPC, TPC), :]

        def turns(eng, body):
            body(0, True, True)
            with eng.Fori(1, NCH - 2) as c:
                body(c, True, True)
            body(NCH - 2, True, False)
            body(NCH - 1, False, False)

        def qkv_bank(t):
            return sbank[2 + t]

        def lay_views(n):
            bank = sbank[n % 6].bitcast(BF16)
            if n < 2 * TPC:
                t, half = divmod(n, 2)
                return (qT[:, half * HALF:(half + 1) * HALF, t * P:(t + 1) * P],
                        bank.rearrange("p (h t) -> p h t", h=HALF))
            t = 2 * (n - 2 * TPC)
            dst = kT[:, :, P + t * P:P + (t + 2) * P].rearrange("p h (t n) -> p t h n", t=2)
            return dst, bank.rearrange("p (t h n) -> p t h n", t=2, h=KVH)

        block = ctx.enter_context(nc.Block())

        @block.sync
        def _(sp):
            sp.dma_start(xr[:, :, :], dram["x"][:, 0:TPC, :]).then_inc(xr_in, 16)
            with sp.Fori(1, NCH) as c:
                sp.wait_ge(xr_added, c)
                sp.dma_start(xr[:, :, :], dram["x"][:, bass.ds(c * TPC, TPC), :]).then_inc(xr_in, 16)

        @block.gpsimd
        def _(pool):
            def copy(out, in_):
                zero = g.zero[:, 0:1]
                for _ in in_.shape[2:]:
                    zero = zero.unsqueeze(2)
                return nc.gpsimd.tensor_tensor(out, in_, zero.to_broadcast(list(in_.shape)), ALU.add)

            gp = nc.gpsimd
            chain = Chain(pool, pool_seq)
            for t in (band, before):
                chain.do(gp.memset(t[:, :], 0.0))
            chain.do(gp.memset(kT[:, :, 0:P], 0.0))
            chain.do(gp.memset(vals[:, :, :, :], 0.0))
            chain.sync()
            chain.link(gp.affine_select(out=band[:, :], in_=band[:, :], compare_op=ALU.is_ge, fill=NEG, base=0,
                                        pattern=[[1, P]], channel_multiplier=-1))
            gp.affine_select(out=band[:, :], in_=band[:, :], compare_op=ALU.is_gt, fill=NEG, base=WIN,
                             pattern=[[-1, P]], channel_multiplier=1).then_inc(masks_ready, 1)
            gp.affine_select(out=before[:, :], in_=before[:, :], compare_op=ALU.is_gt, fill=NEG, base=WIN - P,
                             pattern=[[-1, PW]], channel_multiplier=1).then_inc(masks_ready, 1)
            chain.link(gp.memset(vals[:, 1:TPC + 1, :, HD:HD + 1], 1.0))

            def new_values(c):
                pool.wait_ge(qkv_copied, c * (2 * TPC) + 2 * TPC)
                copy(vals[:, 1:TPC + 1, :, 0:HD], vnew[:, :, :, :]).then_inc(vals_ready, 1)

            def add_input(c):
                pool.wait_ge(xr_in, c * 16 + 16)
                pool.wait_ge(xs_ready, c + 1)
                gp.tensor_tensor(chunk(c), chunk(c), xr[:, :, :], ALU.add).then_inc(xr_added, 1)

            def turn(c, ahead, far):
                add_input(c)
                if ahead:
                    pool.wait_ge(scores_done, c * 8 + 8)
                    copy(kT[:, :, 0:P], kT[:, :, CH:P + CH]).then_inc(k_moved, 1)
                    pool.wait_ge(pv_done, c * KVH + KVH)
                    chain.link(copy(vals[:, 0, :, 0:HD + 1], vals[:, TPC, :, 0:HD + 1]))
                    new_values(c + 1)
                    chain.restart()

            new_values(0)
            chain.restart()
            turns(pool, turn)

        @block.scalar
        def _(act):
            def copy(out, in_, scale=1.0):
                return nc.scalar.activation(out, in_, ACT.Copy, scale=scale)

            def copy_xT(c):
                for p in range(2):
                    act.wait_ge(xT_done, c * 2 + (p + 1))
                    if p == 0:
                        act.wait_ge(qkv_done, c * TPC)
                    copy(xT[:, 2 * p:2 * p + 2, :, :].rearrange("p t k n -> p (t k n)"), sbank[p]).then_inc(xT_copied, 1)

            def copy_qkv(c):
                if not isinstance(c, int) or c:
                    act.wait_ge(split_ready, c * 2 - 1)
                act.wait_ge(vals_ready, c)
                for t in range(TPC):
                    act.wait_ge(qkv_done, c * TPC + (t + 1))
                    bank = qkv_bank(t)
                    copy(qk[:, t * QKW:(t + 1) * QKW], bank[:, 0:QKW]).then_inc(qkv_copied, 1)
                    copy(vnew[:, t, :, :], heads(bank[:, QKW:QKVW], KVH)).then_inc(qkv_copied, 1)

            def lay(c):
                for n in range(1, LAYS, 2):
                    act.wait_ge(lay_done, c * LAYS + (n + 1))
                    if n == LAYS - 1:
                        act.wait_ge(k_moved, c)
                    dst, src = lay_views(n)
                    copy(dst, src).then_inc(lay_act, 1)

            def turn(c, ahead, far):
                for kv in range(KVH):
                    for pr in range(2):
                        act.wait_ge(scores_done, c * 8 + (2 * kv + pr + 1))
                        nc.scalar.activation(probs[:, kv % 2, pr, :], score[pr][:, :], ACT.Exp,
                                             scale=SCORE_SCALE).then_inc(exp_done, 1)
                    if kv:
                        copy_out(c, kv - 1)
                if far:
                    copy_xT(c + 2)
                copy_out(c, KVH - 1)
                if far:
                    copy_qkv(c + 2)
                if ahead:
                    lay(c + 1)
                for p in range(2):
                    act.wait_ge(aT_done, c * 2 + (p + 1))
                    if p == 0:
                        act.wait_ge(proj_done, c * 2)
                    copy(attnT[:, 2 * p:2 * p + 2, :, :].rearrange("p t k n -> p (t k n)"),
                         (out_acc, bank_p)[p][:, :]).then_inc(aT_copied, 1)

            def copy_out(c, kv):
                act.wait_ge(pv_done, c * KVH + (kv + 1))
                act.wait_ge(oT_done, c * KVH + kv)
                copy(oT[:, :], out_acc[:, :]).then_inc(o_copied, 1)

            copy_xT(0)
            copy_qkv(0)
            copy_xT(1)
            copy_qkv(1)
            lay(0)
            turns(act, turn)

        @block.tensor
        def _(pe):
            mm, tr = nc.tensor.matmul, nc.tensor.transpose
            identf, identb = g.identf, g.identb

            def transpose_x(c):
                pe.wait_ge(xs_ready, c + 1)
                for p in range(2):
                    for t in range(2 * p, 2 * p + 2):
                        for k in range(KD):
                            at = ((t % 2) * KD + k) * P
                            last = tr(sbank[p][:, at:at + P], xs[:, t, k * P:(k + 1) * P], identf[:, :])
                    last.then_inc(xT_done, 1)

            def project(c):
                for t in range(TPC):
                    if t % 2 == 0:
                        pe.wait_ge(xT_copied, c * 2 + (t // 2 + 1))
                    for k in range(KD):
                        last = mm(qkv_bank(t)[:, 0:QKVW], xT[:, t, k, :], wqkv[:, k, :], start=(k == 0), stop=(k == KD - 1))
                    last.then_inc(qkv_done, 1)

            def transpose_qk(c, ahead):
                pe.wait_ge(split_ready, c * 2 + 2)
                for n in range(LAYS):
                    if ahead and 2 <= n < 6:
                        pe.wait_ge(qkv_copied, c * (2 * TPC) + (2 * TPC + 2 * (n - 1)))
                    if n >= 6:
                        pe.wait_ge((lay_dve, lay_act)[n % 2], c * (LAYS // 2) + (n - 6) // 2 + 1)
                    bank = sbank[n % 6].bitcast(BF16)
                    for m in range(HALF):
                        if n < 2 * TPC:
                            src = qs[:, (n // 2) * H + (n % 2) * HALF + m, :, :]
                        else:
                            src = ks[:, (n - 2 * TPC) * HALF + m, :, :]
                        last = tr(bank[:, m * P:(m + 1) * P], src.rearrange("p r e -> p (r e)"), identb[:, :])
                    last.then_inc(lay_done, 1)

            def scores(c, kv, pr):
                u = 2 * kv + pr
                if kv:
                    pe.wait_ge(exp_done, c * 8 + (u - 1))
                s = score[pr]
                for a in range(2):
                    mm(s[:, a * CH:(a + 1) * CH], identb[:, :], band[:, :].unsqueeze(1).to_broadcast([P, TPC, P]),
                       start=True, stop=False, skip_group_check=True)
                mm(s[:, 2 * CH:UNIT], identb[:, :], before[:, :].unsqueeze(1).to_broadcast([P, 2 * TPC, PW]),
                   start=True, stop=False, skip_group_check=True)
                for j in range(TPC):
                    for a in range(2):
                        h = kv * GQ + 2 * pr + a
                        mm(s[:, a * CH + j * P:a * CH + (j + 1) * P], kT[:, kv, (j + 1) * P:(j + 2) * P],
                           qT[:, h, j * P:(j + 1) * P], start=False, stop=True, skip_group_check=True)
                    for a in range(2):
                        h = kv * GQ + 2 * pr + a
                        at = 2 * CH + (a * TPC + j) * PW
                        last = mm(s[:, at:at + PW], kT[:, kv, j * P:(j + 1) * P],
                                  qT[:, h, j * P:j * P + PW], start=False, stop=True, skip_group_check=True)
                last.then_inc(scores_done, 1)

            def weighted(c, kv):
                pe.wait_ge(exp_done, c * 8 + (2 * kv + 2))
                if kv:
                    pe.wait_ge(o_copied, c * KVH + kv)
                for j in range(TPC):
                    for own in (True, False):
                        for h in range(GQ):
                            a = h % 2
                            at, n = (a * CH + j * P, P) if own else (2 * CH + (a * TPC + j) * PW, PW)
                            last = mm(out_acc[h * VW:(h + 1) * VW, j * P:j * P + n], vals[:, j + own, kv, :],
                                      probs[:, kv % 2, h // 2, at:at + n], start=(j == 0 and own), stop=(j == TPC - 1 and not own),
                                      skip_group_check=True)
                last.then_inc(pv_done, 1)

            def transpose_out(c, kv):
                pe.wait_ge(o_copied, c * KVH + (kv + 1))
                if kv:
                    pe.wait_ge(o_normed, c * KVH + kv)
                for t in range(TPC):
                    last = tr(bank_p[:, t * P:(t + 1) * P], oT[:, t * P:(t + 1) * P], identf[:, :])
                last.then_inc(oT_done, 1)

            def first_scores(c):
                pe.wait_ge(lay_dve, c * (LAYS // 2) + LAYS // 2)
                pe.wait_ge(lay_act, c * (LAYS // 2) + LAYS // 2)
                scores(c, 0, 0)

            def project_out(c, ahead):
                pe.wait_ge(o_normed, c * KVH + KVH)
                for p in range(2):
                    for t in range(2 * p, 2 * p + 2):
                        for k in range(KD):
                            at = ((t % 2) * KD + k) * P
                            last = tr((out_acc, bank_p)[p][:, at:at + P], attn[:, t, k * P:(k + 1) * P], identf[:, :])
                    last.then_inc(aT_done, 1)
                if ahead:
                    first_scores(c + 1)
                for p in range(2):
                    pe.wait_ge(aT_copied, c * 2 + (p + 1))
                    for t in range(2 * p, 2 * p + 2):
                        for k in range(KD):
                            last = mm((out_acc, bank_p)[p][:, (t % 2) * D:(t % 2 + 1) * D], attnT[:, t, k, :], w("wo", k),
                                      start=(k == 0), stop=(k == KD - 1))
                    last.then_inc(proj_done, 1)

            def turn(c, ahead, far):
                scores(c, 0, 1)
                pe.wait_ge(vals_ready, c + 1)
                pe.wait_ge(added, c * 2)
                for kv in range(1, KVH):
                    scores(c, kv, 0)
                    scores(c, kv, 1)
                    if kv >= 2:
                        transpose_out(c, kv - 2)
                    weighted(c, kv - 1)
                if far:
                    pe.wait_ge(exp_done, c * 8 + 7)
                    transpose_x(c + 2)
                transpose_out(c, KVH - 2)
                weighted(c, KVH - 1)
                if far:
                    project(c + 2)
                transpose_out(c, KVH - 1)
                if ahead:
                    transpose_qk(c + 1, far)
                project_out(c, ahead)

            pe.wait_ge(w_ready, KD)
            pe.wait_ge(masks_ready, 2)
            transpose_x(0)
            project(0)
            transpose_x(1)
            pe.wait_ge(qkv_copied, 2 * TPC)
            project(1)
            transpose_qk(0, True)
            first_scores(0)
            turns(pe, turn)

        @block.vector
        def _(dve):
            v = nc.vector
            chain = Chain(dve, dve_seq)

            def stats(c0, c1):
                ts = slice(c0 * TPC, c1 * TPC)
                for t in range(c0 * TPC, c1 * TPC):
                    chain.do(v.bn_stats(bn[:, t, :], x[:, t, :]))
                chain.sync()
                for t in range(c0 * TPC, c1 * TPC):
                    chain.do(v.bn_aggr(mv[:, t, :], bn[:, t, :]))
                chain.sync()
                chain.link(v.tensor_tensor(var[:, ts], mv[:, ts, 0], mv[:, ts, 0], ALU.mult))
                chain.link(v.scalar_tensor_tensor(var[:, ts], var[:, ts], RMS_EPS, mv[:, ts, 1], ALU.add, ALU.add))
                rsqrt(nc, (chain, rms[:, ts], var[:, ts], s1[:, ts], s2[:, ts]))

            def scale_x(c):
                src = chunk(c)
                dve.wait_ge(xT_done, c * 2)
                for t in range(TPC):
                    last = v.tensor_scalar(xs[:, t, :], src[:, t, :], rms[:, bass.ds(c * TPC + t, 1)], None, ALU.mult)
                    if t < TPC - 1:
                        chain.do(last)
                chain.sync()
                last.then_inc(xs_ready, 1)

            def rope(c):
                dve.wait_ge(qkv_copied, c * (2 * TPC) + 2 * TPC)
                shape = [P, TPC, NQK, HD // 2]
                cos = w("cos")[:, bass.ds(c * (TPC * HD), TPC * HD)].rearrange("p (t e) -> p t e", t=TPC)
                sin = w("sin")[:, bass.ds(c * (TPC * HD), TPC * HD)].rearrange("p (t e) -> p t e", t=TPC)
                as4 = lambda a: a[:, :].rearrange("p (t h e) -> p t h e", t=TPC, h=NQK)
                chain.do(v.tensor_tensor(as4(t1), as4(qk), cos.unsqueeze(2).to_broadcast([P, TPC, NQK, HD]), ALU.mult))
                for e in range(2):
                    chain.do(v.tensor_tensor(as4(t2)[:, :, :, e::2], as4(qk)[:, :, :, 1 - e::2],
                                             sin[:, :, e::2].unsqueeze(2).to_broadcast(shape), ALU.mult))
                chain.sync()
                v.tensor_tensor(t1[:, :], t1[:, :], t2[:, :], ALU.add).then_inc(split_ready, 1)

            def norm(c):
                dve.wait_ge(split_ready, c * 2 + 1)
                chain.link(v.tensor_tensor(t2[:, :], t1[:, :], t1[:, :], ALU.mult))
                chain.link(v.tensor_reduce(ss[:, :], t2[:, :].rearrange("p (h e) -> p h e", e=HD), AX, ALU.add))
                chain.link(v.tensor_scalar(ss[:, :], ss[:, :], 1.0 / HD, RMS_EPS, ALU.mult, ALU.add))
                rsqrt(nc, (chain, rs[:, :], ss[:, :], n1[:, :], n2[:, :]))
                src = t1[:, :].rearrange("p (t h e) -> p t h e", t=TPC, h=NQK)
                scale = rs[:, :].rearrange("p (t h) -> p t h", t=TPC)
                for dst, h0, h1 in ((qn, 0, H), (kn, H, NQK)):
                    chain.do(v.tensor_tensor(dst[:, :, :].rearrange("p (t h) e -> p t h e", t=TPC), src[:, :, h0:h1, :],
                                             scale[:, :, h0:h1].unsqueeze(3).to_broadcast([P, TPC, h1 - h0, HD]), ALU.mult))
                chain.sync()

            def split(c, part):
                q0, q1 = ((0, 3), (3, 6), (6, 8))[part]
                k0, k1 = ((0, 8), (1, 8), (2, 6))[part]
                nk = len(range(k0, k1, 3))
                if part == 0:
                    dve.wait_ge(lay_done, c * LAYS)
                chain.do(v.tensor_copy(qs[:, :, q0:q1, :], qn[:, :, :].unsqueeze(2).to_broadcast([P, TPC * H, q1 - q0, HD])))
                kc = v.tensor_copy(ks[:, :, k0:k1:3, :], kn[:, :, :].unsqueeze(2).to_broadcast([P, TPC * KVH, nk, HD]))
                if part == 2:
                    chain.sync()
                    kc.then_inc(split_ready, 1)
                    return
                chain.link(kc)
                chain.do(v.tensor_tensor(qn[:, :, :], qn[:, :, :], qs[:, :, q0, :], ALU.subtract))
                chain.link(v.tensor_tensor(kn[:, :, :], kn[:, :, :], ks[:, :, k0, :], ALU.subtract))

            def lay(c):
                for n in range(0, LAYS, 2):
                    dve.wait_ge(lay_done, c * LAYS + (n + 1))
                    if n == 2 * TPC:
                        dve.wait_ge(k_moved, c)
                    dst, src = lay_views(n)
                    v.tensor_copy(dst, src).then_inc(lay_dve, 1)

            def normalise_out(c, kv):
                dve.wait_ge(oT_done, c * KVH + (kv + 1))
                dve.wait_ge(aT_done, c * 2)
                o = bank_p[:, :].rearrange("p (m e) -> p m e", e=VW)
                chain.link(v.reciprocal(den[:, :], o[:, :, HD]))
                dst = attn[:, :, kv * GQ * HD:(kv + 1) * GQ * HD]
                v.tensor_tensor(dst.rearrange("p t (h e) -> p t h e", h=GQ),
                                o[:, :, 0:HD].rearrange("p (t h) e -> p t h e", t=TPC),
                                den[:, :].rearrange("p (t h) -> p t h", t=TPC).unsqueeze(3).to_broadcast([P, TPC, GQ, HD]),
                                ALU.mult).then_inc(o_normed, 1)

            def add_proj(c):
                dve.wait_ge(xr_added, c + 1)
                for p in range(2):
                    dve.wait_ge(proj_done, c * 2 + (p + 1))
                    dst = chunk(c)[:, 2 * p:2 * p + 2, :]
                    v.tensor_tensor(dst, dst, (out_acc, bank_p)[p][:, :].rearrange("p (t d) -> p t d", t=2), ALU.add).then_inc(added, 1)

            def measure(c):
                dve.wait_ge(added, c * 2 + 2)
                for t in range(TPC):
                    tile = bass.ds(c * TPC + t, 1)
                    chain.do(v.bn_stats(g.bn[:, tile, :], x[:, tile, :]))

            def turn(c, ahead, far):
                if not isinstance(c, int) or c:
                    measure(c - 1)
                if ahead:
                    norm(c + 1)
                    normalise_out(c, 0)
                    split(c + 1, 0)
                    if far:
                        scale_x(c + 2)
                    normalise_out(c, 1)
                    split(c + 1, 1)
                    normalise_out(c, 2)
                    split(c + 1, 2)
                    normalise_out(c, 3)
                    lay(c + 1)
                else:
                    for kv in range(KVH):
                        normalise_out(c, kv)
                if far:
                    rope(c + 2)
                add_proj(c)
                if ahead:
                    chain.restart()

            dve.wait_ge(g.later_in["wb"], 16)
            for k in range(KD):
                v.tensor_scalar(wqkv[:, k, :], w("wqkv", k), w("norm2")[:, k:k + 1], None, ALU.mult).then_inc(w_ready, 1)
            stats(0, 2)
            scale_x(0)
            stats(2, NCH)
            scale_x(1)
            rope(0)
            norm(0)
            for part in range(3):
                split(0, part)
            lay(0)
            rope(1)
            chain.restart()
            turns(dve, turn)
            measure(NCH - 1)
            chain.sync()


def tree_ffn(nc, g, tag, first, store):
    ctx = ExitStack()
    with ctx:
        def sb(name, shape, dt=F32):
            return ctx.enter_context(nc.sbuf_tensor(f"{tag}_{name}", shape, dt))

        def sem(name):
            return g.tree_sems[name]

        x, w = g.x, piece(g.later["wc"], PACKS["wc"][0])
        DEPTH = 8
        xs = sb("xs", [P, TPC, D])
        xT = sb("xT", [P, TPC, KD, P])
        gate = sb("gate", [P, TPC, D])
        leaf = [sb(f"leaf{i}", [P, TPC, D]) for i in range(2)]
        leafT = sb("leafT", [P, TPC, KD, P])
        bn, mv = g.bn, sb("mv", [P, NT, 2])
        var, rstd, s1, s2 = (sb(n, [P, NT]) for n in ("var", "rstd", "s1", "s2"))

        def banks(name):
            return [ctx.enter_context(nc.psum_tensor(f"{tag}_{name}{i}", [P, 512], F32)) for i in range(2)]

        bank_x, bank_g, bank_l, bank_o = banks("bank_x"), banks("bank_g"), banks("bank_l"), banks("bank_o")
        dve_seq, w_prod, w_ready = sem("dve_seq"), sem("w_prod"), sem("w_ready")
        xs_ready, biased = sem("xs_ready"), sem("biased")
        xT_done, xT_copied, logits_done, gates_ready = sem("xT_done"), sem("xT_copied"), sem("logits_done"), sem("gates_ready")
        leaf_ready, leafT_done, leafT_copied = sem("leaf_ready"), sem("leafT_done"), sem("leafT_copied")
        out_done, added, stored = sem("out_done"), sem("added"), g.stored

        def chunk(c):
            return x[:, bass.ds(c * TPC, TPC), :]

        def turns(eng, body):
            body(0, True, True)
            with eng.Fori(1, NCH - 2) as c:
                body(c, True, True)
            body(NCH - 2, True, False)
            body(NCH - 1, False, False)

        block = ctx.enter_context(nc.Block())

        if store:
            @block.sync
            def _(sp):
                with sp.Fori(0, NCH) as c:
                    sp.wait_ge(added, c * 2 + 2)
                    sp.dma_start(g.out[:, bass.ds(c * TPC, TPC), :], chunk(c)).then_inc(stored, 16)
                sp.wait_ge(stored, 16 * NCH)

        @block.gpsimd
        def _(pool):
            pool.wait_ge(g.later_in["wd"], 16)
            with pool.Fori(0, NCH) as c:
                pool.wait_ge(xs_ready, c + 1)
                nc.gpsimd.tensor_tensor(chunk(c), chunk(c), piece(g.later["wd"], PACKS["wd"][0])("bias").unsqueeze(1).to_broadcast([P, TPC, D]),
                                        ALU.add).then_inc(biased, 1)

        @block.scalar
        def _(act):
            def copy(out, in_):
                return nc.scalar.activation(out, in_, ACT.Copy)

            def copy_x(c):
                for p in range(2):
                    act.wait_ge(xT_done, c * 2 + (p + 1))
                    if p == 0:
                        act.wait_ge(logits_done, c * 2)
                    copy(xT[:, 2 * p:2 * p + 2, :, :].rearrange("p t k n -> p (t k n)"), bank_x[p][:, :]).then_inc(xT_copied, 1)

            def gates(c):
                act.wait_ge(leaf_ready, c)
                for p in range(2):
                    act.wait_ge(logits_done, c * 2 + (p + 1))
                    nc.scalar.activation(gate[:, 2 * p:2 * p + 2, :].rearrange("p t n -> p (t n)"), bank_g[p][:, :],
                                         ACT.Sigmoid).then_inc(gates_ready, 1)

            def turn(c, ahead, far):
                if ahead:
                    gates(c + 1)
                for p in range(2):
                    act.wait_ge(leafT_done, c * 2 + (p + 1))
                    if p == 0:
                        act.wait_ge(out_done, c * 2)
                    copy(leafT[:, 2 * p:2 * p + 2, :, :].rearrange("p t k n -> p (t k n)"), bank_l[p][:, :]).then_inc(leafT_copied, 1)
                if far:
                    copy_x(c + 2)

            copy_x(0)
            gates(0)
            copy_x(1)
            turns(act, turn)

        @block.tensor
        def _(pe):
            mm, tr = nc.tensor.matmul, nc.tensor.transpose

            def transposed(src, banks, done):
                for p in range(2):
                    for t in range(2 * p, 2 * p + 2):
                        for k in range(KD):
                            at = ((t % 2) * KD + k) * P
                            last = tr(banks[p][:, at:at + P], src[:, t, k * P:(k + 1) * P], g.identf[:, :])
                    last.then_inc(done, 1)

            def product(src, weight, banks, done, ready, c):
                for p in range(2):
                    pe.wait_ge(ready, c * 2 + (p + 1))
                    for t in range(2 * p, 2 * p + 2):
                        for k in range(KD):
                            last = mm(banks[p][:, (t % 2) * D:(t % 2 + 1) * D], src[:, t, k, :], weight[:, k, :],
                                      start=(k == 0), stop=(k == KD - 1))
                    last.then_inc(done, 1)

            def transpose_x(c):
                pe.wait_ge(xs_ready, c + 1)
                transposed(xs, bank_x, xT_done)

            def logits(c):
                pe.wait_ge(gates_ready, c * 2)
                product(xT, g.w_gate, bank_g, logits_done, xT_copied, c)

            def turn(c, ahead, far):
                if ahead:
                    logits(c + 1)
                pe.wait_ge(leaf_ready, c + 1)
                transposed(leaf[DEPTH % 2], bank_l, leafT_done)
                if far:
                    transpose_x(c + 2)
                pe.wait_ge(added, c * 2)
                product(leafT, g.w_out, bank_o, out_done, leafT_copied, c)

            if first:
                pe.wait_ge(g.later_in["wc"], 16)
                for banks_, a, b in ((bank_g, "wq", "routersT"), (bank_o, "valuesT", "woutT")):
                    for m in range(KD):
                        for k in range(KD):
                            last = mm(banks_[m][:, 0:D], w(a, k)[:, m * P:(m + 1) * P], w(b, k), start=(k == 0), stop=(k == KD - 1))
                        last.then_inc(w_prod, 1)
                pe.wait_ge(w_ready, 2 * KD)
            transpose_x(0)
            logits(0)
            transpose_x(1)
            turns(pe, turn)

        @block.vector
        def _(dve):
            v = nc.vector
            chain = Chain(dve, dve_seq)

            def stats():
                for t in range(NT):
                    chain.do(v.bn_aggr(mv[:, t, :], bn[:, t, :]))
                chain.sync()
                chain.link(v.tensor_scalar(var[:, :], mv[:, :, 1], LN_EPS, None, ALU.add))
                rsqrt(nc, (chain, rstd[:, :], var[:, :], s1[:, :], s2[:, :]))

            def measure(c):
                dve.wait_ge(added, c * 2 + 2)
                for t in range(TPC):
                    tile = bass.ds(c * TPC + t, 1)
                    chain.do(v.bn_stats(bn[:, tile, :], x[:, tile, :]))

            def normalise(c):
                src = chunk(c)
                dve.wait_ge(xT_done, c * 2)
                for t in range(TPC):
                    at = bass.ds(c * TPC + t, 1)
                    last = v.tensor_scalar(xs[:, t, :], src[:, t, :], mv[:, at, 0], rstd[:, at], ALU.subtract, ALU.mult)
                    if t < TPC - 1:
                        chain.do(last)
                last.then_inc(xs_ready, 1)
                chain.sync()

            def leaves(c):
                dve.wait_ge(gates_ready, c * 2 + 2)
                dve.wait_ge(leafT_done, c * 2)
                chain.do(v.tensor_copy(leaf[1][:, :, 1:2], gate[:, :, 0:1]))
                chain.link(v.tensor_scalar(leaf[1][:, :, 0:1], gate[:, :, 0:1], -1.0, 1.0, ALU.mult, ALU.add))
                for level in range(1, DEPTH):
                    n = 2 ** level
                    a, b = leaf[level % 2], leaf[(level + 1) % 2]
                    chain.link(v.tensor_tensor(b[:, :, 1:2 * n:2], a[:, :, 0:n], gate[:, :, n - 1:2 * n - 1], ALU.mult))
                    last = v.tensor_tensor(b[:, :, 0:2 * n:2], a[:, :, 0:n], b[:, :, 1:2 * n:2], ALU.subtract)
                    if level < DEPTH - 1:
                        chain.link(last)
                last.then_inc(leaf_ready, 1)

            def add_out(c):
                dve.wait_ge(biased, c + 1)
                for p in range(2):
                    dve.wait_ge(out_done, c * 2 + (p + 1))
                    dst = chunk(c)[:, 2 * p:2 * p + 2, :]
                    v.tensor_tensor(dst, dst, bank_o[p][:, :].rearrange("p (t d) -> p t d", t=2), ALU.add).then_inc(added, 1)

            def turn(c, ahead, far):
                leaves(c)
                if far:
                    normalise(c + 2)
                if not isinstance(c, int) or c:
                    add_out(c - 1)
                if first and (not isinstance(c, int) or c):
                    measure(c - 1)
                if ahead:
                    chain.sync()
                    chain.restart()

            stats()
            if first:
                for m, (banks_, dst) in enumerate(((bank_g, g.w_gate), (bank_o, g.w_out))):
                    for k in range(KD):
                        dve.wait_ge(w_prod, m * KD + k + 1)
                        v.tensor_copy(dst[:, k, :], banks_[k][:, 0:D]).then_inc(w_ready, 1)
            normalise(0)
            normalise(1)
            chain.restart()
            turns(dve, turn)
            add_out(NCH - 1)
            if first:
                measure(NCH - 1)
                chain.sync()


def mamba_norms(nc, g):
    ctx = ExitStack()
    with ctx:
        def sb(name, shape, dt=F32):
            return ctx.enter_context(nc.sbuf_tensor("mn_" + name, shape, dt))

        def sem(name):
            return ctx.enter_context(nc.semaphore("mn_" + name))

        x, w = g.x, piece(g.later["wd"], PACKS["wd"][0])
        xs = sb("xs", [P, 2, TPC, D])
        bn, mv = g.bn, sb("mv", [P, NT, 2])
        var, rln, rln2, s1, s2 = (sb(n, [P, NT]) for n in ("var", "rln", "rln2", "s1", "s2"))
        sT = sb("sT", [P, 2, KD, CH])
        obank = [[ctx.enter_context(nc.psum_tensor(f"mn_obank{i}{p}", [P, 2 * D], F32)) for p in range(2)] for i in range(2)]
        bank = [[ctx.enter_context(nc.psum_tensor(f"mn_bank{i}{k}", [P, CH], F32)) for k in range(KD)] for i in range(2)]
        dve_seq, xs_ready, xT_done, xT_copied, biased = (sem("dve_seq"), sem("xs_ready"), sem("xT_done"),
                                                         sem("xT_copied"), sem("biased"))
        h_copied, out_done, added = sem("h_copied"), sem("out_done"), sem("added")
        block = ctx.enter_context(nc.Block())

        def pairs(eng, body):
            for c in range(4):
                body(c, c % 2)
            with eng.Fori(2, NCH // 2) as i:
                for b in range(2):
                    body(i * 2 + b, b)

        @block.gpsimd
        def _(pool):
            for name in g.tree_sems:
                pool.sem_clear(g.tree_sems[name])

            def turn(c, b):
                pool.wait_ge(xs_ready, c + 1)
                nc.gpsimd.tensor_tensor(x[:, bass.ds(c * TPC, TPC), :], x[:, bass.ds(c * TPC, TPC), :],
                                        w("po_b").unsqueeze(1).to_broadcast([P, TPC, D]), ALU.add).then_inc(biased, 1)
            pairs(pool, turn)

        @block.scalar
        def _(act):
            def turn(c, b):
                if not isinstance(c, int) or c >= 2:
                    act.wait_ge(out_done, c * 2 - 2)
                for k in range(KD):
                    act.wait_ge(xT_done, c * KD + (k + 1))
                    nc.scalar.activation(sT[:, b, k, :], bank[b][k][:, :], ACT.Identity,
                                         scale=w("ln_g")[:, k:k + 1], bias=w("ln_b")[:, k:k + 1]).then_inc(xT_copied, 1)
                act.wait_ge(xT_copied, c * KD + 1)
                nc.scalar.activation(g.hT[:, bass.ds(c * CH, CH)], sT[:, b, 0, :], ACT.Copy).then_inc(h_copied, 1)
            pairs(act, turn)

        @block.tensor
        def _(pe):
            def transposes(c, b):
                pe.wait_ge(xs_ready, c + 1)
                for k in range(KD):
                    if not isinstance(c, int) or c >= 2:
                        pe.wait_ge(xT_copied, c * KD + (k + 1 - 2 * KD))
                    for t in range(TPC):
                        last = nc.tensor.transpose(bank[b][k][:, t * P:(t + 1) * P], xs[:, b, t, k * P:(k + 1) * P], g.identf[:, :])
                    last.then_inc(xT_done, 1)

            def products(c, b):
                pe.wait_ge(xT_copied, c * KD + KD)
                for p in range(2):
                    if not isinstance(c, int) or c >= 2:
                        pe.wait_ge(added, c * 2 + (p + 1 - 4))
                    for t in range(2):
                        for k in range(KD):
                            rows = sT[:, b, k, (2 * p + t) * P:(2 * p + t + 1) * P]
                            nc.tensor.matmul(obank[b][p][:, t * D:(t + 1) * D], rows, w("po_WT", k),
                                             start=(t == 0 and k == 0), stop=False, skip_group_check=True)
                            last = nc.tensor.matmul(obank[b][p][:, t * D + k * P:t * D + (k + 1) * P], rows, g.identf[:, :],
                                                    start=False, stop=True, skip_group_check=True)
                    last.then_inc(out_done, 1)

            def turn(c, b):
                transposes(c, b)
                if not isinstance(c, int) or c:
                    products(c - 1, 1 - b)
            pairs(pe, turn)
            products(NCH - 1, 1)

        @block.vector
        def _(dve):
            v = nc.vector
            chain = Chain(dve, dve_seq)

            def add_out(c):
                dve.wait_ge(biased, c + 1)
                for p in range(2):
                    dve.wait_ge(out_done, c * 2 + (p + 1))
                    dst = x[:, c * TPC + 2 * p:c * TPC + 2 * p + 2, :]
                    v.tensor_tensor(dst, dst, obank[c % 2][p][:, :].rearrange("p (t d) -> p t d", t=2), ALU.add).then_inc(added, 1)

            dve.wait_ge(g.later_in["wd"], 16)

            def stats():
                ts = slice(0, NT)
                for i in range(NT):
                    chain.do(v.bn_aggr(mv[:, i, :], bn[:, i, :]))
                chain.sync()
                chain.link(v.tensor_scalar(var[:, ts], mv[:, ts, 1], LN_EPS, None, ALU.add))
                rsqrt(nc, (chain, rln[:, ts], var[:, ts], s1[:, ts], s2[:, ts]))
                chain.link(v.tensor_tensor(var[:, ts], rln[:, ts], rln[:, ts], ALU.mult))
                chain.link(v.tensor_tensor(var[:, ts], var[:, ts], mv[:, ts, 1], ALU.mult))
                chain.link(v.tensor_scalar(var[:, ts], var[:, ts], MAMBA_EPS, None, ALU.add))
                rsqrt(nc, (chain, rln2[:, ts], var[:, ts], s1[:, ts], s2[:, ts]))
                chain.link(v.tensor_tensor(rln[:, ts], rln[:, ts], rln2[:, ts], ALU.mult))

            stats()
            for c in range(NCH):
                if c >= 2:
                    dve.wait_ge(xT_done, KD * (c - 1))
                for t in range(TPC):
                    i = c * TPC + t
                    last = v.tensor_scalar(xs[:, c % 2, t, :], x[:, i, :], mv[:, i, 0:1], rln[:, i:i + 1], ALU.subtract, ALU.mult)
                    if t < TPC - 1:
                        chain.do(last)
                last.then_inc(xs_ready, 1)
                if c >= 2:
                    add_out(c - 2)
            for c in (NCH - 2, NCH - 1):
                add_out(c)


def mamba_layers(nc, g):
    BCR = 2 * NS
    ctx = ExitStack()
    with ctx:
        def sb(name, shape, dt=F32):
            return ctx.enter_context(nc.sbuf_tensor("mb_" + name, shape, dt))

        def sem(name):
            return ctx.enter_context(nc.semaphore("mb_" + name))

        w = piece(g.later["wd"], PACKS["wd"][0])
        hT = g.hT
        decay, decay_neg = (sb(n, [P, NL * 2 * NS]) for n in ("decay", "decay_neg"))
        mean_w, zeros, eps = sb("mean_w", [P, P]), sb("zeros", [P, 2 * TAPS]), sb("eps", [P, 1])
        pick = sb("pick", [3 * BCR, BCR], BF16)
        hn = sb("hn", [P, CH])
        xpad = sb("xpad", [P, 2, TAPS - 1 + CH])
        conv = sb("conv", [P, 2, CH])
        xc, zs = sb("xc", [P, 2, 2, CH]), sb("zs", [P, 2, 2, CH])
        delta, u = sb("delta", [P, 2, 2, CH]), sb("u", [P, 2, 2, CH])
        proj = sb("proj", [3 * BCR + DTR, CH])
        bc = sb("bc", [3 * BCR, 2, CH], BF16)
        rest = sb("rest", [2 * BCR, CH])
        ea, lg, rl, w1 = (sb(n, [P, 2, CH]) for n in ("ea", "lg", "rl", "w1"))
        yz, zraw = sb("yz", [P, 2, CH]), sb("zraw", [P, 2, CH])
        RB, RX, RH, RC = 4, 4, 4, 4
        AHEAD = RB - 1
        bsb = sb("bsb", [P, RB, CH])
        dbx, hs, hc = sb("dbx", [P, RX, 2, CH]), sb("hs", [P, RH, 2, CH]), sb("hc", [P, RC, 2, CH])
        carry = sb("carry", [P, NS, 2])

        def bank(name):
            return ctx.enter_context(nc.psum_tensor("mb_" + name, [P, CH], F32))

        ybank, abank, fbank = ([bank(f"{n}{i}") for i in range(2)] for n in ("y", "a", "f"))
        bbank, cbank = bank("b"), bank("c")
        front = [fbank[1], *abank, ybank[0]]

        const_seq, consts, inw_ready = sem("const_seq"), sem("consts"), sem("inw_ready")
        w_ready, decay_ready = sem("w_ready"), sem("decay_ready")
        sq_ready, ms_done, ln_done, rms_ready, hn_ready = (sem(n) for n in ("sq_ready", "ms_done", "ln_done", "rms_ready", "hn_ready"))
        x_done, z_done, x_copied, z_copied = sem("x_done"), sem("z_done"), sem("x_copied"), sem("z_copied")
        tail_moved, conv_seq, conv_done = sem("tail_moved"), sem("conv_seq"), [sem(f"conv_done{i}") for i in range(2)]
        xc_ready, z_ready = sem("xc_ready"), sem("z_ready")
        xp_done, p_copied, bc1, split_seq, bc_ready = (sem(n) for n in ("xp_done", "p_copied", "bc1", "split_seq", "bc_ready"))
        dt_done, dt_read = sem("dt_done"), sem("dt_read")
        e_ready, l_ready, w1_ready, soft_seq, delta_ready, u_ready = (
            sem(n) for n in ("e_ready", "l_ready", "w1_ready", "soft_seq", "delta_ready", "u_ready"))
        b_done, b_copied, c_done, dbx_done, hc_done, y_acc, carried = (
            sem(n) for n in ("b_done", "b_copied", "c_done", "dbx_done", "hc_done", "y_acc", "carried"))
        da_done, scan_done = sem("da_done"), sem("scan_done")
        y_read, yz_ready, mo_done, h_added = (sem(n) for n in ("y_read", "yz_ready", "mo_done", "h_added"))
        HS = 2 * NS

        def slab(ap, c):
            return ap[:, bass.ds(c * CH, CH)]

        def turns(eng, first, body, last):
            def chunk(l, c, b):
                if isinstance(c, int):
                    l, c = l + c // NCH, c % NCH
                    if l >= NL:
                        return None
                return (c + l * NCH, l, c, b)

            def turn(l, c, b):
                before = (c + (l * NCH - 1), None, None, 1 - b) if not isinstance(c, int) else \
                    (l * NCH + c - 1, (l * NCH + c - 1) // NCH, (c - 1) % NCH, 1 - b) if l + c else None
                if before and not isinstance(c, int):
                    before = (before[0], l, c - 1, 1 - b)
                body(chunk(l, c, b), before, chunk(l, c + 1, 1 - b), chunk(l, c + 2, b))

            first(chunk(0, 0, 0), chunk(0, 1, 1))
            for l in range(NL):
                for c in range(2):
                    turn(l, c, c)
                with eng.Fori(1, NCH // 2 - 1) as i:
                    for b in range(2):
                        turn(l, i * 2 + b, b)
                for c in (NCH - 2, NCH - 1):
                    turn(l, c, c % 2)
            last(chunk(NL - 1, NCH - 1, 1))

        block = ctx.enter_context(nc.Block())

        @block.gpsimd
        def _(pool):
            gp = nc.gpsimd
            setup = Chain(pool, const_seq)
            for t, val in ((mean_w, 1.0 / P), (zeros, 0.0), (eps, MAMBA_EPS)):
                gp.memset(t[:, :], val).then_inc(consts, 1)
            gp.memset(carry[:, :, :], 0.0).then_inc(consts, 1)
            setup.link(gp.memset(pick[:, :], 0.0))
            for q in range(3):
                ins = gp.affine_select(out=pick[:, :], in_=pick[:, :], compare_op=ALU.not_equal, fill=1.0, base=-q * BCR,
                                       pattern=[[-1, BCR]], channel_multiplier=1)
                if q < 2:
                    setup.link(ins)
            ins.then_inc(consts, 1)
            pool.wait_ge(consts, 5)

            def split(f, b):
                pool.wait_ge(bc1, f + 1)
                gp.tensor_tensor(rest[:, :], proj[0:2 * BCR, :], bc[0:2 * BCR, b, :], ALU.subtract).then_inc(split_seq, 1)
                pool.wait_ge(split_seq, f * 2 + 1)
                gp.tensor_tensor(bc[0:2 * BCR, b, :], rest[:, :], g.zero[0:2 * BCR, 0:1].to_broadcast([2 * BCR, CH]),
                                 ALU.add).then_inc(split_seq, 1)
                pool.wait_ge(split_seq, f * 2 + 2)
                gp.tensor_tensor(bc[0:BCR, b, :], rest[0:BCR, :], bc[0:BCR, b, :], ALU.subtract).then_inc(bc_ready, 1)

            def softplus_1(f):
                pool.wait_ge(w1_ready, f + 1)
                gp.tensor_tensor(w1[:, :, :], ea[:, :, :], w1[:, :, :], ALU.subtract).then_inc(soft_seq, 1)

            def softplus_2(f):
                pool.wait_ge(soft_seq, f * 2 + 1)
                pool.wait_ge(l_ready, f + 1)
                gp.tensor_tensor(w1[:, :, :], w1[:, :, :], lg[:, :, :], ALU.add).then_inc(soft_seq, 1)

            def softplus_3(f, b, m):
                pool.wait_ge(da_done, m * HS)
                pool.wait_ge(soft_seq, f * 2 + 2)
                gp.tensor_tensor(delta[:, b, :, :], w1[:, :, :], rl[:, :, :], ALU.add).then_inc(delta_ready, 1)

            def first(one, two):
                split(0, 0)
                softplus_1(0)
                softplus_2(0)
                softplus_3(0, 0, 0)

            def body(now, before, nxt, far):
                m, l, c, b = now
                pool.wait_ge(u_ready, m + 1)
                for n in range(NS):
                    pool.wait_ge(b_copied, m * NS + (n + 1))
                    if before or n >= RX:
                        pool.wait_ge(scan_done, m * HS + 2 * (n - RX + 1))
                    gp.tensor_tensor(dbx[:, n % RX, :, :], u[:, b, :, :],
                                     bsb[:, n % RB, :].unsqueeze(1).to_broadcast([P, 2, CH]), ALU.mult).then_inc(dbx_done, 1)
                    if nxt:
                        f, _, _, fb = nxt
                        if n == 7:
                            split(f, fb)
                        if n == 12:
                            softplus_1(f)
                        if n == 13:
                            softplus_2(f)
                        if n == 14:
                            softplus_3(f, fb, m)

            turns(pool, first, body, lambda end: None)

        @block.scalar
        def _(act):
            def fn(out, in_, func=ACT.Copy, **kw):
                return nc.scalar.activation(out, in_, func, **kw)

            def exp_ln_tables():
                nc.scalar.preload_act_table_set("natural_log_exp_and_others")

            def square(f, l, c):
                if l:
                    act.wait_ge(h_added, c + 1)
                act.wait_ge(z_done, f * 2)
                fn(hn[:, :], slab(hT, c), ACT.Square).then_inc(sq_ready, 1)

            def rms(f):
                act.wait_ge(ms_done, f + 1)
                fn(fbank[1][:, :], fbank[1][:, :], ACT.Ln, bias=eps[:, 0:1]).then_inc(ln_done, 1)
                act.wait_ge(ln_done, f + 1)
                fn(fbank[1][:, :], fbank[1][:, :], ACT.Exp, scale=-0.5).then_inc(rms_ready, 1)

            def move_tail(f, c):
                for done in conv_done:
                    act.wait_ge(done, f)
                src = zeros[:, 0:2 * (TAPS - 1)].rearrange("p (h t) -> p h t", h=2) if isinstance(c, int) and c == 0 \
                    else xpad[:, :, CH:CH + TAPS - 1]
                fn(xpad[:, :, 0:TAPS - 1], src).then_inc(tail_moved, 1)

            def copy_x(f, half, src=fbank[1]):
                if half == 0:
                    act.wait_ge(tail_moved, f + 1)
                act.wait_ge(x_done, f * 2 + (half + 1))
                fn(xpad[:, half, TAPS - 1:], src[:, :]).then_inc(x_copied, 1)

            def copy_z(f, half, src=fbank[1]):
                act.wait_ge(z_done, f * 2 + (half + 1))
                if half == 0:
                    act.wait_ge(z_ready, f)
                fn(zraw[:, half, :], src[:, :]).then_inc(z_copied, 1)

            def silus(f, l, b, before):
                if before:
                    act.wait_ge(yz_ready, before[0] + 1)
                for half in range(2):
                    act.wait_ge(conv_done[half], f + 1)
                    fn(xc[:, b, half, :], conv[:, half, :], ACT.Silu,
                       bias=w("conv_b", l)[:, half:half + 1]).then_inc(xc_ready, 1)
                act.wait_ge(z_copied, f * 2 + 2)
                fn(zs[:, b, :, :], zraw[:, :, :], ACT.Silu).then_inc(z_ready, 1)
                exp_ln_tables()

            def project(f, b, before):
                act.wait_ge(xp_done, f + 1)
                act.wait_ge(bc_ready, f)
                fn(proj[:, :], fbank[0][0:3 * BCR + DTR, :]).then_inc(p_copied, 1)
                act.wait_ge(p_copied, f + 1)
                if before:
                    act.wait_ge(c_done, (before[0] + 1) * NS)
                fn(bc[:, b, :], proj[0:3 * BCR, :]).then_inc(bc1, 1)

            def abs_relu(f, l, half):
                act.wait_ge(dt_done, f * 2 + (half + 1))
                if half == 0:
                    act.wait_ge(delta_ready, f)
                bias = w("dt_b", l)[:, half:half + 1]
                fn(ea[:, half, :], fbank[0][:, :], ACT.Abs, bias=bias).then_inc(dt_read, 1)
                fn(rl[:, half, :], fbank[0][:, :], ACT.Relu, bias=bias).then_inc(dt_read, 1)

            def exp_e(f):
                act.wait_ge(dt_read, f * 4 + 4)
                fn(ea[:, :, :], ea[:, :, :], ACT.Exp, scale=-1.0).then_inc(e_ready, 1)

            def ln_e(f):
                act.wait_ge(e_ready, f + 1)
                fn(lg[:, :, :], ea[:, :, :], ACT.Ln, bias=1.0).then_inc(l_ready, 1)

            def copy_b(m, n, fresh):
                act.wait_ge(b_done, m * NS + (n + 1))
                if not fresh:
                    act.wait_ge(dbx_done, m * NS + (n - RB + 1))
                fn(bsb[:, n % RB, :], bbank[:, :]).then_inc(b_copied, 1)

            def carry_on(m, n, end):
                act.wait_ge(scan_done, m * HS + 2 * (n + 1))
                src = zeros[:, 0:2] if end else hs[:, n % RH, :, CH - 1]
                fn(carry[:, n, :], src).then_inc(carried, 1)

            def first(one, two):
                exp_ln_tables()
                act.wait_ge(g.later_in["wd"], 16)
                fn(decay[:, :], w("A_log"), ACT.Exp).then_inc(w_ready, 1)
                act.wait_ge(consts, 5)
                (f, l, c, b), (f2, l2, c2, _) = one, two
                square(f, l, c)
                rms(f)
                move_tail(f, c)
                for half in range(2):
                    copy_x(f, half, front[half])
                for half in range(2):
                    copy_z(f, half, front[2 + half])
                square(f2, l2, c2)
                silus(f, l, b, None)
                project(f, b, None)
                rms(f2)
                abs_relu(f, l, 0)
                move_tail(f2, c2)
                abs_relu(f, l, 1)
                exp_e(f)
                for half in range(2):
                    copy_x(f2, half, front[half])
                ln_e(f)
                for half in range(2):
                    copy_z(f2, half, front[2 + half])
                for n in range(AHEAD - 1):
                    copy_b(0, n, True)
                act.wait_ge(decay_ready, 1)

            def body(now, before, nxt, far):
                m, l, c, b = now
                act.wait_ge(delta_ready, m + 1)
                for n in range(NS):
                    for half in range(2):
                        s = 2 * n + half
                        if before or s >= 2:
                            act.wait_ge(scan_done, m * HS + (s - 1))
                        at = (l * 2 + half) * NS + n
                        fn(abank[half][:, :], delta[:, b, half, :], ACT.Exp, scale=decay_neg[:, at:at + 1]).then_inc(da_done, 1)
                    if nxt and n == 2:
                        silus(nxt[0], nxt[1], nxt[3], before)
                    if n:
                        carry_on(m, n - 1, nxt is None or nxt[1] != l)
                    elif before:
                        carry_on(before[0], NS - 1, before[1] != l)
                    k = n + AHEAD - 1
                    if k < NS:
                        copy_b(m, k, k < RB and not before)
                    elif nxt:
                        copy_b(nxt[0], k - NS, False)
                    if nxt:
                        f, fl, fc, fb = nxt
                        if n == 6:
                            project(f, fb, before)
                        if n in (7, 9):
                            abs_relu(f, fl, (n - 7) // 2)
                        if n == 10:
                            exp_e(f)
                        if n == 11:
                            ln_e(f)
                    if far:
                        f, fl, fc, fb = far
                        if n == 1:
                            square(f, fl, fc)
                        if n == 7:
                            rms(f)
                        if n == 8:
                            move_tail(f, fc)
                        if n in (9, 11):
                            copy_x(f, (n - 9) // 2)
                        if n in (13, 15):
                            copy_z(f, (n - 13) // 2)
            turns(act, first, body, lambda end: None)

        @block.tensor
        def _(pe):
            mm = nc.tensor.matmul

            def mean_sq(f):
                pe.wait_ge(sq_ready, f + 1)
                if not isinstance(f, int) or f:
                    pe.wait_ge(z_copied, f * 2)
                mm(fbank[1][:, :], mean_w[:, :], hn[:, :], start=True, stop=True).then_inc(ms_done, 1)

            def in_proj(f, l, e, out=None):
                if e == 0:
                    pe.wait_ge(hn_ready, f + 1)
                elif out:
                    pass
                elif e < 3:
                    pe.wait_ge(x_copied, f * 2 + e)
                else:
                    pe.wait_ge(z_copied, f * 2 + 1)
                mm((out or fbank[1])[:, :], w("in_WT", l)[:, e * P:(e + 1) * P], hn[:, :], start=True, stop=True).then_inc((x_done, z_done)[e // 2], 1)

            def x_proj(f, l, b, half):
                if half == 0 and (not isinstance(f, int) or f):
                    pe.wait_ge(dt_read, f * 4)
                pe.wait_ge(xc_ready, f * 2 + (half + 1))
                last = mm(fbank[0][0:3 * BCR + DTR, :], w("xp_WT", l * 2 + half), xc[:, b, half, :], start=(half == 0), stop=(half == 1))
                if half:
                    last.then_inc(xp_done, 1)

            def dt_proj(f, l, half):
                if half == 0:
                    pe.wait_ge(p_copied, f + 1)
                else:
                    pe.wait_ge(dt_read, f * 4 + 2)
                at = 3 * BCR
                mm(fbank[0][:, :], w("dt_WT", l)[at:at + DTR, half * P:(half + 1) * P], proj[at:at + DTR, :],
                   start=True, stop=True).then_inc(dt_done, 1)

            def mo_proj(m, l):
                pe.wait_ge(yz_ready, m + 1)
                for half in range(2):
                    last = mm(ybank[0][:, :], w("mo_WT", l * 2 + half), yz[:, half, :], start=(half == 0), stop=(half == 1))
                last.then_inc(mo_done, 1)

            def rows_b(m, b, n, fresh=False):
                if not fresh:
                    pe.wait_ge(b_copied, m * NS + n)
                mm(bbank[:, :], pick[:, n:n + 1].to_broadcast([3 * BCR, P]), bc[:, b, :], start=True, stop=True).then_inc(b_done, 1)

            def rows_c(m, b, n, fresh):
                if not fresh:
                    pe.wait_ge(hc_done, m * NS + n)
                mm(cbank[:, :], pick[:, NS + n:NS + n + 1].to_broadcast([3 * BCR, P]), bc[:, b, :],
                   start=True, stop=True).then_inc(c_done, 1)

            def add_state(m, n):
                pe.wait_ge(hc_done, m * NS + (n + 1))
                for half in range(2):
                    last = mm(ybank[half][:, :], g.identf[:, :], hc[:, n % RC, half, :], start=(n == 0), stop=(n == NS - 1))
                last.then_inc(y_acc, 1)

            def first(one, two):
                pe.wait_ge(consts, 5)
                pe.wait_ge(inw_ready, NL)
                (f, l, c, b), (f2, l2, _, _) = one, two
                mean_sq(f)
                for e in range(4):
                    in_proj(f, l, e, front[e])
                mean_sq(f2)
                for half in range(2):
                    x_proj(f, l, b, half)
                dt_proj(f, l, 0)
                in_proj(f2, l2, 0, front[0])
                dt_proj(f, l, 1)
                for e in range(1, 4):
                    in_proj(f2, l2, e, front[e])
                pe.wait_ge(bc_ready, 1)
                for n in range(AHEAD):
                    rows_b(0, 0, n, n == 0)

            def body(now, before, nxt, far):
                m, l, c, b = now
                for n in range(NS):
                    if n + AHEAD < NS:
                        rows_b(m, b, n + AHEAD)
                    elif nxt:
                        if n + AHEAD == NS:
                            pe.wait_ge(bc_ready, nxt[0] + 1)
                        rows_b(nxt[0], nxt[3], n + AHEAD - NS)
                    rows_c(m, b, n, n == 0 and not before)
                    if n == 1 and before:
                        pe.wait_ge(h_added, m)
                    if n:
                        add_state(m, n - 1)
                    elif before:
                        add_state(before[0], NS - 1)
                    if far and n == 5:
                        mean_sq(far[0])
                    if n == 0 and before:
                        mo_proj(before[0], before[1])
                    if nxt:
                        f, fl, fc, fb = nxt
                        if n in (3, 4):
                            x_proj(f, fl, fb, n - 3)
                        if n in (5, 7):
                            dt_proj(f, fl, (n - 5) // 2)
                    if far and n in (7, 9, 11, 13):
                        in_proj(far[0], far[1], (n - 7) // 2)

            def last(end):
                m, l, c, b = end
                add_state(m, NS - 1)
                mo_proj(m, l)

            turns(pe, first, body, last)

        @block.vector
        def _(dve):
            v = nc.vector

            def normed(f, l, c):
                dve.wait_ge(rms_ready, f + 1)
                if l:
                    dve.wait_ge(h_added, c + 1)
                v.tensor_tensor(hn[:, :], slab(hT, c), fbank[1][:, :], ALU.mult).then_inc(hn_ready, 1)

            def convolve(f, l, k):
                if k == 0:
                    dve.wait_ge(x_copied, f * 2 + 2)
                    dve.wait_ge(xc_ready, f * 2)
                for half in range(2):
                    tap = w("conv_w", l)[:, half * TAPS + k:half * TAPS + k + 1]
                    src = xpad[:, half, k:k + CH]
                    if k == 0:
                        ins = v.tensor_scalar(conv[:, half, :], src, tap, None, ALU.mult)
                    else:
                        dve.wait_ge(conv_seq, f * 6 + (2 * k + half - 1))
                        ins = v.scalar_tensor_tensor(conv[:, half, :], src, tap, conv[:, half, :], ALU.mult, ALU.add)
                    ins.then_inc(conv_done[half] if k == TAPS - 1 else conv_seq, 1)

            def one_plus(f):
                dve.wait_ge(e_ready, f + 1)
                dve.wait_ge(delta_ready, f)
                v.tensor_scalar(w1[:, :, :], ea[:, :, :], 1.0, -1.0, ALU.add, ALU.add).then_inc(w1_ready, 1)

            def inputs(f, b):
                dve.wait_ge(delta_ready, f + 1)
                dve.wait_ge(xc_ready, f * 2 + 2)
                v.tensor_tensor(u[:, b, :, :], delta[:, b, :, :], xc[:, b, :, :], ALU.mult).then_inc(u_ready, 1)

            def finish_y(m, l, b):
                dve.wait_ge(y_acc, m * NS + NS)
                for half in range(2):
                    v.scalar_tensor_tensor(yz[:, half, :], xc[:, b, half, :], w("Dp", l)[:, half:half + 1], ybank[half][:, :],
                                           ALU.mult, ALU.add).then_inc(y_read, 1)
                dve.wait_ge(y_read, m * 2 + 2)
                dve.wait_ge(z_ready, m + 1)
                v.tensor_tensor(yz[:, :, :], yz[:, :, :], zs[:, b, :, :], ALU.mult).then_inc(yz_ready, 1)

            def add_h(m, l, c):
                dve.wait_ge(mo_done, m + 1)
                v.tensor_tensor(slab(hT, c), slab(hT, c), ybank[0][:, :], ALU.add).then_inc(h_added, 1)

            def weighted(m, n):
                dve.wait_ge(scan_done, m * HS + 2 * (n + 1))
                dve.wait_ge(c_done, m * NS + (n + 1))
                if not isinstance(m, int) or m or n >= RC:
                    dve.wait_ge(y_acc, m * NS + (n - RC + 1))
                v.tensor_tensor(hc[:, n % RC, :, :], hs[:, n % RH, :, :], cbank[:, :].unsqueeze(1).to_broadcast([P, 2, CH]),
                                ALU.mult).then_inc(hc_done, 1)

            def first(one, two):
                dve.wait_ge(g.later_in["wd"], 16)
                for i in range(NL):
                    v.tensor_scalar(w("in_WT", i), w("in_WT", i), w("rms_w")[:, i:i + 1], None, ALU.mult).then_inc(inw_ready, 1)
                dve.wait_ge(w_ready, 1)
                v.tensor_scalar(decay_neg[:, :], decay[:, :], -1.0, None, ALU.mult).then_inc(decay_ready, 1)
                (f, l, c, b), (f2, l2, c2, _) = one, two
                normed(f, l, c)
                for k in range(TAPS):
                    convolve(f, l, k)
                normed(f2, l2, c2)
                one_plus(f)
                for k in range(TAPS):
                    convolve(f2, l2, k)
                inputs(f, b)

            def body(now, before, nxt, far):
                m, l, c, b = now
                for n in range(NS):
                    if nxt and n == NS - 1:
                        inputs(nxt[0], nxt[3])
                    dve.wait_ge(dbx_done, m * NS + (n + 1))
                    if before or n >= RH:
                        dve.wait_ge(carried, m * NS + (n - RH + 1))
                    for half in range(2):
                        dve.wait_ge(da_done, m * HS + (2 * n + half + 1))
                        if before and n == NS - 1 and half == 0:
                            dve.wait_ge(carried, m * NS)
                        v.tensor_tensor_scan(hs[:, n % RH, half, :], abank[half][:, :], dbx[:, n % RX, half, :],
                                             carry[:, n, half:half + 1], ALU.mult, ALU.add).then_inc(scan_done, 1)
                    if before and n == 1:
                        finish_y(before[0], before[1], before[3])
                    if before and n == 2:
                        add_h(before[0], before[1], before[2])
                    if n:
                        weighted(m, n - 1)
                    elif before:
                        weighted(before[0], NS - 1)
                    if nxt:
                        f, fl, fc, fb = nxt
                        if n == 10:
                            one_plus(f)
                    if far:
                        f, fl, fc, fb = far
                        if n == 7:
                            normed(f, fl, fc)
                        if n >= NS - TAPS:
                            convolve(f, fl, n - (NS - TAPS))

            def last(end):
                m, l, c, b = end
                weighted(m, NS - 1)
                finish_y(m, l, b)
                add_h(m, l, c)

            turns(dve, first, body, last)


def mamba_out(nc, g):
    ctx = ExitStack()
    with ctx:
        def sem(name):
            return ctx.enter_context(nc.semaphore("mo_" + name))

        w = piece(g.later["wd"], PACKS["wd"][0])
        obank = [[ctx.enter_context(nc.psum_tensor(f"mo_o{b}{p}", [P, 2 * D], F32)) for p in range(2)] for b in range(2)]
        out_done, added, measured = sem("out_done"), sem("added"), sem("measured")
        block = ctx.enter_context(nc.Block())

        def pairs(eng, body):
            for b in range(2):
                body(b, b, False)
            with eng.Fori(1, NCH // 2) as i:
                for b in range(2):
                    body(i * 2 + b, b, True)

        @block.tensor
        def _(pe):
            def turn(c, b, again):
                for p in range(2):
                    if again:
                        pe.wait_ge(added, c * 2 + (p + 1 - 4))
                    for t in range(2):
                        at = c * CH + (2 * p + t) * P
                        rows = g.hT[:, at:at + P]
                        last = nc.tensor.matmul(obank[b][p][:, t * D:(t + 1) * D], rows, w("po_WT", KD - 1), start=True, stop=True)
                    last.then_inc(out_done, 1)

            for c in range(NCH):
                turn(c, c % 2, c >= 2)

        @block.vector
        def _(dve):
            v = nc.vector

            def measure(c):
                dve.wait_ge(added, c * 2 + 2)
                for t in range(TPC):
                    tile = bass.ds(c * TPC + t, 1)
                    v.bn_stats(g.bn[:, tile, :], g.x[:, tile, :]).then_inc(measured, 1)

            def turn(c, b, again):
                for p in range(2):
                    dve.wait_ge(out_done, c * 2 + (p + 1))
                    dst = g.x[:, bass.ds(c * TPC + 2 * p, 2), :]
                    v.tensor_tensor(dst, dst, obank[b][p][:, :].rearrange("p (t d) -> p t d", t=2), ALU.add).then_inc(added, 1)
                if not isinstance(c, int) or c:
                    measure(c - 1)

            pairs(dve, turn)
            measure(NCH - 1)
            dve.wait_ge(measured, NT)


def kernel(**inputs):
    import concourse.bacc as bacc
    from concourse.bass_utils import run_bass_kernel_spmd
    nc = bacc.Bacc("TRN2", target_bir_lowering=False, num_devices=1)
    arrays = lay_out(inputs)
    dram = {name: nc.dram_tensor("in_" + name, a.shape, mybir.dt.from_np(a.dtype), kind="ExternalInput").ap()
            for name, a in arrays.items()}
    out = nc.dram_tensor("out_x", (P, NT, D), F32, kind="ExternalOutput").ap()
    build(nc, dram, out)
    nc.compile()
    res = run_bass_kernel_spmd(nc, [{"in_" + name: a for name, a in arrays.items()}], core_ids=[0])
    return np.asarray(res.results[0]["out_x"]).transpose(1, 0, 2).reshape(1, S, D)
```
